# Optimizing a Trainium2 kernel written in Bass

```python
import numpy as np
import jax
import jax.numpy as jnp

def _softmax(x, axis=-1):
    return jax.nn.softmax(x, axis=axis)

def _gelu(x):
    return jax.nn.gelu(x, approximate=True)

def _silu(x):
    return jax.nn.silu(x)

def _sigmoid(x):
    return jax.nn.sigmoid(x)

def _layernorm(x, axis=-1, eps=1e-05):
    m = jnp.mean(x, axis=axis, keepdims=True)
    v = jnp.var(x, axis=axis, keepdims=True)
    return (x - m) / jnp.sqrt(v + eps)

def _scatter_add(tgt, idx, src, axis=0):
    return tgt.at[idx].add(src)

def _segment_sum(src, seg, n):
    return jax.ops.segment_sum(src, seg, n)
kernel_name = 'mk_lm_tower_d2_tok_ids512_r4_522131'

def setup_inputs(seed: int=0):
    np.random.seed(seed)
    _w = jnp.asarray

    def _rec_inputs():
        import jax
        import jax.numpy as jnp
        _rk = jax.random.key(seed)
        x = jax.random.randint(jax.random.fold_in(_rk, 1), (64, 256), 0, 8000, jnp.int32)
        return x
    x = _rec_inputs()

    def _L0_tok_setup():
        import jax, jax.numpy as jnp
        import numpy as np
        VOCAB = 8000
        DIM = 128
        PAD_IDX = 0
        key = jax.random.key(seed)
        k_tok, k_w = jax.random.split(key)
        tensor = jax.random.randint(k_tok, (16, 512), 0, VOCAB, dtype=jnp.int64)
        weight = jax.random.normal(k_w, (VOCAB, DIM), dtype=jnp.float32)
        weight = weight.at[PAD_IDX].set(0.0)
        return {'tensor': tensor, 'weight': weight}
    _L0_tok_all = _L0_tok_setup()
    _L0_tok_in = {k: v for k, v in _L0_tok_all.items() if k in ('weight',)}
    del _L0_tok_all

    def _L0_attn_setup():
        import jax, jax.numpy as jnp
        import numpy as np
        DIM = 128
        HEADS = 8

        def _reference_tuple_inner(x, Wqkv, temperature, Wproj, bproj):
            B, N, C = x.shape
            H = temperature.shape[0]
            D = C // H
            qkv = (x @ Wqkv.T).reshape(B, N, 3, H, D).transpose(2, 0, 3, 1, 4)
            q, k, v = (qkv[0], qkv[1], qkv[2])
            q = jax.nn.relu(q)
            k = jax.nn.relu(k)
            ksum = k.sum(axis=2)
            denom = jnp.clip(jnp.einsum('bhnd,bhd->bhn', q, ksum), 100.0)[..., None]
            attn = jnp.einsum('bhnd,bhne->bhde', k, v) * temperature
            attn1 = jnp.einsum('bhnd,bhde->bhne', q, attn)
            out = attn1 / denom
            y = out.transpose(0, 2, 1, 3).reshape(B, N, C) @ Wproj.T + bproj
            return (y, attn1)
        key = jax.random.key(seed)
        k1, k2, k3, k4 = jax.random.split(key, 4)
        head_dim = DIM // HEADS
        scale = head_dim ** (-0.5)
        x = jax.random.normal(k1, (4, 1024, DIM), dtype=jnp.float32)
        Wqkv = jax.random.normal(k2, (3 * DIM, DIM), dtype=jnp.float32) * DIM ** (-0.5)
        temperature = jnp.ones((HEADS, 1, 1), dtype=jnp.float32) * scale
        Wproj = jax.random.normal(k3, (DIM, DIM), dtype=jnp.float32) * DIM ** (-0.5)
        bproj = jnp.zeros((DIM,), dtype=jnp.float32)
        return {'x': x, 'Wqkv': Wqkv, 'temperature': temperature, 'Wproj': Wproj, 'bproj': bproj}
    _L0_attn_all = _L0_attn_setup()
    _L0_attn_in = {k: v for k, v in _L0_attn_all.items() if k in ('Wqkv', 'temperature', 'Wproj', 'bproj')}
    del _L0_attn_all

    def _L0_ffn_setup():
        import jax, jax.numpy as jnp
        import numpy as np
        NUM_EXPERTS = 32
        GROUP_SIZE = 4
        NUM_GROUPS = NUM_EXPERTS // GROUP_SIZE
        C_CAP = 1.0
        key = jax.random.key(seed)
        ks = jax.random.split(key, 5)
        B, S, H = (16, 512, 128)
        D_FF = int(H * 4 * (2.0 / 3.0))
        x = jax.random.normal(ks[0], (B, S, H), dtype=jnp.float32)
        W_router = jax.random.normal(ks[1], (H, NUM_EXPERTS), dtype=jnp.float32) * (1.0 / np.sqrt(H))
        b_router = jnp.zeros((NUM_EXPERTS,), dtype=jnp.float32)
        W_up = jax.random.normal(ks[2], (NUM_GROUPS, H, D_FF), dtype=jnp.float32) * (1.0 / np.sqrt(H))
        b_up = jnp.zeros((NUM_GROUPS, D_FF), dtype=jnp.float32)
        W_down = jax.random.normal(ks[3], (NUM_EXPERTS, D_FF, H), dtype=jnp.float32) * (1.0 / np.sqrt(D_FF))
        b_down = jnp.zeros((NUM_EXPERTS, H), dtype=jnp.float32)
        return {'x': x, 'W_router': W_router, 'b_router': b_router, 'W_up': W_up, 'b_up': b_up, 'W_down': W_down, 'b_down': b_down}
    _L0_ffn_all = _L0_ffn_setup()
    _L0_ffn_in = {k: v for k, v in _L0_ffn_all.items() if k in ('W_router', 'b_router', 'W_up', 'b_up', 'W_down', 'b_down')}
    del _L0_ffn_all

    def _L1_attn_setup():
        import math
        import jax, jax.numpy as jnp
        import numpy as np
        key = jax.random.key(seed)
        ks = jax.random.split(key, 6)
        b, t, e, h = (4, 256, 128, 8)
        x = jax.random.normal(ks[0], (b, t, e), dtype=jnp.float32)
        s = 0.02
        Wq = jax.random.normal(ks[1], (e, e * h), dtype=jnp.float32) * s
        Wk = jax.random.normal(ks[2], (e, e * h), dtype=jnp.float32) * s
        Wv = jax.random.normal(ks[3], (e, e * h), dtype=jnp.float32) * s
        Wo = jax.random.normal(ks[4], (e * h, e), dtype=jnp.float32) * s
        bo = jnp.zeros((e,), dtype=jnp.float32)
        return {'x': x, 'Wq': Wq, 'Wk': Wk, 'Wv': Wv, 'Wo': Wo, 'bo': bo}
    _L1_attn_all = _L1_attn_setup()
    _L1_attn_in = {k: v for k, v in _L1_attn_all.items() if k in ('Wq', 'Wk', 'Wv', 'Wo', 'bo')}
    del _L1_attn_all

    def _L1_ffn_setup():
        import jax, jax.numpy as jnp
        import numpy as np
        B, S, H, E, K = (8, 1024, 128, 8, 2)
        key = jax.random.key(seed)
        ks = jax.random.split(key, 7)
        s_h = 1.0 / np.sqrt(H)
        s_2h = 1.0 / np.sqrt(2 * H)
        return {'x': jax.random.normal(ks[0], (B, S, H), dtype=jnp.float32), 'gate_w': jax.random.uniform(ks[1], (H, E), minval=-s_h, maxval=s_h, dtype=jnp.float32), 'gate_b': jax.random.uniform(ks[2], (E,), minval=-s_h, maxval=s_h, dtype=jnp.float32), 'w1': jax.random.uniform(ks[3], (E, H, 2 * H), minval=-s_h, maxval=s_h, dtype=jnp.float32), 'b1': jax.random.uniform(ks[4], (E, 2 * H), minval=-s_h, maxval=s_h, dtype=jnp.float32), 'w2': jax.random.uniform(ks[5], (E, 2 * H, H), minval=-s_2h, maxval=s_2h, dtype=jnp.float32), 'b2': jax.random.uniform(ks[6], (E, H), minval=-s_2h, maxval=s_2h, dtype=jnp.float32)}
    _L1_ffn_all = _L1_ffn_setup()
    _L1_ffn_in = {k: v for k, v in _L1_ffn_all.items() if k in ('gate_w', 'gate_b', 'w1', 'b1', 'w2', 'b2')}
    del _L1_ffn_all
    return {'x': x, 'L0_tok_weight': _L0_tok_in['weight'], 'L0_attn_Wqkv': _L0_attn_in['Wqkv'], 'L0_attn_temperature': _L0_attn_in['temperature'], 'L0_attn_Wproj': _L0_attn_in['Wproj'], 'L0_attn_bproj': _L0_attn_in['bproj'], 'L0_ffn_W_router': _L0_ffn_in['W_router'], 'L0_ffn_b_router': _L0_ffn_in['b_router'], 'L0_ffn_W_up': _L0_ffn_in['W_up'], 'L0_ffn_b_up': _L0_ffn_in['b_up'], 'L0_ffn_W_down': _L0_ffn_in['W_down'], 'L0_ffn_b_down': _L0_ffn_in['b_down'], 'L1_attn_Wq': _L1_attn_in['Wq'], 'L1_attn_Wk': _L1_attn_in['Wk'], 'L1_attn_Wv': _L1_attn_in['Wv'], 'L1_attn_Wo': _L1_attn_in['Wo'], 'L1_attn_bo': _L1_attn_in['bo'], 'L1_ffn_gate_w': _L1_ffn_in['gate_w'], 'L1_ffn_gate_b': _L1_ffn_in['gate_b'], 'L1_ffn_w1': _L1_ffn_in['w1'], 'L1_ffn_b1': _L1_ffn_in['b1'], 'L1_ffn_w2': _L1_ffn_in['w2'], 'L1_ffn_b2': _L1_ffn_in['b2']}

def reference(x, L0_tok_weight, L0_attn_Wqkv, L0_attn_temperature, L0_attn_Wproj, L0_attn_bproj, L0_ffn_W_router, L0_ffn_b_router, L0_ffn_W_up, L0_ffn_b_up, L0_ffn_W_down, L0_ffn_b_down, L1_attn_Wq, L1_attn_Wk, L1_attn_Wv, L1_attn_Wo, L1_attn_bo, L1_ffn_gate_w, L1_ffn_gate_b, L1_ffn_w1, L1_ffn_b1, L1_ffn_w2, L1_ffn_b2):
    import jax
    import jax.numpy as jnp

    def _L0_tok_ref(tensor, weight):
        import jax, jax.numpy as jnp
        import numpy as np
        VOCAB = 8000
        DIM = 128
        PAD_IDX = 0
        return jnp.take(weight, tensor, axis=0)

    def _L0_attn_ref(x, Wqkv, temperature, Wproj, bproj):
        import jax, jax.numpy as jnp
        import numpy as np
        DIM = 128
        HEADS = 8

        def _reference_tuple_inner(x, Wqkv, temperature, Wproj, bproj):
            B, N, C = x.shape
            H = temperature.shape[0]
            D = C // H
            qkv = (x @ Wqkv.T).reshape(B, N, 3, H, D).transpose(2, 0, 3, 1, 4)
            q, k, v = (qkv[0], qkv[1], qkv[2])
            q = jax.nn.relu(q)
            k = jax.nn.relu(k)
            ksum = k.sum(axis=2)
            denom = jnp.clip(jnp.einsum('bhnd,bhd->bhn', q, ksum), 100.0)[..., None]
            attn = jnp.einsum('bhnd,bhne->bhde', k, v) * temperature
            attn1 = jnp.einsum('bhnd,bhde->bhne', q, attn)
            out = attn1 / denom
            y = out.transpose(0, 2, 1, 3).reshape(B, N, C) @ Wproj.T + bproj
            return (y, attn1)
        return _reference_tuple_inner(x, Wqkv, temperature, Wproj, bproj)[0]

    def _L0_ffn_ref(x, W_router, b_router, W_up, b_up, W_down, b_down):
        import jax, jax.numpy as jnp
        import numpy as np
        NUM_EXPERTS = 32
        GROUP_SIZE = 4
        NUM_GROUPS = NUM_EXPERTS // GROUP_SIZE
        C_CAP = 1.0
        B, S, H = x.shape
        bs = B * S
        E = NUM_EXPERTS
        k = min(int(bs * C_CAP) // E, bs)
        xf = x.reshape(bs, H)
        h = xf @ W_router + b_router
        Sm = jax.nn.softmax(h, axis=-1)
        G_ek, idx_ek = jax.lax.top_k(Sm.T, k)
        tokens = xf[idx_ek]
        D_FF = W_up.shape[-1]
        tok_g = tokens.reshape(NUM_GROUPS, GROUP_SIZE, k, H)
        up = jnp.einsum('gjkh,ghf->gjkf', tok_g, W_up) + b_up[:, None, None, :]
        act = jax.nn.silu(up).reshape(E, k, D_FF)
        Eout = jnp.einsum('ekf,efh->ekh', act, W_down) + b_down[:, None, :]
        weighted = G_ek[..., None] * Eout
        y = jnp.zeros((bs, H), dtype=x.dtype).at[idx_ek.reshape(-1)].add(weighted.reshape(-1, H))
        return y.reshape(B, S, H)

    def _L1_attn_ref(x, Wq, Wk, Wv, Wo, bo):
        import math
        import jax, jax.numpy as jnp
        import numpy as np
        b, t, e = x.shape
        h = Wq.shape[1] // e
        q = (x @ Wq).reshape(b, t, h, e).transpose(0, 2, 1, 3)
        k = (x @ Wk).reshape(b, t, h, e).transpose(0, 2, 1, 3)
        v = (x @ Wv).reshape(b, t, h, e).transpose(0, 2, 1, 3)
        q = q / math.sqrt(e)
        dot = jnp.einsum('bhqe,bhke->bhqk', q, k)
        causal = jnp.tril(jnp.ones((t, t), dtype=bool))
        dot = jnp.where(causal[None, None], dot, -jnp.inf)
        att = jax.nn.softmax(dot, axis=-1)
        out = jnp.einsum('bhqk,bhke->bhqe', att, v)
        out = out.transpose(0, 2, 1, 3).reshape(b, t, h * e)
        return out @ Wo + bo

    def _L1_ffn_ref(x, gate_w, gate_b, w1, b1, w2, b2):
        import jax, jax.numpy as jnp
        import numpy as np
        B, S, H, E, K = (8, 1024, 128, 8, 2)
        logits = jnp.einsum('bsh,he->bse', x, gate_w) + gate_b
        topk_vals, topk_idx = jax.lax.top_k(logits, K)
        topk_weights = jax.nn.softmax(topk_vals, axis=-1)
        mask = jax.nn.one_hot(topk_idx, E, dtype=topk_weights.dtype)
        weights = jnp.einsum('bske,bsk->bse', mask, topk_weights)
        h = jax.nn.relu(jnp.einsum('bsh,ehf->bsef', x, w1) + b1)
        expert_out = jnp.einsum('bsef,efh->bseh', h, w2) + b2
        return jnp.einsum('bseh,bse->bsh', expert_out, weights)
    h = _L0_tok_ref(x, L0_tok_weight)
    h = h + _L0_attn_ref(_layernorm(h, axis=-1), L0_attn_Wqkv, L0_attn_temperature, L0_attn_Wproj, L0_attn_bproj)
    h = h + _L0_ffn_ref(_layernorm(h, axis=-1), L0_ffn_W_router, L0_ffn_b_router, L0_ffn_W_up, L0_ffn_b_up, L0_ffn_W_down, L0_ffn_b_down)
    h = h + _L1_attn_ref(_layernorm(h, axis=-1), L1_attn_Wq, L1_attn_Wk, L1_attn_Wv, L1_attn_Wo, L1_attn_bo)
    h = h + _L1_ffn_ref(_layernorm(h, axis=-1), L1_ffn_gate_w, L1_ffn_gate_b, L1_ffn_w1, L1_ffn_b1, L1_ffn_w2, L1_ffn_b2)
    return h

_drawn_inputs = setup_inputs


def setup_inputs(seed=0):
    import zlib

    import numpy as np

    out = dict(_drawn_inputs(seed))
    spreads = {'L0_attn_temperature': (0.25, 0.6),
     'L0_attn_bproj': (0.0, 0.1),
     'L0_ffn_b_router': (0.0, 0.364),
     'L0_ffn_b_up': (0.0, 0.416),
     'L0_ffn_b_down': (0.0, 0.311),
     'L1_attn_bo': (0.0, 0.1)}
    factors = {'L1_attn_Wq': 8.0, 'L1_attn_Wk': 8.0, 'L1_ffn_b1': 3.947}
    for name, (base, spread) in spreads.items():
        noise = np.random.default_rng([zlib.crc32(name.encode()), seed]).standard_normal(out[name].shape)
        drawn = base * np.exp(spread * noise) if base else spread * noise
        out[name] = jnp.asarray(drawn.astype(out[name].dtype))
    for name, factor in factors.items():
        out[name] = (out[name] * factor).astype(out[name].dtype)
    return out
```

```python
from contextlib import ExitStack

import concourse.bass as bass
from concourse import mybir

F32 = mybir.dt.float32
F16 = mybir.dt.float16
BF16 = mybir.dt.bfloat16
U32 = mybir.dt.uint32
I32 = mybir.dt.int32
ALU = mybir.AluOpType
ACT = mybir.ActivationFunctionType
AX = mybir.AxisListType

P = 128
C = 128
NTOK = 64 * 256
NT = NTOK // P
TG = 4
NG = NT // TG
EPS = 1e-5
H0, D0 = 8, 16
E0 = 32
CAP = NTOK // E0
FF = 341
FCH = (128, 128, FF - 256)
ROW = C + E0
H1 = 8
E1, F1 = 8, 256
BIG = 1e30


def first(i):
    return isinstance(i, int) and i == 0


class Steps:

    def __init__(self, eng, sem, base=0):
        self.eng, self.sem, self.base, self.n = eng, sem, base, 0

    def done(self, ins):
        ins.then_inc(self.sem, 1)
        self.n += 1

    def wait(self):
        self.eng.wait_ge(self.sem, self.base + self.n)


def lm_tower(nc, x, L0_tok_weight, L0_attn_Wqkv, L0_attn_temperature, L0_attn_Wproj, L0_attn_bproj,
             L0_ffn_W_router, L0_ffn_b_router, L0_ffn_W_up, L0_ffn_b_up, L0_ffn_W_down, L0_ffn_b_down,
             L1_attn_Wq, L1_attn_Wk, L1_attn_Wv, L1_attn_Wo, L1_attn_bo,
             L1_ffn_gate_w, L1_ffn_gate_b, L1_ffn_w1, L1_ffn_b1, L1_ffn_w2, L1_ffn_b2, out):
    with ExitStack() as ctx:
        def sb(name, shape, dt=F32):
            return ctx.enter_context(nc.sbuf_tensor(name, shape, dt))

        def sem(name):
            return ctx.enter_context(nc.semaphore(name))

        bank = [ctx.enter_context(nc.psum_tensor(f"bank{n}", [P, 512], F32)) for n in range(8)]

        hbuf = nc.dram_tensor("hbuf", (NTOK, C), F32).ap()
        xrow = nc.dram_tensor("xrow", (NTOK, ROW), F32).ap()
        h3buf = nc.dram_tensor("h3buf", (NTOK, C), F32).ap()
        hbuf_b = hbuf.rearrange("(n j p) c -> n p j c", j=2, p=P)
        h3buf_g = h3buf.rearrange("(g j p) c -> g p j c", j=TG, p=P)
        out_g = out.rearrange("b (j p) c -> (b j) p c", p=P).rearrange("(g j) p c -> g p j c", j=TG)
        h3buf_b = h3buf.rearrange("(n j p) c -> n p j c", j=2, p=P)
        hbuf_g = hbuf.rearrange("(g j p) c -> g p j c", j=TG, p=P)
        xrow_g = xrow.rearrange("(g j p) c -> g p j c", j=TG, p=P)

        ident = sb("ident", [P, P])
        ones = sb("ones", [P, P])
        head = sb("head", [H0, P])
        headt = sb("headt", [H0, P])
        headc = sb("headc", [P, H0])
        mtemp = sb("mtemp", [P, P])
        temp = sb("temp", [H0, 1])
        junkf = sb("junkf", [P, CAP], I32)
        slotf = sb("slotf", [P, TG], I32)
        tilef = sb("tilef", [P, 1], I32)
        whichi = sb("whichi", [P, E1], I32)
        wqkv_n = sb("wqkv_n", [P, 3, C])
        wproj_n = sb("wproj_n", [P, C])
        wqkvT = sb("wqkvT", [P, 3 * C])
        wprojT = sb("wprojT", [P, C])
        bproj = sb("bproj", [P, C])
        wrout = sb("wrout", [P, E0])
        brout = sb("brout", [P, E0])
        idrow = sb("idrow", [P, P], I32)
        idrowf = sb("idrowf", [P, P])
        ids = sb("ids", [P, NT], U32)
        vo_place = sb("vo_place", [P, 4, 2 * TG * C])
        pr_place = sb("pr_place", [P, 3, 2 * TG * C])

        def group_view(place, k):
            return place[:, k].rearrange("p (q j c) -> p q j c", q=2, j=TG)
        idst = sb("idst", [P, 2, TG], U32)
        xg = group_view(vo_place, 0)
        xb = group_view(vo_place, 1)
        st = sb("st", [P, 2, TG, 6])
        mv = sb("mv", [P, 2, TG, 2])
        lnv = sb("lnv", [P, 2, TG])
        rs = sb("rs", [P, 2, TG])
        rt = sb("rt", [P, 2, TG])
        xn = group_view(vo_place, 2)
        xT = vo_place[:, 3].rearrange("p (q t) -> p q t", q=2)
        kk = group_view(pr_place, 0)
        vv = sb("vv", [P, 2, TG, C + 1])
        qT = sb("qT", [P, 2, TG * P])
        md = sb("md", [P, 2, 2, C + H0])
        den = sb("den", [P, 2, TG, H0])
        oo = group_view(pr_place, 1)
        oT = pr_place[:, 2].rearrange("p (q t) -> p q t", q=2)
        h1 = sb("h1", [P, 2, TG, C])
        xr = sb("xr", [P, 2, TG, ROW])
        x2T = sb("x2T", [P, 2, TG * P])
        lg = sb("lg", [P, 2, TG, E0])
        mx = sb("mx", [P, 2, TG])
        sm = sb("sm", [P, 2, TG])
        pg = sb("pg", [P, 2, TG, E0])
        pa = sb("pa", [P, NT, E0])
        kb = sb("kb", [P, NG * P])

        lanes = sb("lanes", [P, P])
        before = sb("before", [P, P])
        slot16 = sb("slot16", [P, CAP], F16)
        slotc = sb("slotc", [P, TG])
        junk = sb("junk", [P, NG * P], BF16)
        thr = sb("thr", [P, 1], U32)
        cand = sb("cand", [P, 1], U32)
        bit = sb("bit", [P, 1], U32)
        keep = sb("keep", [P, 1], U32)
        cnt = sb("cnt", [P, 1])
        quota = sb("quota", [P, 1])
        diag = sb("diag", [E0, 2, E0])
        tq = sb("tq", [P, 2, E0])
        pc = sb("pc", [P, E0, P])
        sel = sb("sel", [P, 2, P])
        cum = sb("cum", [P, 2, P])
        base = sb("base", [P, 2])
        edge = sb("edge", [P, 2])
        tab = sb("tab", [P, P + 1], F16)
        from0 = sb("from0", [P, CAP], F16)
        oneh = sb("oneh", [P, CAP], F16)
        tbase = sb("tbase", [P, TG])
        cnt4 = sb("cnt4", [P, TG])
        idx = sb("idx", [P, 2, TG], U32)
        xe = sb("xe", [P, 2, TG, ROW])
        xeT = sb("xeT", [P, TG * P])
        wup = sb("wup", [P, 2, FF])
        bup_n = sb("bup_n", [8, FF])
        bupT = sb("bupT", [P, 3, 8])
        bupg = sb("bupg", [P, 3])
        wdn = sb("wdn", [P, 2, 3, C])
        ac = sb("ac", [P, 3, TG * P])
        gate = sb("gate", [P, 2, TG])
        ye = sb("ye", [P, 2, TG, C])

        identb = sb("identb", [P, P], BF16)
        causal = sb("causal", [P, P], BF16)
        wqn = sb("wqn", [P, H1 * C])
        wkn = sb("wkn", [P, H1 * C])
        wvn = sb("wvn", [P, H1 * C])
        won = sb("won", [P, H1, C])
        wT = sb("wT", [P, 3, C])
        wqk = sb("wqk", [P, H1, C])
        wvo = sb("wvo", [P, H1, C])
        bo = sb("bo", [P, C])
        hx = sb("hx", [P, 2, 2, C])
        hb = sb("hb", [P, 2, 2, C])
        h3 = sb("h3", [P, 2, 2, C])
        st3 = sb("st3", [P, 2, 6])
        mv3 = sb("mv3", [P, 2, 2])
        r3 = sb("r3", [P, 3, 2])
        xn3 = sb("xn3", [P, 2, C])
        xT3 = sb("xT3", [P, 2, 2 * P])
        gT = sb("gT", [P, 2, 4 * P])
        vo = vo_place[:].rearrange("p (q j) n -> p q j n", q=2)
        nmax = sb("nmax", [P, 4, 2])
        rsum = sb("rsum", [P, 4, 2])
        rinv = sb("rinv", [P, 4, 2])
        pr_flat = pr_place[:].rearrange("p k n -> p (k n)")
        pr = pr_flat[:, 0:12 * P].rearrange("p (k n) -> p k n", k=4)
        prT = pr_flat[:, 12 * P:18 * P].rearrange("p (k n) -> p k n", k=2)

        w1s = pa[:, 0:64].rearrange("p j e -> p (j e)").rearrange("p (x f) -> p x f", x=E1)
        w2s = pa[:, 64:128].rearrange("p j e -> p (j e)").rearrange("p (x k m) -> p x k m", x=E1, k=2)
        gw = sb("gw", [P, E1])
        gb = sb("gb", [P, E1])
        b1n = sb("b1n", [E1, F1])
        b2n = sb("b2n", [E1, C])
        b1T = sb("b1T", [P, 2, E1])
        which = sb("which", [P, E1])
        h4x = kb[:, 0:1024].rearrange("p (q j c) -> p q j c", q=2, j=TG)
        acc = kb[:, 1024:2048].rearrange("p (q j c) -> p q j c", q=2, j=TG)
        xn4 = kb[:, 2048:2560].rearrange("p (j c) -> p j c", j=TG)
        xT4 = kb[:, 2560:3584].rearrange("p (q t) -> p q t", q=2)
        hT = pc[:, 0:16].rearrange("p e t -> p (e t)").rearrange("p (q k t) -> p q k t", q=2, k=2)
        wtT = pc[0:E1, 16:20].rearrange("p e t -> p (e t)")
        st4 = sb("st4", [P, TG, 6])
        mv4 = sb("mv4", [P, TG, 2])
        r4 = sb("r4", [P, 3, TG])
        lg4 = sb("lg4", [P, TG, E1])
        top = sb("top", [P, TG, 8])
        topi = sb("topi", [P, TG, 8], U32)
        topf = sb("topf", [P, TG, 2])
        gap = sb("gap", [P, TG])
        tw = sb("tw", [P, 2, TG])
        hit = sb("hit", [P, 2, TG, E1])
        wt = sb("wt", [P, 2, TG, E1])

        w_in = sem("w_in")
        consts = sem("consts")
        prep_t = sem("prep_t")
        prep_c = sem("prep_c")
        ids_ready = sem("ids_ready")
        idst_ready = sem("idst_ready")
        gathered = [sem(f"gathered{p}") for p in range(2)]
        xb_ready = sem("xb_ready")
        xn_ready = sem("xn_ready")
        xT_mm = sem("xT_mm")
        xT_ready = sem("xT_ready")
        kv_mm = sem("kv_mm")
        kv_ready = sem("kv_ready")
        q_mm = sem("q_mm")
        q_ready = sem("q_ready")
        kvs_mm = sem("kvs_mm")
        md_ready = sem("md_ready")
        o_mm = sem("o_mm")
        o_ready = sem("o_ready")
        oT_mm = sem("oT_mm")
        oT_ready = sem("oT_ready")
        y_mm = sem("y_mm")
        h1_ready = sem("h1_ready")
        x2_ready = sem("x2_ready")
        x2T_mm = sem("x2T_mm")
        x2T_ready = sem("x2T_ready")
        lg_mm = sem("lg_mm")
        lg_sub = sem("lg_sub")
        lg_exp = sem("lg_exp")
        p_ready = sem("p_ready")
        pa_ready = sem("pa_ready")
        pT_mm = sem("pT_mm")
        pT_ready = sem("pT_ready")
        stored = [sem(f"stored{p}") for p in range(2)]
        dve_step = sem("dve_step")

        consts2 = sem("consts2")
        lanes_s = sem("lanes_s")
        w_b = sem("w_b")
        pcT_mm = sem("pcT_mm")
        pc_ready = sem("pc_ready")
        bup_mm = sem("bup_mm")
        bup_ready = sem("bup_ready")
        cnt_ready = sem("cnt_ready")
        cnt_mm = sem("cnt_mm")
        find_step = sem("find_step")
        diag_ready = sem("diag_ready")
        tq_mm = sem("tq_mm")
        tq_ready = sem("tq_ready")
        cum_ready = sem("cum_ready")
        base_mm = sem("base_mm")
        sel_step = sem("sel_step")
        oneh_ready = sem("oneh_ready")
        tab_mm = sem("tab_mm")
        idx_ready = sem("idx_ready")
        xe_in = [sem(f"xe_in{p}") for p in range(2)]
        xeT_mm = sem("xeT_mm")
        xeT_ready = sem("xeT_ready")
        wup_in = [sem(f"wup_in{p}") for p in range(2)]
        wdn_in = [sem(f"wdn_in{p}") for p in range(2)]
        up_mm = sem("up_mm")
        ac_ready = sem("ac_ready")
        dn_mm = sem("dn_mm")
        ye_ready = sem("ye_ready")
        added = [sem(f"added{p}") for p in range(2)]

        consts3 = sem("consts3")
        w_c = sem("w_c")
        wT_mm = sem("wT_mm")
        wT_ready = sem("wT_ready")
        fold_mm = sem("fold_mm")
        fold_ready = sem("fold_ready")
        h2_in = [sem(f"h2_in{p}") for p in range(2)]
        hb_ready = sem("hb_ready")
        prep_step = sem("prep_step")
        xn3_ready = sem("xn3_ready")
        xT3_mm = sem("xT3_mm")
        xT3_ready = sem("xT3_ready")
        g_mm = sem("g_mm")
        g_ready = sem("g_ready")
        vo_mm = sem("vo_mm")
        vo_ready = sem("vo_ready")
        s_mm = sem("s_mm")
        max_ready = sem("max_ready")
        exp_ready = sem("exp_ready")
        rinv_ready = sem("rinv_ready")
        pr_ready = sem("pr_ready")
        prT_mm = sem("prT_mm")
        prT_ready = sem("prT_ready")
        head_mm = sem("head_mm")
        h3_ready = sem("h3_ready")
        h3_out = [sem(f"h3_out{p}") for p in range(2)]

        NB = NTOK // (2 * P)
        GBANK, VBANK, SBANK, TBANK, OBANK = 0, 2, (3, 4), (5, 6), (1, 7)
        S_LAG, T_LAG, O_LAG = 1, 3, 4

        def there(u):
            return not isinstance(u, int) or 0 <= u < NB * H1

        consts4 = sem("consts4")
        w_d = sem("w_d")
        w_d2 = sem("w_d2")
        b1_mm = sem("b1_mm")
        b1_ready = sem("b1_ready")
        h3_in = [sem(f"h3_in{p}") for p in range(2)]
        d_step = sem("d_step")
        xn4_ready = sem("xn4_ready")
        xT4_mm = sem("xT4_mm")
        xT4_ready = sem("xT4_ready")
        gate_mm = sem("gate_mm")
        gap_ready = sem("gap_ready")
        gap_exp = sem("gap_exp")
        wt_ready = sem("wt_ready")
        wtT_mm = sem("wtT_mm")
        wtT_ready = sem("wtT_ready")
        b2_mm = sem("b2_mm")
        b2_ready = sem("b2_ready")
        up1_mm = sem("up1_mm")
        hT_ready = sem("hT_ready")
        dn1_mm = sem("dn1_mm")
        acc_ready = sem("acc_ready")
        out_done = [sem(f"out_done{p}") for p in range(2)]

        NU = E0 // 4
        block = ctx.enter_context(nc.Block())

        @block.sync
        def _(sp):
            sp.dma_start(idrow[:], x.rearrange("b (t p) -> (b t) p", p=P)).then_inc(w_in, 16)
            sp.dma_start(wqkv_n[:], L0_attn_Wqkv.rearrange("(k p) c -> p k c", p=P)).then_inc(w_in, 16)
            sp.dma_start(wproj_n[:], L0_attn_Wproj).then_inc(w_in, 16)
            sp.dma_start(bproj[:], L0_attn_bproj.partition_broadcast(P)).then_inc(w_in, 16)
            sp.dma_start(wrout[:], L0_ffn_W_router).then_inc(w_in, 16)
            sp.dma_start(brout[:], L0_ffn_b_router.partition_broadcast(P)).then_inc(w_in, 16)
            sp.dma_start(temp[:], L0_attn_temperature.rearrange("h a b -> h (a b)")).then_inc(w_in, 16)

            sp.dma_start(wqn[:], L1_attn_Wq).then_inc(w_c, 16)
            sp.dma_start(wkn[:], L1_attn_Wk).then_inc(w_c, 16)
            sp.dma_start(wvn[:], L1_attn_Wv).then_inc(w_c, 16)
            sp.dma_start(won[:], L1_attn_Wo.rearrange("(h e) m -> e h m", h=H1)).then_inc(w_c, 16)
            sp.dma_start(bo[:], L1_attn_bo.partition_broadcast(P)).then_inc(w_c, 16)

            sp.dma_start(gw[:], L1_ffn_gate_w).then_inc(w_d, 16)
            sp.dma_start(gb[:], L1_ffn_gate_b.partition_broadcast(P)).then_inc(w_d, 16)
            sp.dma_start(b1n[:], L1_ffn_b1).then_inc(w_d, 16)
            sp.dma_start(b2n[:], L1_ffn_b2).then_inc(w_d, 16)

            def store(i):
                for p in range(2):
                    g = 2 * i + p
                    sp.wait_ge(h1_ready, g + 1)
                    sp.dma_start(hbuf_g[bass.ds(g, 1)].rearrange("a p j c -> (a p) j c"), h1[:, p]).then_inc(stored[p], 16)
                for p in range(2):
                    g = 2 * i + p
                    sp.wait_ge(p_ready, g + 1)
                    sp.dma_start(xrow_g[bass.ds(g, 1)].rearrange("a p j c -> (a p) j c"), xr[:, p]).then_inc(stored[p], 16)
            with sp.Fori(0, NG // 2) as i:
                store(i)
            for p in range(2):
                sp.wait_ge(stored[p], 32 * (NG // 2))


            sp.dma_start(bup_n[:], L0_ffn_b_up).then_inc(w_b, 16)

            def load_up(u, p):
                sp.dma_start(wup[:, p], L0_ffn_W_up[bass.ds(u, 1)].rearrange("a h f -> (a h) f")).then_inc(wup_in[p], 16)

            def load_down(e, p):
                w = L0_ffn_W_down[bass.ds(e, 1)].rearrange("a f h -> (a f) h")
                sp.dma_start(wdn[:, p, 0:2], w[0:2 * P].rearrange("(k p) h -> p k h", p=P)).then_inc(wdn_in[p], 16)
                sp.dma_start(wdn[0:FCH[2], p, 2], w[2 * P:FF]).then_inc(wdn_in[p], 16)
                sp.dma_start(wdn[FCH[2]:FCH[2] + 1, p, 2], L0_ffn_b_down[bass.ds(e, 1)]).then_inc(wdn_in[p], 16)

            for e in range(2):
                load_up(0, e)
                load_down(e, e)

            def reload(v, last):
                for q in range(2 if last else 4):
                    e, p = 4 * v + q, q % 2
                    sp.wait_ge(dn_mm, e + 1)
                    load_up(v + q // 2, p)
                    load_down(e + 2, p)
            with sp.Fori(0, NU - 1) as v:
                reload(v, False)
            reload(NU - 1, True)

            def load_h2(n, p):
                sp.dma_start(hx[:, p], hbuf_b[bass.ds(n, 1)].rearrange("a p j c -> (a p) j c")).then_inc(h2_in[p], 16)

            for p in range(2):
                sp.wait_ge(added[p], 64 * (E0 // 2))
            for p in range(2):
                load_h2(p, p)

            def pass_h(i, last):
                for p in range(2):
                    n = 2 * i + p
                    if not last:
                        sp.wait_ge(hb_ready, n + 1)
                        sp.wait_ge(xn3_ready, n + 1)
                        load_h2(n + 2, p)
                    sp.wait_ge(h3_ready, n + 1)
                    sp.dma_start(h3buf_b[bass.ds(n, 1)].rearrange("a p j c -> (a p) j c"), h3[:, p]).then_inc(h3_out[p], 16)
            with sp.Fori(0, NB // 2 - 1) as i:
                pass_h(i, False)
            pass_h(NB // 2 - 1, True)
            for p in range(2):
                sp.wait_ge(h3_out[p], 16 * (NB // 2))

            sp.dma_start(w1s, L1_ffn_w1.rearrange("x h f -> h x f")).then_inc(w_d2, 16)
            sp.dma_start(w2s, L1_ffn_w2.rearrange("x (k p) m -> p x k m", p=P)).then_inc(w_d2, 16)

            def load_h3(g, p):
                sp.dma_start(h4x[:, p], h3buf_g[bass.ds(g, 1)].rearrange("a p j c -> (a p) j c")).then_inc(h3_in[p], 16)

            for p in range(2):
                load_h3(p, p)

            def results(i, last):
                for p in range(2):
                    g = 2 * i + p
                    sp.wait_ge(acc_ready, g + 1)
                    sp.dma_start(out_g[bass.ds(g, 1)].rearrange("a p j c -> (a p) j c"), acc[:, p]).then_inc(out_done[p], 16)
                    if not last:
                        load_h3(g + 2, p)
            with sp.Fori(0, NG // 2 - 1) as i:
                results(i, False)
            results(NG // 2 - 1, True)
            for p in range(2):
                sp.wait_ge(out_done[p], 16 * (NG // 2))

        @block.gpsimd
        def _(pool):
            pool.memset(ident[:], 0.0).then_inc(consts, 1)
            pool.memset(ones[:], 1.0).then_inc(consts, 1)
            pool.memset(head[:], 1.0).then_inc(consts, 1)
            pool.memset(vv[:, :, :, C:C + 1], 1.0).then_inc(consts, 1)
            pool.wait_ge(consts, 4)
            pool.affine_select(out=ident[:], in_=ident[:], compare_op=ALU.not_equal, fill=1.0, base=0,
                               pattern=[[-1, P]], channel_multiplier=1).then_inc(consts, 1)
            pool.affine_select(out=head[:], in_=head[:], compare_op=ALU.is_ge, fill=0.0, base=0,
                               pattern=[[1, P]], channel_multiplier=-D0).then_inc(consts, 1)
            pool.wait_ge(consts, 6)
            pool.affine_select(out=head[:], in_=head[:], compare_op=ALU.is_ge, fill=0.0, base=D0 - 1,
                               pattern=[[-1, P]], channel_multiplier=D0).then_inc(consts, 1)
            pool.memset(lanes[:], 0.0).then_inc(consts2, 1)
            pool.memset(before[:], 1.0).then_inc(consts2, 1)
            pool.memset(ac[:], 1.0).then_inc(consts2, 1)
            pool.iota(junkf[:], pattern=[[1, CAP]], base=0, channel_multiplier=0).then_inc(consts2, 1)
            pool.iota(slotf[:], pattern=[[P, TG]], base=0, channel_multiplier=1).then_inc(consts2, 1)
            pool.iota(tilef[:], pattern=[[0, 1]], base=0, channel_multiplier=P).then_inc(consts2, 1)
            pool.wait_ge(consts2, 6)
            pool.affine_select(out=before[:], in_=before[:], compare_op=ALU.is_gt, fill=0.0, base=0,
                               pattern=[[1, P]], channel_multiplier=-1).then_inc(consts2, 1)
            pool.tensor_copy(slot16[:], junkf[:]).then_inc(consts2, 1)
            pool.tensor_copy(slotc[:], slotf[:]).then_inc(consts2, 1)
            pool.tensor_copy(tab[:, P:P + 1], tilef[:]).then_inc(consts2, 1)
            for k in range(4):
                v = lanes[:].rearrange("p (b m) -> p b m", b=4)
                pool.affine_select(out=v, in_=v, compare_op=ALU.not_equal, fill=1.0, base=-E0 * k,
                                   pattern=[[0, 4], [-1, E0]], channel_multiplier=1).then_inc(lanes_s, 1)
                pool.wait_ge(lanes_s, k + 1)
            pool.iota(whichi[:], pattern=[[1, E1]], base=0, channel_multiplier=0).then_inc(consts4, 1)
            pool.wait_ge(consts4, 1)
            pool.tensor_copy(which[:], whichi[:]).then_inc(consts4, 1)
            pool.memset(causal[:], 0.0).then_inc(consts3, 1)
            pool.tensor_copy(identb[:], ident[:]).then_inc(consts3, 1)
            pool.wait_ge(consts3, 2)
            pool.affine_select(out=causal[:], in_=causal[:], compare_op=ALU.is_ge, fill=-BIG, base=0,
                               pattern=[[-1, P]], channel_multiplier=1).then_inc(consts3, 1)
            pool.wait_ge(ids_ready, 1)

            def gather(g, p):
                pool.tensor_copy(idst[:, p], ids[:, bass.ds(TG * g, TG)]).then_inc(idst_ready, 1)
                pool.wait_ge(idst_ready, g + 1)
                pool.nop(nofuse=True)
                for j in range(TG):
                    pool.indirect_dma_start(out=xg[:, p, j], out_offset=None, in_=L0_tok_weight,
                                            in_offset=bass.IndirectOffsetOnAxis(ap=idst[:, p, j:j + 1], axis=0))\
                        .then_inc(gathered[p], 16)

            def pair(i, more):
                for p in range(2):
                    g = 2 * i + p
                    pool.wait_ge(gathered[p], 64 * (i + 1))
                    if not first(i):
                        pool.wait_ge(h1_ready, g - 1)
                    pool.tensor_tensor(xb[:, p], xg[:, p], bproj[:].unsqueeze(1).to_broadcast([P, TG, C]), ALU.add)\
                        .then_inc(xb_ready, 1)
                if more:
                    for p in range(2):
                        g = 2 * i + p
                        pool.wait_ge(xn_ready, g + 1)
                        pool.wait_ge(xb_ready, g + 1)
                        gather(g + 2, p)
                for p in range(2):
                    g = 2 * i + p
                    pool.wait_ge(p_ready, g + 1)
                    pool.nop(nofuse=True)
                    pool.tensor_copy(pa[:, bass.ds(g * TG, TG)], pg[:, p]).then_inc(pa_ready, 1)

            for p in range(2):
                gather(p, p)
            pair(0, True)
            with pool.Fori(1, NG // 2 - 1) as i:
                pair(i, True)
            pair(NG // 2 - 1, False)

            def take(e, p):
                pool.wait_ge(idx_ready, e + 1)
                pool.nop(nofuse=True)
                for c in range(TG):
                    pool.indirect_dma_start(out=xe[:, p, c], out_offset=None, in_=xrow,
                                            in_offset=bass.IndirectOffsetOnAxis(ap=idx[:, p, c:c + 1], axis=0))\
                        .then_inc(xe_in[p], 16)

            def give(e, p, v, q):
                pool.wait_ge(ye_ready, e + 1)
                pool.nop(nofuse=True)
                for c in range(TG):
                    pool.indirect_dma_start(out=hbuf, out_offset=bass.IndirectOffsetOnAxis(ap=idx[:, p, c:c + 1], axis=0),
                                            in_=ye[:, p, c], in_offset=None, compute_op=ALU.add).then_inc(added[p], 16)

            for p in range(2):
                pool.wait_ge(stored[p], 32 * (NG // 2))
            take(0, 0)

            def serve(v, last):
                for q in range(4):
                    e, p = 4 * v + q, q % 2
                    if not (last and q == 3):
                        take(e + 1, 1 - p)
                    if not (first(v) and q == 0):
                        n = 2 * v + (q + 1) // 2 if q % 2 else 2 * v + q // 2
                        pool.wait_ge(added[1 - p], 64 * n)
                    give(e, p, v, q)
            serve(0, False)
            with pool.Fori(1, NU - 1) as v:
                serve(v, False)
            serve(NU - 1, True)
            for p in range(2):
                pool.wait_ge(added[p], 64 * (E0 // 2))

            pool.wait_ge(w_c, 16 * 5)

            def residual(i):
                for p in range(2):
                    n = 2 * i + p
                    pool.wait_ge(h2_in[p], 16 * (i + 1))
                    if not first(i):
                        pool.wait_ge(h3_ready, n - 1)
                    pool.tensor_tensor(hb[:, p], hx[:, p], bo[:].unsqueeze(1).to_broadcast([P, 2, C]), ALU.add)\
                        .then_inc(hb_ready, 1)
            residual(0)
            with pool.Fori(1, NB // 2) as i:
                residual(i)

        @block.scalar
        def _(act):
            act.wait_ge(consts, 7)
            act.wait_ge(prep_t, 5)
            act.activation(ids[:], bank[0][:, 0:P], ACT.Copy).then_inc(ids_ready, 1)
            act.activation(wqkvT[:], bank[1][:, 0:3 * C], ACT.Copy).then_inc(prep_c, 1)
            act.activation(wprojT[:], bank[2][:, 0:C], ACT.Copy).then_inc(prep_c, 1)
            act.wait_ge(prep_t, 7)
            act.activation(headc[:], bank[3][:, 0:H0], ACT.Copy).then_inc(prep_c, 1)
            act.activation(mtemp[:], bank[4][:, 0:P], ACT.Copy).then_inc(prep_c, 1)

            def pair(i, more):
                for p in range(2):
                    g = 2 * i + p
                    act.wait_ge(xT_mm, g + 1)
                    act.activation(xT[:, p], bank[4 * p][:, :], ACT.Copy).then_inc(xT_ready, 1)
                for p in range(2):
                    g = 2 * i + p
                    for m in range(2):
                        b2 = bank[4 * p + 1 + m][:, :].rearrange("p (j n) -> p j n", j=2)
                        act.wait_ge(kv_mm, 2 * g + m + 1)
                        act.activation(kk[:, p, 2 * m:2 * m + 2], b2[:, :, 0:C], ACT.Relu).then_inc(kv_ready, 1)
                        act.activation(vv[:, p, 2 * m:2 * m + 2, 0:C], b2[:, :, C:2 * C], ACT.Copy).then_inc(kv_ready, 1)
                for p in range(2):
                    g = 2 * i + p
                    act.wait_ge(q_mm, g + 1)
                    act.activation(qT[:, p], bank[4 * p + 3][:, :], ACT.Relu).then_inc(q_ready, 1)
                for p in range(2):
                    g = 2 * i + p
                    act.wait_ge(oT_mm, g + 1)
                    act.activation(oT[:, p], bank[4 * p][:, :], ACT.Copy).then_inc(oT_ready, 1)
                for p in range(2):
                    g = 2 * i + p
                    act.wait_ge(x2T_mm, g + 1)
                    act.activation(x2T[:, p], bank[4 * p][:, :], ACT.Copy).then_inc(x2T_ready, 1)
                for p in range(2):
                    g = 2 * i + p
                    act.wait_ge(lg_sub, g + 1)
                    act.activation(lg[:, p], lg[:, p], ACT.Exp).then_inc(lg_exp, 1)
                for p in range(2):
                    g = 2 * i + p
                    act.wait_ge(pT_mm, g + 1)
                    act.activation(kb[:, bass.ds(g * P, P)], bank[4 * p + 3][:, 0:P], ACT.Copy).then_inc(pT_ready, 1)

            with act.Fori(0, NG // 2 - 1) as i:
                pair(i, True)
            pair(NG // 2 - 1, False)

            for k in range(0, 8, 2):
                act.wait_ge(pcT_mm, k + 1)
                act.activation(pc[:, 4 * k:4 * k + 4], bank[k][:, :].rearrange("p (e t) -> p e t", e=4), ACT.Copy).then_inc(pc_ready, 1)
            act.wait_ge(bup_mm, 1)
            act.activation(bupT[:, 0:2], bank[1][:, 0:16].rearrange("p (k u) -> p k u", k=2), ACT.Copy).then_inc(bup_ready, 1)
            act.activation(bupT[0:FCH[2], 2], bank[1][0:FCH[2], 16:24], ACT.Copy).then_inc(bup_ready, 1)

            for h in range(H1):
                act.wait_ge(wT_mm, h + 1)
                act.activation(wT[:], bank[2][:, 0:3 * C].rearrange("p (k c) -> p k c", k=3), ACT.Copy).then_inc(wT_ready, 1)
                act.wait_ge(fold_mm, h + 1)
                act.activation(wqk[:, h], bank[3][:, 0:C], ACT.Copy, scale=float(C) ** -0.5).then_inc(fold_ready, 1)
                act.activation(wvo[:, h], bank[3][:, C:2 * C], ACT.Copy).then_inc(fold_ready, 1)

            act.wait_ge(b1_mm, 1)
            act.activation(b1T[:], bank[2][:, 0:2 * E1].rearrange("p (k x) -> p k x", k=2), ACT.Copy).then_inc(b1_ready, 1)
            act.wait_ge(bup_ready, 2)
            act.wait_ge(consts2, 10)

            def hidden(v):
                if not first(v):
                    act.wait_ge(ac_ready, 12 * v)
                act.activation(bupg[:, 0:2], bupT[:, 0:2, bass.ds(v, 1)].rearrange("p k a -> p (k a)"), ACT.Copy).then_inc(bup_ready, 1)
                act.activation(bupg[0:FCH[2], 2:3], bupT[0:FCH[2], 2, bass.ds(v, 1)], ACT.Copy).then_inc(bup_ready, 1)
                act.wait_ge(bup_ready, 4 + 2 * v)
                for q in range(4):
                    e = 4 * v + q
                    act.wait_ge(xeT_mm, e + 1)
                    act.activation(xeT[:], bank[0][:, :], ACT.Copy).then_inc(xeT_ready, 1)
                    for k in range(3):
                        act.wait_ge(up_mm, 3 * e + k + 1)
                        act.activation(ac[0:FCH[k], k], bank[1 + k][0:FCH[k], :], ACT.Silu, bias=bupg[0:FCH[k], k:k + 1])\
                            .then_inc(ac_ready, 1)
            hidden(0)
            with act.Fori(1, NU) as v:
                hidden(v)

            def turned(n, p):
                act.wait_ge(xT3_mm, n + 1)
                act.activation(xT3[:, p], bank[VBANK][:, 0:2 * P], ACT.Copy).then_inc(xT3_ready, 1)

            def exps(u, h):
                act.wait_ge(max_ready, u + 1)
                if not isinstance(u, int) or u >= 4:
                    act.wait_ge(prT_mm, u - 3)
                s2 = bank[SBANK[h % 2]]
                act.activation(pr[:, h % 4, 0:P], s2[:, 0:P], ACT.Exp, bias=nmax[:, h % 4, 0:1],
                               accum_out=rsum[:, h % 4, 0:1])
                act.activation(pr[:, h % 4, P:3 * P], s2[:, P:3 * P], ACT.Exp, bias=nmax[:, h % 4, 1:2],
                               accum_out=rsum[:, h % 4, 1:2]).then_inc(exp_ready, 1)

            turned(0, 0)

            def heads(i, last):
                for p in range(2):
                    n = 2 * i + p
                    for h in range(H1):
                        u = H1 * n + h
                        if h % 2 == 0:
                            act.wait_ge(g_mm, 4 * n + h // 2 + 1)
                            act.activation(gT[:, h // 2 % 2], bank[GBANK][:, :], ACT.Copy).then_inc(g_ready, 1)
                        if h < 4:
                            act.wait_ge(vo_mm, 4 * n + h + 1)
                            act.activation(vo[:, p, h % 2, (h // 2) * 512:(h // 2 + 1) * 512], bank[VBANK][:, :], ACT.Copy)\
                                .then_inc(vo_ready, 1)
                        if h == 5 and not (last and p == 1):
                            turned(n + 1, 1 - p)
                        if there(u - S_LAG):
                            exps(u - S_LAG, (h - S_LAG) % H1)
            heads(0, False)
            with act.Fori(1, NB // 2 - 1) as i:
                heads(i, False)
            heads(NB // 2 - 1, True)
            exps(NB * H1 - 1, H1 - 1)

            act.wait_ge(b1_ready, 1)

            def last_layer(i):
                for p in range(2):
                    g = 2 * i + p
                    act.wait_ge(xT4_mm, g + 1)
                    act.activation(xT4[:, p], bank[0][:, :], ACT.Copy).then_inc(xT4_ready, 1)
                    act.wait_ge(gap_ready, g + 1)
                    act.activation(tw[:, 1], gap[:], ACT.Exp).then_inc(gap_exp, 1)
                    act.wait_ge(wtT_mm, g + 1)
                    act.activation(wtT, bank[2][0:E1, :], ACT.Copy).then_inc(wtT_ready, 1)
                    for x in range(E1):
                        for k in range(2):
                            act.wait_ge(up1_mm, (E1 * g + x) * 2 + k + 1)
                            if not (isinstance(g, int) and g == 0 and x < 2):
                                act.wait_ge(dn1_mm, E1 * g + x - 1)
                            act.activation(hT[:, x % 2, k], bank[4 + k][:, :], ACT.Relu, bias=b1T[:, k, x:x + 1]).then_inc(hT_ready, 1)
            last_layer(0)
            with act.Fori(1, NG // 2) as i:
                last_layer(i)

        @block.vector
        def _(dve):
            dve.wait_ge(w_in, 16 * 7)
            dve.tensor_copy(idrowf[:], idrow[:]).then_inc(prep_c, 1)
            dve.wait_ge(consts, 7)
            dve.tensor_scalar(headt[:], head[:], temp[:, 0:1], None, ALU.mult).then_inc(prep_c, 1)

            def stats(src, p, steps):
                for j in range(TG):
                    steps.done(dve.bn_stats(st[:, p, j], src[:, p, j]))
                steps.wait()
                dve.nop(nofuse=True)
                for j in range(TG):
                    ins = dve.bn_aggr(mv[:, p, j], st[:, p, j])
                steps.done(ins)

            def inv_sqrt(steps, v, y, t, h):
                steps.done(dve.tensor_scalar(h, v, EPS, None, ALU.add))
                steps.wait()
                steps.done(dve.tensor_scalar(t.bitcast(U32), h.bitcast(U32), 1, None, ALU.logical_shift_right))
                steps.wait()
                steps.done(dve.tensor_scalar(y.bitcast(I32), t.bitcast(I32), -1.0, float(0x5F3759DF), ALU.mult, ALU.add))
                steps.done(dve.tensor_scalar(h, h, -0.5, None, ALU.mult))
                steps.wait()
                for _ in range(3):
                    steps.done(dve.tensor_tensor(t, y, y, ALU.mult))
                    steps.wait()
                    steps.done(dve.tensor_tensor(t, t, h, ALU.mult))
                    steps.wait()
                    steps.done(dve.scalar_tensor_tensor(out=y, in0=t, scalar=1.5, in1=y, op0=ALU.add, op1=ALU.mult))
                    steps.wait()

            def normalise(dst, src, p, out_sem):
                for j in range(TG):
                    ins = dve.tensor_scalar(dst[:, p, j, 0:C], src[:, p, j], mv[:, p, j, 0:1], rs[:, p, j:j + 1],
                                            ALU.subtract, ALU.mult)
                ins.then_inc(out_sem, 1)

            PER_LN = 2 * TG + 2 + 13
            REST = 2 * (2 + 2 + 2) + PER_LN

            def ln_first(i, steps):
                for p in range(2):
                    g = 2 * i + p
                    dve.wait_ge(gathered[p], 64 * (i + 1))
                    stats(xg, p, steps)
                steps.wait()
                inv_sqrt(steps, mv[:, :, :, 1], rs[:], rt[:], lnv[:])
                for p in range(2):
                    g = 2 * i + p
                    if not first(i):
                        dve.wait_ge(xT_mm, g - 1)
                    normalise(xn, xg, p, xn_ready)

            steps = Steps(dve, dve_step)
            ln_first(0, steps)
            assert steps.n == PER_LN, steps.n

            def pair(i, more):
                steps = Steps(dve, dve_step, PER_LN + (REST + PER_LN) * i)
                for p in range(2):
                    g = 2 * i + p
                    s4 = bank[4 * p][:, 0:2 * (C + 1)].rearrange("p (b n) -> p b n", b=2)
                    dve.wait_ge(kvs_mm, g + 1)
                    dve.tensor_tensor(md[:, p, :, 0:C], s4[:, :, 0:C], mtemp[:].unsqueeze(1).to_broadcast([P, 2, C]), ALU.mult)
                    dve.tensor_tensor(md[:, p, :, C:C + H0], headc[:].unsqueeze(1).to_broadcast([P, 2, H0]),
                                      s4[:, :, C:C + 1].to_broadcast([P, 2, H0]), ALU.mult).then_inc(md_ready, 1)
                for p in range(2):
                    g = 2 * i + p
                    for m in range(2):
                        o5 = bank[4 * p + 1 + m][:, 0:2 * (C + H0)].rearrange("p (j n) -> p j n", j=2)
                        dve.wait_ge(o_mm, 2 * g + m + 1)
                        last = dve.tensor_scalar(den[:, p, 2 * m:2 * m + 2], o5[:, :, C:C + H0], 100.0, None, ALU.max)
                    steps.done(last)
                    steps.wait()
                    steps.done(dve.reciprocal(den[:, p], den[:, p]))
                    steps.wait()
                    for m in range(2):
                        for j in range(2):
                            o5 = bank[4 * p + 1 + m][:, j * (C + H0):j * (C + H0) + C].rearrange("p (h d) -> p h d", h=H0)
                            last = dve.tensor_tensor(oo[:, p, 2 * m + j].rearrange("p (h d) -> p h d", h=H0), o5,
                                                     den[:, p, 2 * m + j].unsqueeze(2).to_broadcast([P, H0, D0]), ALU.mult)
                    last.then_inc(o_ready, 1)
                for p in range(2):
                    g = 2 * i + p
                    dve.wait_ge(y_mm, g + 1)
                    dve.wait_ge(xb_ready, g + 1)
                    if not first(i):
                        dve.wait_ge(stored[p], 32 * i)
                    dve.tensor_tensor(h1[:, p], bank[4 * p + 1][:, :].rearrange("p (j c) -> p j c", j=TG), xb[:, p], ALU.add)\
                        .then_inc(h1_ready, 1)
                    dve.wait_ge(h1_ready, g + 1)
                    stats(h1, p, steps)
                steps.wait()
                inv_sqrt(steps, mv[:, :, :, 1], rs[:], rt[:], lnv[:])
                for p in range(2):
                    normalise(xr, h1, p, x2_ready)
                if more:
                    ln_first(i + 1, steps)
                for p in range(2):
                    g = 2 * i + p
                    dve.wait_ge(lg_mm, g + 1)
                    steps.done(dve.tensor_tensor(lg[:, p], bank[4 * p + 2][:, 0:TG * E0].rearrange("p (j e) -> p j e", j=TG),
                                                 brout[:].unsqueeze(1).to_broadcast([P, TG, E0]), ALU.add))
                    steps.wait()
                    steps.done(dve.tensor_reduce(mx[:, p], lg[:, p], AX.X, ALU.max))
                    steps.wait()
                    dve.tensor_tensor(lg[:, p], lg[:, p], mx[:, p].unsqueeze(2).to_broadcast([P, TG, E0]), ALU.subtract)\
                        .then_inc(lg_sub, 1)
                for p in range(2):
                    g = 2 * i + p
                    dve.wait_ge(lg_exp, g + 1)
                    steps.done(dve.tensor_reduce(sm[:, p], lg[:, p], AX.X, ALU.add))
                    steps.wait()
                    steps.done(dve.reciprocal(sm[:, p], sm[:, p]))
                    steps.wait()
                    if not first(i):
                        dve.wait_ge(pa_ready, g - 1)
                        dve.wait_ge(pT_mm, g - 1)
                    dve.tensor_tensor(pg[:, p], lg[:, p], sm[:, p].unsqueeze(2).to_broadcast([P, TG, E0]), ALU.mult)
                    dve.tensor_tensor(xr[:, p, :, C:ROW], lg[:, p], sm[:, p].unsqueeze(2).to_broadcast([P, TG, E0]), ALU.mult)\
                        .then_inc(p_ready, 1)
                return steps.n

            assert pair(0, True) == REST + PER_LN
            with dve.Fori(1, NG // 2 - 1) as i:
                pair(i, True)
            pair(NG // 2 - 1, False)

            for k in range(1, 8, 2):
                dve.wait_ge(pcT_mm, k + 1)
                dve.tensor_copy(pc[:, 4 * k:4 * k + 4], bank[k][:, :].rearrange("p (e t) -> p e t", e=4)).then_inc(pc_ready, 1)

            dve.wait_ge(pT_ready, NG)
            find = Steps(dve, find_step)
            find.done(dve.memset(thr[:], 0))
            find.done(dve.memset(bit[:], 1 << 29))
            find.done(dve.memset(cand[:], 1 << 29))
            find.wait()

            def settle(b):
                n = Steps(dve, find_step, 3 + 4 * b)
                dve.tensor_scalar(junk[:], kb[:], cand[:, 0:1].bitcast(F32), None, ALU.is_ge, ALU.add, accum_out=cnt[:, 0:1])\
                    .then_inc(cnt_ready, 1)
                dve.wait_ge(cnt_mm, b + 1)
                n.done(dve.tensor_scalar(keep[:].bitcast(I32), bank[0][:, 0:1], float(CAP), -1.0, ALU.is_ge, ALU.mult))
                n.wait()
                n.done(dve.scalar_tensor_tensor(out=thr[:], in0=keep[:], scalar=bit[:, 0:1], in1=thr[:],
                                                op0=ALU.bitwise_and, op1=ALU.bitwise_or))
                n.wait()
                n.done(dve.tensor_scalar(bit[:], bit[:], 1, None, ALU.logical_shift_right))
                n.wait()
                n.done(dve.tensor_tensor(cand[:], thr[:], bit[:], ALU.bitwise_or))
                n.wait()
            with dve.Fori(0, 30) as b:
                settle(b)
            dve.tensor_scalar(junk[:], kb[:], thr[:, 0:1].bitcast(F32), None, ALU.is_gt, ALU.add, accum_out=cnt[:, 0:1])\
                .then_inc(cnt_ready, 1)
            dve.wait_ge(cnt_mm, 31)
            find = Steps(dve, find_step, 3 + 4 * 30)
            find.done(dve.tensor_scalar(quota[:], bank[0][:, 0:1], -1.0, float(CAP), ALU.mult, ALU.add))
            find.wait()
            dve.tensor_scalar(diag[:, 0], ident[0:E0, 0:E0], thr[0:E0, 0:1].bitcast(F32), None, ALU.mult)
            dve.tensor_scalar(diag[:, 1], ident[0:E0, 0:E0], quota[0:E0, 0:1], None, ALU.mult).then_inc(diag_ready, 1)
            dve.wait_ge(tq_mm, 1)
            dve.tensor_copy(tq[:], bank[1][:, 0:2 * E0].rearrange("p (k e) -> p k e", k=2)).then_inc(tq_ready, 1)
            dve.wait_ge(tq_ready, 1)
            dve.wait_ge(pc_ready, 8)
            dve.wait_ge(consts2, 10)

            def rank(e, n):
                v = pc[:, bass.ds(e, 1)].rearrange("p a t -> p (a t)")
                n.done(dve.tensor_scalar(sel[:, 0], v, tq[:, 0, bass.ds(e, 1)], None, ALU.is_gt))
                n.done(dve.tensor_scalar(sel[:, 1], v, tq[:, 0, bass.ds(e, 1)], None, ALU.is_equal))
                n.wait()
                dve.tensor_tensor_scan(cum[:, 0], ones[:], sel[:, 0], 0.0, ALU.mult, ALU.add)
                dve.tensor_tensor_scan(cum[:, 1], ones[:], sel[:, 1], 0.0, ALU.mult, ALU.add).then_inc(cum_ready, 1)

            def place(e, n):
                dve.wait_ge(base_mm, e + 1)
                n.done(dve.tensor_copy(base[:], bank[7][:, 0:2]))
                n.wait()
                q = tq[:, 1, bass.ds(e, 1)]
                n.done(dve.tensor_scalar(edge[:, 0:1], base[:, 1:2], q, base[:, 0:1], ALU.min, ALU.add))
                n.done(dve.tensor_scalar(sel[:, 1], cum[:, 1], base[:, 1:2], q, ALU.add, ALU.min))
                n.wait()
                n.done(dve.scalar_tensor_tensor(out=tab[:, 0:P], in0=cum[:, 0], scalar=base[:, 0:1], in1=sel[:, 1],
                                                op0=ALU.add, op1=ALU.add))
                n.done(dve.tensor_scalar(from0[:], slot16[:], edge[:, 0:1], None, ALU.is_ge))
                n.wait()
                n.done(dve.tensor_copy(edge[:, 1:2], tab[:, P - 1:P]))
                n.wait()
                dve.scalar_tensor_tensor(out=oneh[:], in0=slot16[:], scalar=edge[:, 1:2], in1=from0[:],
                                         op0=ALU.is_lt, op1=ALU.mult).then_inc(oneh_ready, 1)

            def number(e, p, n, guard):
                dve.wait_ge(tab_mm, e + 1)
                n.done(dve.tensor_copy(tbase[:].rearrange("p (k c) -> p k c", k=2)[:, 0], bank[5][:, 0:2 * (P + 1)].rearrange("p (c t) -> p c t", c=2)[:, :, P]))
                n.done(dve.tensor_copy(tbase[:].rearrange("p (k c) -> p k c", k=2)[:, 1], bank[6][:, 0:2 * (P + 1)].rearrange("p (c t) -> p c t", c=2)[:, :, P]))
                n.wait()
                for c in range(TG):
                    row = bank[5 + c // 2][:, (c % 2) * (P + 1):(c % 2) * (P + 1) + P]
                    ins = dve.tensor_scalar(junk[:, c * P:(c + 1) * P], row, slotc[:, c:c + 1], tbase[:, c:c + 1], ALU.is_le, ALU.add,
                                            accum_out=cnt4[:, c:c + 1])
                    if c == TG - 1:
                        n.done(ins)
                n.wait()
                if guard is not None:
                    dve.wait_ge(added[p], guard)
                dve.tensor_copy(idx[:, p], cnt4[:]).then_inc(idx_ready, 1)

            def weigh(e, p, n, guard):
                dve.wait_ge(xe_in[p], guard)
                n.done(dve.tensor_copy(gate[:, p], xe[:, p, :, bass.ds(C + e, 1)].rearrange("p c a -> p (c a)")))
                n.wait()
                dve.wait_ge(dn_mm, e + 1)
                dve.tensor_tensor(ye[:, p], bank[4][:, :].rearrange("p (c h) -> p c h", c=TG),
                                  gate[:, p].unsqueeze(2).to_broadcast([P, TG, C]), ALU.mult).then_inc(ye_ready, 1)

            PER = 12
            n = Steps(dve, sel_step)
            rank(0, n)
            place(0, n)
            number(0, 0, n, None)
            rank(1, n)
            pre = n.n

            def serve(v, last):
                n = Steps(dve, sel_step, pre + 4 * PER * v)
                for q in range(4):
                    e, p = 4 * v + q, q % 2
                    if not (last and q == 3):
                        place(e + 1, n)
                        guard = None if first(v) and q == 0 else 64 * (2 * v + (q + 1) // 2)
                        number(e + 1, 1 - p, n, guard)
                    weigh(e, p, n, 64 * (2 * v + q // 2 + 1))
                    if not (last and q >= 2):
                        rank(e + 2, n)
                return n.n
            assert serve(0, False) == 4 * PER
            with dve.Fori(1, NU - 1) as v:
                serve(v, False)
            serve(NU - 1, True)

            PREP = 2 + 1 + 13

            def prep(n, p, i, n_):
                dve.wait_ge(h2_in[p], 16 * (i + 1))
                for j in range(2):
                    n_.done(dve.bn_stats(st3[:, j], hx[:, p, j]))
                n_.wait()
                dve.nop(nofuse=True)
                for j in range(2):
                    ins = dve.bn_aggr(mv3[:, j], st3[:, j])
                n_.done(ins)
                n_.wait()
                inv_sqrt(n_, mv3[:, :, 1], r3[:, 0], r3[:, 1], r3[:, 2])
                if not first(n):
                    dve.wait_ge(xT3_mm, n)
                for j in range(2):
                    ins = dve.tensor_scalar(xn3[:, j], hx[:, p, j], mv3[:, j, 0:1], r3[:, 0, j:j + 1], ALU.subtract, ALU.mult)
                ins.then_inc(xn3_ready, 1)

            def maxima(u, h):
                dve.wait_ge(s_mm, u + 1)
                s2 = bank[SBANK[h % 2]]
                dve.tensor_reduce(nmax[:, h % 4, 0:1], s2[:, 0:P], AX.X, ALU.max, negate=True)
                dve.tensor_reduce(nmax[:, h % 4, 1:2], s2[:, P:3 * P], AX.X, ALU.max, negate=True).then_inc(max_ready, 1)

            def norms(u, h):
                dve.wait_ge(exp_ready, u + 1)
                dve.reciprocal(rinv[:, h % 4], rsum[:, h % 4]).then_inc(rinv_ready, 1)
                dve.wait_ge(rinv_ready, u + 1)
                dve.tensor_scalar(pr[:, h % 4, 0:P], pr[:, h % 4, 0:P], rinv[:, h % 4, 0:1], None, ALU.mult)
                dve.tensor_scalar(pr[:, h % 4, P:3 * P], pr[:, h % 4, P:3 * P], rinv[:, h % 4, 1:2], None, ALU.mult)\
                    .then_inc(pr_ready, 1)

            def turn(u, h):
                dve.wait_ge(prT_mm, u + 1)
                if not isinstance(u, int) or u >= 2:
                    dve.wait_ge(head_mm, u - 1)
                dve.tensor_copy(prT[:, h % 2], bank[TBANK[h % 2]][:, 0:3 * P]).then_inc(prT_ready, 1)

            n_ = Steps(dve, prep_step)
            prep(0, 0, 0, n_)
            assert n_.n == PREP, n_.n

            def finish(n, q, i, p):
                dve.wait_ge(head_mm, H1 * n + H1)
                dve.wait_ge(hb_ready, n + 1)
                if not isinstance(n, int) or n >= 2:
                    dve.wait_ge(h3_out[q], 16 * (i - 1 + p))
                dve.tensor_tensor(h3[:, q], bank[OBANK[q]][:, 0:2 * P].rearrange("p (j c) -> p j c", j=2), hb[:, q], ALU.add)\
                    .then_inc(h3_ready, 1)

            def slots(i, last):
                for p in range(2):
                    n = 2 * i + p
                    for h in range(H1):
                        u = H1 * n + h
                        if there(u - S_LAG):
                            maxima(u - S_LAG, (h - S_LAG) % H1)
                        if there(u - T_LAG):
                            turn(u - T_LAG, (h - T_LAG) % H1)
                        if h == 0 and not (last and p == 1):
                            prep(n + 1, 1 - p, i + p, Steps(dve, prep_step, PREP * (n + 1)))
                        if there(u - S_LAG):
                            norms(u - S_LAG, (h - S_LAG) % H1)
                        if h == O_LAG - 1 and there(u - O_LAG):
                            finish(n - 1, 1 - p, i, p)
            slots(0, False)
            with dve.Fori(1, NB // 2 - 1) as i:
                slots(i, False)
            slots(NB // 2 - 1, True)
            U = NB * H1
            maxima(U - 1, H1 - 1)
            turn(U - 3, H1 - 3)
            norms(U - 1, H1 - 1)
            turn(U - 2, H1 - 2)
            turn(U - 1, H1 - 1)
            finish(NB - 1, 1, NB // 2, 0)

            dve.wait_ge(consts4, 2)
            dve.wait_ge(w_d, 16 * 4)

            def last_layer(i):
                for p in range(2):
                    g = 2 * i + p
                    n_ = Steps(dve, d_step, D_STEPS * g)
                    dve.wait_ge(h3_in[p], 16 * (i + 1))
                    for j in range(TG):
                        n_.done(dve.bn_stats(st4[:, j], h4x[:, p, j]))
                    n_.wait()
                    dve.nop(nofuse=True)
                    for j in range(TG):
                        ins = dve.bn_aggr(mv4[:, j], st4[:, j])
                    n_.done(ins)
                    n_.wait()
                    inv_sqrt(n_, mv4[:, :, 1], r4[:, 0], r4[:, 1], r4[:, 2])
                    for j in range(TG):
                        ins = dve.tensor_scalar(xn4[:, j], h4x[:, p, j], mv4[:, j, 0:1], r4[:, 0, j:j + 1], ALU.subtract, ALU.mult)
                    ins.then_inc(xn4_ready, 1)
                    dve.wait_ge(gate_mm, g + 1)
                    n_.done(dve.tensor_tensor(lg4[:], bank[1][:, 0:TG * E1].rearrange("p (j x) -> p j x", j=TG),
                                              gb[:].unsqueeze(1).to_broadcast([P, TG, E1]), ALU.add))
                    n_.wait()
                    dve.nop(nofuse=True)
                    for j in range(TG):
                        ins = dve.max(top[:, j], lg4[:, j])
                    n_.done(ins)
                    n_.wait()
                    dve.nop(nofuse=True)
                    for j in range(TG):
                        ins = dve.max_index(topi[:, j], top[:, j], lg4[:, j])
                    n_.done(ins)
                    dve.tensor_tensor(gap[:], top[:, :, 1], top[:, :, 0], ALU.subtract).then_inc(gap_ready, 1)
                    n_.wait()
                    n_.done(dve.tensor_copy(topf[:], topi[:, :, 0:2]))
                    n_.wait()
                    for k in range(2):
                        ins = dve.tensor_tensor(hit[:, k], which[:].unsqueeze(1).to_broadcast([P, TG, E1]),
                                                topf[:, :, k:k + 1].to_broadcast([P, TG, E1]), ALU.is_equal)
                    n_.done(ins)
                    dve.wait_ge(gap_exp, g + 1)
                    n_.done(dve.tensor_scalar(tw[:, 0], tw[:, 1], 1.0, None, ALU.add))
                    n_.wait()
                    n_.done(dve.reciprocal(tw[:, 0], tw[:, 0]))
                    n_.wait()
                    n_.done(dve.tensor_tensor(tw[:, 1], tw[:, 1], tw[:, 0], ALU.mult))
                    n_.wait()
                    for k in range(2):
                        ins = dve.tensor_tensor(hit[:, k], hit[:, k], tw[:, k].unsqueeze(2).to_broadcast([P, TG, E1]), ALU.mult)
                    n_.done(ins)
                    n_.wait()
                    dve.tensor_tensor(wt[:, p], hit[:, 0], hit[:, 1], ALU.add).then_inc(wt_ready, 1)
                    dve.wait_ge(b2_mm, g + 1)
                    if not first(i):
                        dve.wait_ge(out_done[p], 16 * i)
                    n_.done(dve.tensor_tensor(acc[:, p], bank[3][:, :].rearrange("p (j c) -> p j c", j=TG), h4x[:, p], ALU.add))
                    for x in range(E1):
                        n_.wait()
                        dve.wait_ge(dn1_mm, E1 * g + x + 1)
                        for j in range(TG):
                            ins = dve.scalar_tensor_tensor(out=acc[:, p, j], in0=bank[6 + x % 2][:, j * C:(j + 1) * C],
                                                           scalar=wt[:, p, j, x:x + 1], in1=acc[:, p, j], op0=ALU.mult, op1=ALU.add)
                        if x < E1 - 1:
                            n_.done(ins)
                        else:
                            ins.then_inc(acc_ready, 1)
                    assert n_.n == D_STEPS, n_.n
            D_STEPS = TG + 1 + 13 + 9 + 1 + 7
            last_layer(0)
            with dve.Fori(1, NG // 2) as i:
                last_layer(i)

        @block.tensor
        def _(pe):
            pe.wait_ge(consts, 7)
            pe.wait_ge(w_in, 16 * 7)
            pe.wait_ge(prep_c, 2)
            pe.transpose(bank[0][:, 0:P], idrowf[:], ident[:]).then_inc(prep_t, 1)
            for k in range(3):
                pe.transpose(bank[1][:, k * P:(k + 1) * P], wqkv_n[:, k], ident[:]).then_inc(prep_t, 1)
            pe.transpose(bank[2][:, 0:P], wproj_n[:], ident[:]).then_inc(prep_t, 1)
            pe.transpose(bank[3][:, 0:H0], head[:], ident[0:H0, 0:H0]).then_inc(prep_t, 1)
            pe.matmul(bank[4][:, 0:P], headt[:], head[:], start=True, stop=True).then_inc(prep_t, 1)
            pe.wait_ge(prep_c, 6)

            def pair(i):
                for p in range(2):
                    g = 2 * i + p
                    pe.wait_ge(xn_ready, g + 1)
                    for j in range(TG):
                        ins = pe.transpose(bank[4 * p][:, j * P:(j + 1) * P], xn[:, p, j], ident[:])
                    ins.then_inc(xT_mm, 1)
                for p in range(2):
                    g = 2 * i + p
                    pe.wait_ge(xT_ready, g + 1)
                    for m in range(2):
                        for j in range(2):
                            t = 2 * m + j
                            ins = pe.matmul(bank[4 * p + 1 + m][:, j * 2 * C:(j + 1) * 2 * C], xT[:, p, t * P:(t + 1) * P],
                                            wqkvT[:, C:3 * C], start=True, stop=True)
                        ins.then_inc(kv_mm, 1)
                for p in range(2):
                    g = 2 * i + p
                    if not first(i):
                        pe.wait_ge(pT_ready, g - 1)
                    pe.matmul(bank[4 * p + 3][:, :], wqkvT[:, 0:C], xT[:, p], start=True, stop=True).then_inc(q_mm, 1)
                for p in range(2):
                    g = 2 * i + p
                    pe.wait_ge(kv_ready, 4 * g + 4)
                    for b in range(2):
                        for j in range(2):
                            ins = pe.matmul(bank[4 * p][:, b * (C + 1):(b + 1) * (C + 1)], kk[:, p, 2 * b + j],
                                            vv[:, p, 2 * b + j], start=(j == 0), stop=(j == 1))
                    ins.then_inc(kvs_mm, 1)
                for p in range(2):
                    g = 2 * i + p
                    pe.wait_ge(q_ready, g + 1)
                    pe.wait_ge(md_ready, g + 1)
                    for m in range(2):
                        for j in range(2):
                            t = 2 * m + j
                            ins = pe.matmul(bank[4 * p + 1 + m][:, j * (C + H0):(j + 1) * (C + H0)], qT[:, p, t * P:(t + 1) * P],
                                            md[:, p, m], start=True, stop=True)
                        ins.then_inc(o_mm, 1)
                for p in range(2):
                    g = 2 * i + p
                    pe.wait_ge(o_ready, g + 1)
                    for j in range(TG):
                        ins = pe.transpose(bank[4 * p][:, j * P:(j + 1) * P], oo[:, p, j], ident[:])
                    ins.then_inc(oT_mm, 1)
                for p in range(2):
                    g = 2 * i + p
                    pe.wait_ge(oT_ready, g + 1)
                    for j in range(TG):
                        ins = pe.matmul(bank[4 * p + 1][:, j * P:(j + 1) * P], oT[:, p, j * P:(j + 1) * P], wprojT[:],
                                        start=True, stop=True)
                    ins.then_inc(y_mm, 1)
                for p in range(2):
                    g = 2 * i + p
                    pe.wait_ge(x2_ready, g + 1)
                    for j in range(TG):
                        ins = pe.transpose(bank[4 * p][:, j * P:(j + 1) * P], xr[:, p, j, 0:C], ident[:])
                    ins.then_inc(x2T_mm, 1)
                for p in range(2):
                    g = 2 * i + p
                    pe.wait_ge(x2T_ready, g + 1)
                    for j in range(TG):
                        ins = pe.matmul(bank[4 * p + 2][:, j * E0:(j + 1) * E0], x2T[:, p, j * P:(j + 1) * P], wrout[:],
                                        start=True, stop=True)
                    ins.then_inc(lg_mm, 1)
                for p in range(2):
                    g = 2 * i + p
                    pe.wait_ge(p_ready, g + 1)
                    pe.transpose(bank[4 * p + 3][:, 0:P], pg[:, p].rearrange("p j e -> p (j e)"), ident[:]).then_inc(pT_mm, 1)

            pair(0)
            with pe.Fori(1, NG // 2) as i:
                pair(i)

            pe.wait_ge(pa_ready, NG)
            pe.wait_ge(pT_ready, NG)
            for k in range(8):
                for j in range(4):
                    ins = pe.transpose(bank[k][:, j * P:(j + 1) * P], pa[:, :, 4 * k + j], ident[:])
                ins.then_inc(pcT_mm, 1)
            pe.wait_ge(w_b, 16)
            pe.wait_ge(pc_ready, 8)
            for k in range(3):
                ins = pe.transpose(bank[1][0:FCH[k], 8 * k:8 * k + 8], bup_n[:, k * P:k * P + FCH[k]], ident[0:8, 0:8])
            ins.then_inc(bup_mm, 1)
            pe.wait_ge(bup_ready, 2)
            pe.wait_ge(lanes_s, 4)

            def count(b):
                pe.wait_ge(cnt_ready, b + 1)
                pe.matmul(bank[0][:, 0:1], lanes[:], cnt[:, 0:1], start=True, stop=True).then_inc(cnt_mm, 1)

            pe.wait_ge(w_c, 16 * 5)
            for h in range(H1):
                count(h)
                if h > 0:
                    pe.wait_ge(fold_ready, 2 * h)
                for k, w in enumerate((wqn, wkn, wvn)):
                    ins = pe.transpose(bank[2][:, k * C:(k + 1) * C], w[:, h * C:(h + 1) * C], ident[:])
                ins.then_inc(wT_mm, 1)
                pe.wait_ge(wT_ready, h + 1)
                pe.matmul(bank[3][:, 0:C], wT[:, 0], wT[:, 1], start=True, stop=True)
                pe.matmul(bank[3][:, C:2 * C], wT[:, 2], won[:, h], start=True, stop=True).then_inc(fold_mm, 1)
            pe.wait_ge(w_d, 16 * 4)
            pe.wait_ge(fold_ready, 2 * H1)
            for k in range(2):
                ins = pe.transpose(bank[2][:, k * E1:(k + 1) * E1], b1n[:, k * P:(k + 1) * P], ident[0:E1, 0:E1])
            ins.then_inc(b1_mm, 1)
            with pe.Fori(H1, 31) as b:
                count(b)
            pe.wait_ge(diag_ready, 1)
            for k in range(2):
                ins = pe.matmul(bank[1][:, k * E0:(k + 1) * E0], ones[0:E0, :], diag[:, k], start=True, stop=True)
            ins.then_inc(tq_mm, 1)

            def bases(e):
                pe.wait_ge(cum_ready, e + 1)
                pe.matmul(bank[7][:, 0:2], before[:], cum[:, :, P - 1], start=True, stop=True).then_inc(base_mm, 1)

            def rows(e):
                pe.wait_ge(oneh_ready, e + 1)
                for c in range(TG):
                    o = bank[5 + c // 2][:, (c % 2) * (P + 1):(c % 2 + 1) * (P + 1)]
                    ins = pe.matmul(o, oneh[:, c * P:(c + 1) * P], tab[:], start=True, stop=True)
                ins.then_inc(tab_mm, 1)

            pe.wait_ge(tq_ready, 1)
            bases(0)
            rows(0)
            bases(1)

            def serve(v, last):
                for q in range(4):
                    e, p = 4 * v + q, q % 2
                    pe.wait_ge(xe_in[p], 64 * (2 * v + q // 2 + 1))
                    for c in range(TG):
                        ins = pe.transpose(bank[0][:, c * P:(c + 1) * P], xe[:, p, c, 0:C], ident[:])
                    ins.then_inc(xeT_mm, 1)
                    pe.wait_ge(xeT_ready, e + 1)
                    pe.wait_ge(wup_in[p], 16 * (2 * v + q // 2 + 1))
                    for k in range(3):
                        pe.matmul(bank[1 + k][0:FCH[k], :], wup[:, p, k * P:k * P + FCH[k]], xeT[:], start=True, stop=True)\
                            .then_inc(up_mm, 1)
                    if not (last and q == 3):
                        rows(e + 1)
                    pe.wait_ge(ac_ready, 3 * e + 3)
                    pe.wait_ge(wdn_in[p], 48 * (2 * v + q // 2 + 1))
                    if not (first(v) and q == 0):
                        pe.wait_ge(ye_ready, e)
                    for c in range(TG):
                        for k in range(3):
                            m = FCH[k] + (k == 2)
                            ins = pe.matmul(bank[4][:, c * P:(c + 1) * P], ac[0:m, k, c * P:(c + 1) * P], wdn[0:m, p, k],
                                            start=(k == 0), stop=(k == 2))
                    ins.then_inc(dn_mm, 1)
                    if not (last and q >= 2):
                        bases(e + 2)
            serve(0, False)
            with pe.Fori(1, NU - 1) as v:
                serve(v, False)
            serve(NU - 1, True)

            pe.wait_ge(fold_ready, 2 * H1)
            pe.wait_ge(consts3, 3)
            pe.wait_ge(ye_ready, E0)
            pe.wait_ge(idx_ready, E0)

            def turned(n):
                pe.wait_ge(xn3_ready, n + 1)
                if not first(n):
                    pe.wait_ge(vo_ready, 4 * n)
                for j in range(2):
                    ins = pe.transpose(bank[VBANK][:, j * P:(j + 1) * P], xn3[:, j], ident[:])
                ins.then_inc(xT3_mm, 1)

            def scores(u, h, p, n):
                s2 = bank[SBANK[h % 2]]
                g = gT[:, h // 2 % 2, (h % 2) * 2 * P:(h % 2 + 1) * 2 * P]
                pe.wait_ge(g_ready, 4 * n + h // 2 + 1)
                if not isinstance(u, int) or u >= 2:
                    pe.wait_ge(exp_ready, u - 1)
                pe.matmul(s2[:, 0:P], g[:, 0:P], xT3[:, p, 0:P], start=True, stop=False)
                pe.matmul(s2[:, 0:P], identb[:], causal[:], start=False, stop=True)
                pe.matmul(s2[:, 2 * P:3 * P], identb[:], causal[:], start=True, stop=False, skip_group_check=True)
                pe.matmul(s2[:, P:3 * P], g[:, P:2 * P], xT3[:, p], start=False, stop=True, skip_group_check=True)\
                    .then_inc(s_mm, 1)

            def turns(u, h):
                pe.wait_ge(pr_ready, u + 1)
                if not isinstance(u, int) or u >= 2:
                    pe.wait_ge(prT_ready, u - 1)
                for k in range(3):
                    ins = pe.transpose(bank[TBANK[h % 2]][:, k * P:(k + 1) * P], pr[:, h % 4, k * P:(k + 1) * P], ident[:])
                ins.then_inc(prT_mm, 1)

            def sums(u, h, p, n):
                o = bank[OBANK[p]]
                pe.wait_ge(prT_ready, u + 1)
                if h == 0:
                    pe.wait_ge(vo_ready, 4 * n + 4)
                    if not isinstance(n, int) or n >= 2:
                        pe.wait_ge(h3_ready, n - 1)
                v0, v1 = (vo[:, p, j, h * C:(h + 1) * C] for j in range(2))
                pe.matmul(o[:, 0:P], prT[:, h % 2, 0:P], v0, start=(h == 0), stop=False, skip_group_check=True)
                pe.matmul(o[:, P:2 * P], prT[:, h % 2, P:2 * P], v0, start=False, stop=False, skip_group_check=True)
                pe.matmul(o[:, P:2 * P], prT[:, h % 2, 2 * P:3 * P], v1, start=False, stop=(h == H1 - 1),
                          skip_group_check=True).then_inc(head_mm, 1)

            def slots(i, last):
                for p in range(2):
                    n = 2 * i + p
                    for h in range(H1):
                        u = H1 * n + h
                        if h == 0:
                            pe.wait_ge(xT3_ready, n + 1)
                        if h % 2 == 0:
                            for k in range(2):
                                ins = pe.matmul(bank[GBANK][:, k * 2 * P:(k + 1) * 2 * P], wqk[:, h + k], xT3[:, p], start=True, stop=True)
                            ins.then_inc(g_mm, 1)
                        if h < 4:
                            if h > 0:
                                pe.wait_ge(vo_ready, 4 * n + h)
                            pe.matmul(bank[VBANK][:, :], xT3[:, p, (h % 2) * P:(h % 2 + 1) * P],
                                      wvo[:, 4 * (h // 2):4 * (h // 2) + 4], start=True, stop=True).then_inc(vo_mm, 1)
                        if h == 5 and not (last and p == 1):
                            turned(n + 1)
                        if there(u - S_LAG):
                            scores(u - S_LAG, (h - S_LAG) % H1, p if h >= S_LAG else 1 - p, n if h >= S_LAG else n - 1)
                        if there(u - T_LAG):
                            turns(u - T_LAG, (h - T_LAG) % H1)
                        if there(u - O_LAG):
                            sums(u - O_LAG, (h - O_LAG) % H1, p if h >= O_LAG else 1 - p, n if h >= O_LAG else n - 1)
            turned(0)
            slots(0, False)
            with pe.Fori(1, NB // 2 - 1) as i:
                slots(i, False)
            slots(NB // 2 - 1, True)
            U = NB * H1
            scores(U - 1, H1 - 1, 1, NB - 1)
            turns(U - 3, H1 - 3)
            sums(U - 4, H1 - 4, 1, NB - 1)
            turns(U - 2, H1 - 2)
            sums(U - 3, H1 - 3, 1, NB - 1)
            turns(U - 1, H1 - 1)
            sums(U - 2, H1 - 2, 1, NB - 1)
            sums(U - 1, H1 - 1, 1, NB - 1)

            pe.wait_ge(h3_ready, NB)
            pe.wait_ge(vo_ready, 4 * NB)
            pe.wait_ge(b1_ready, 1)
            pe.wait_ge(w_d2, 32)

            def last_layer(i):
                for p in range(2):
                    g = 2 * i + p
                    pe.wait_ge(xn4_ready, g + 1)
                    for j in range(TG):
                        ins = pe.transpose(bank[0][:, j * P:(j + 1) * P], xn4[:, j], ident[:])
                    ins.then_inc(xT4_mm, 1)
                    pe.wait_ge(xT4_ready, g + 1)
                    for j in range(TG):
                        ins = pe.matmul(bank[1][:, j * E1:(j + 1) * E1], xT4[:, p, j * P:(j + 1) * P], gw[:], start=True, stop=True)
                    ins.then_inc(gate_mm, 1)

                    def up(x):
                        for k in range(2):
                            if not (isinstance(g, int) and g == 0 and x == 0):
                                pe.wait_ge(hT_ready, (E1 * g + x) * 2 + k - 1)
                            pe.matmul(bank[4 + k][:, :], w1s[:, x, k * P:(k + 1) * P], xT4[:, p], start=True, stop=True)\
                                .then_inc(up1_mm, 1)

                    up(0)
                    pe.wait_ge(wt_ready, g + 1)
                    for j in range(TG):
                        ins = pe.transpose(bank[2][0:E1, j * P:(j + 1) * P], wt[:, p, j], ident[:])
                    ins.then_inc(wtT_mm, 1)
                    for x in range(E1):
                        if x < E1 - 1:
                            up(x + 1)
                        if x == 0:
                            pe.wait_ge(wtT_ready, g + 1)
                            for j in range(TG):
                                ins = pe.matmul(bank[3][:, j * C:(j + 1) * C], wtT[:, j * P:(j + 1) * P], b2n[:], start=True, stop=True)
                            ins.then_inc(b2_mm, 1)
                        pe.wait_ge(hT_ready, (E1 * g + x) * 2 + 2)
                        if x >= 2:
                            pe.wait_ge(d_step, D_STEPS * g + D_STEPS - 7 + x - 1)
                        for j in range(TG):
                            for k in range(2):
                                ins = pe.matmul(bank[6 + x % 2][:, j * C:(j + 1) * C], hT[:, x % 2, k, j * P:(j + 1) * P],
                                                w2s[:, x, k], start=(k == 0), stop=(k == 1))
                        ins.then_inc(dn1_mm, 1)
            D_STEPS = TG + 1 + 13 + 9 + 1 + 7
            last_layer(0)
            with pe.Fori(1, NG // 2) as i:
                last_layer(i)


_INS = ['x', 'L0_tok_weight', 'L0_attn_Wqkv', 'L0_attn_temperature', 'L0_attn_Wproj', 'L0_attn_bproj',
        'L0_ffn_W_router', 'L0_ffn_b_router', 'L0_ffn_W_up', 'L0_ffn_b_up', 'L0_ffn_W_down', 'L0_ffn_b_down',
        'L1_attn_Wq', 'L1_attn_Wk', 'L1_attn_Wv', 'L1_attn_Wo', 'L1_attn_bo', 'L1_ffn_gate_w', 'L1_ffn_gate_b',
        'L1_ffn_w1', 'L1_ffn_b1', 'L1_ffn_w2', 'L1_ffn_b2']


def kernel(**inputs):
    import numpy as _np
    import concourse.bacc as _bacc
    from concourse import mybir as _mybir
    from concourse.bass_utils import run_bass_kernel_spmd as _run

    nc = _bacc.Bacc("TRN2", target_bir_lowering=False, num_devices=1)
    arrays, args = {}, []
    for name in _INS:
        a = _np.ascontiguousarray(inputs[name])
        arrays[f"in_{name}_dram"] = a
        args.append(nc.dram_tensor(f"in_{name}_dram", a.shape, _mybir.dt.from_np(a.dtype), kind="ExternalInput").ap())
    args.append(nc.dram_tensor("out_0_dram", (64, 256, C), F32, kind="ExternalOutput").ap())
    lm_tower(nc, *args)
    r = _run(nc, [arrays], core_ids=[0])
    return r.results[0]["out_0_dram"]
```

```python
from contextlib import ExitStack

import concourse.bass as bass
from concourse import mybir

F32 = mybir.dt.float32
F16 = mybir.dt.float16
BF16 = mybir.dt.bfloat16
U32 = mybir.dt.uint32
I32 = mybir.dt.int32
ALU = mybir.AluOpType
ACT = mybir.ActivationFunctionType
AX = mybir.AxisListType

P = 128
C = 128
NTOK = 64 * 256
NT = NTOK // P
TG = 4
NG = NT // TG
EPS = 1e-5
H0, D0 = 8, 16
E0 = 32
CAP = NTOK // E0
FF = 341
FCH = (128, 128, FF - 256)
ROW = C + E0
H1 = 8
E1, F1 = 8, 256
BIG = 1e30
UT = 2 * P
XR = 8
YR = 4
NUN = XR * ((NTOK * 2 // UT + E1 - 1 + XR - 1) // XR)
REG = NTOK + UT
XW = C + 2
NOWHERE = 1 << 20


def first(i):
    return isinstance(i, int) and i == 0


class Steps:

    def __init__(self, eng, sem, base=0):
        self.eng, self.sem, self.base, self.n = eng, sem, base, 0

    def done(self, ins):
        ins.then_inc(self.sem, 1)
        self.n += 1

    def wait(self):
        self.eng.wait_ge(self.sem, self.base + self.n)


def lm_tower(nc, x, L0_tok_weight, L0_attn_Wqkv, L0_attn_temperature, L0_attn_Wproj, L0_attn_bproj,
             L0_ffn_W_router, L0_ffn_b_router, L0_ffn_W_up, L0_ffn_b_up, L0_ffn_W_down, L0_ffn_b_down,
             L1_attn_Wq, L1_attn_Wk, L1_attn_Wv, L1_attn_Wo, L1_attn_bo,
             L1_ffn_gate_w, L1_ffn_gate_b, L1_ffn_w1, L1_ffn_b1, L1_ffn_w2, L1_ffn_b2, out):
    with ExitStack() as ctx:
        def sb(name, shape, dt=F32):
            return ctx.enter_context(nc.sbuf_tensor(name, shape, dt))

        def sem(name):
            return ctx.enter_context(nc.semaphore(name))

        bank = [ctx.enter_context(nc.psum_tensor(f"bank{n}", [P, 512], F32)) for n in range(8)]

        hbuf = nc.dram_tensor("hbuf", (NTOK, C), F32).ap()
        xrow = nc.dram_tensor("xrow", (NTOK, ROW), F32).ap()
        h3buf = nc.dram_tensor("h3buf", (NTOK, C), F32).ap()
        hbuf_b = hbuf.rearrange("(n j p) c -> n p j c", j=2, p=P)
        h3buf_g = h3buf.rearrange("(g j p) c -> g p j c", j=TG, p=P)
        out_g = out.rearrange("b (j p) c -> (b j) p c", p=P).rearrange("(g j) p c -> g p j c", j=TG)
        spread_rows = nc.dram_tensor("spread_rows", (E1 * REG + 8 * UT, XW), F32).ap()
        zbuf = nc.dram_tensor("zbuf", (2 * NTOK, C), F32).ap()
        zbuf_g = zbuf.rearrange("(g j p k) c -> g p j (k c)", j=TG, p=P, k=2)
        h3buf_b = h3buf.rearrange("(n j p) c -> n p j c", j=2, p=P)
        hbuf_g = hbuf.rearrange("(g j p) c -> g p j c", j=TG, p=P)
        xrow_g = xrow.rearrange("(g j p) c -> g p j c", j=TG, p=P)

        ident = sb("ident", [P, P])
        ones = sb("ones", [P, P])
        head = sb("head", [H0, P])
        headt = sb("headt", [H0, P])
        headc = sb("headc", [P, H0])
        mtemp = sb("mtemp", [P, P])
        temp = sb("temp", [H0, 1])
        junkf = sb("junkf", [P, CAP], I32)
        slotf = sb("slotf", [P, TG], I32)
        tilef = sb("tilef", [P, 1], I32)
        whichi = sb("whichi", [P, E1], I32)
        wqkv_n = sb("wqkv_n", [P, 3, C])
        wproj_n = sb("wproj_n", [P, C])
        wqkvT = sb("wqkvT", [P, 3 * C])
        wprojT = sb("wprojT", [P, C])
        bproj = sb("bproj", [P, C])
        wrout = sb("wrout", [P, E0])
        brout = sb("brout", [P, E0])
        idrow = sb("idrow", [P, P], I32)
        idrowf = sb("idrowf", [P, P])
        ids = sb("ids", [P, NT], U32)
        vo_place = sb("vo_place", [P, 4, 2 * TG * C])
        pr_place = sb("pr_place", [P, 3, 2 * TG * C])

        def group_view(place, k):
            return place[:, k].rearrange("p (q j c) -> p q j c", q=2, j=TG)
        idst = sb("idst", [P, 2, TG], U32)
        xg = group_view(vo_place, 0)
        xb = group_view(vo_place, 1)
        st = sb("st", [P, 2, TG, 6])
        mv = sb("mv", [P, 2, TG, 2])
        lnv = sb("lnv", [P, 2, TG])
        rs = sb("rs", [P, 2, TG])
        rt = sb("rt", [P, 2, TG])
        xn = group_view(vo_place, 2)
        xT = vo_place[:, 3].rearrange("p (q t) -> p q t", q=2)
        kk = group_view(pr_place, 0)
        vv = sb("vv", [P, 2, TG, C + 1])
        qT = sb("qT", [P, 2, TG * P])
        md = sb("md", [P, 2, 2, C + H0])
        den = sb("den", [P, 2, TG, H0])
        oo = group_view(pr_place, 1)
        oT = pr_place[:, 2].rearrange("p (q t) -> p q t", q=2)
        h1 = sb("h1", [P, 2, TG, C])
        xr = sb("xr", [P, 2, TG, ROW])
        x2T = sb("x2T", [P, 2, TG * P])
        lg = sb("lg", [P, 2, TG, E0])
        mx = sb("mx", [P, 2, TG])
        sm = sb("sm", [P, 2, TG])
        pg = sb("pg", [P, 2, TG, E0])
        pa = sb("pa", [P, NT, E0])
        kb = sb("kb", [P, NG * P])

        lanes = sb("lanes", [P, P])
        before = sb("before", [P, P])
        slot16 = sb("slot16", [P, CAP], F16)
        slotc = sb("slotc", [P, TG])
        junk = sb("junk", [P, NG * P], BF16)
        thr = sb("thr", [P, 1], U32)
        cand = sb("cand", [P, 1], U32)
        bit = sb("bit", [P, 1], U32)
        keep = sb("keep", [P, 1], U32)
        cnt = sb("cnt", [P, 1])
        quota = sb("quota", [P, 1])
        diag = sb("diag", [E0, 2, E0])
        tq = sb("tq", [P, 2, E0])
        pc = sb("pc", [P, E0, P])
        sel = sb("sel", [P, 2, P])
        cum = sb("cum", [P, 2, P])
        base = sb("base", [P, 2])
        edge = sb("edge", [P, 2])
        tab = sb("tab", [P, P + 1], F16)
        from0 = sb("from0", [P, CAP], F16)
        oneh = sb("oneh", [P, CAP], F16)
        tbase = sb("tbase", [P, TG])
        cnt4 = sb("cnt4", [P, TG])
        idx = sb("idx", [P, 4, TG], U32)
        xe = sb("xe", [P, 2, TG, ROW])
        xeT = sb("xeT", [P, TG * P])
        wup = sb("wup", [P, 2, FF])
        bup_n = sb("bup_n", [8, FF])
        bupT = sb("bupT", [P, 3, 8])
        bupg = sb("bupg", [P, 3])
        wdn = sb("wdn", [P, 2, 3, C])
        ac = sb("ac", [P, 3, TG * P])
        gate = sb("gate", [P, 2, TG])
        ye = sb("ye", [P, 2, TG, C])

        identb = sb("identb", [P, P], BF16)
        causal = sb("causal", [P, P], BF16)
        wqn = sb("wqn", [P, H1 * C])
        wkn = sb("wkn", [P, H1 * C])
        wvn = sb("wvn", [P, H1 * C])
        won = sb("won", [P, H1, C])
        wT = sb("wT", [P, 3, C])
        wqk = sb("wqk", [P, H1, C])
        wvo = sb("wvo", [P, H1, C])
        bo = sb("bo", [P, C])
        hx = sb("hx", [P, 2, 2, C])
        hb = sb("hb", [P, 2, 2, C])
        h3 = sb("h3", [P, 2, 2, C])
        st3 = sb("st3", [P, 2, 6])
        mv3 = sb("mv3", [P, 2, 2])
        r3 = sb("r3", [P, 3, 2])
        xn3 = sb("xn3", [P, 2, C])
        xT3 = sb("xT3", [P, 2, 2 * P])
        gT = sb("gT", [P, 2, 4 * P])
        vo = vo_place[:].rearrange("p (q j) n -> p q j n", q=2)
        nmax = sb("nmax", [P, 4, 2])
        rsum = sb("rsum", [P, 4, 2])
        rinv = sb("rinv", [P, 4, 2])
        pr_flat = pr_place[:].rearrange("p k n -> p (k n)")
        pr = pr_flat[:, 0:12 * P].rearrange("p (k n) -> p k n", k=4)
        prT = pr_flat[:, 12 * P:18 * P].rearrange("p (k n) -> p k n", k=2)

        w1s = pa[:, 0:64].rearrange("p j e -> p (j e)").rearrange("p (x f) -> p x f", x=E1)
        w2s = pa[:, 64:128].rearrange("p j e -> p (j e)").rearrange("p (x k m) -> p x (k m)", x=E1, k=2)
        gw = sb("gw", [P, E1])
        gb = sb("gb", [P, E1])
        b1n = sb("b1n", [E1, F1])
        b1T = sb("b1T", [P, 2, E1])
        which = sb("which", [P, E1])
        beforeb = sb("beforeb", [P, P], BF16)
        onesb = sb("onesb", [P, P], BF16)
        xr4 = kb[:, 0:8 * XW].rearrange("p (k j c) -> p k j c", k=2, j=TG)
        xT4 = kb[:, 1040:1552]
        st4 = sb("st4", [P, TG, 6])
        mv4 = sb("mv4", [P, TG, 2])
        r4 = sb("r4", [P, 3, TG])
        lg4 = sb("lg4", [P, TG, E1])
        top = sb("top", [P, TG, 8])
        topi = sb("topi", [P, TG, 8], U32)
        topf = sb("topf", [P, TG, 2])
        gap = sb("gap", [P, TG])
        tw = sb("tw", [P, 2, TG])
        hit = sb("hit", [P, 2, TG, E1])
        mask = sb("mask", [P, TG, E1], BF16)
        row0 = sb("row0", [P, E1], I32)
        desti = sb("desti", [P, 2, TG], I32)
        dest = sb("dest", [P, 2, TG])
        nextrow = sb("nextrow", [P, E1])
        rk = sb("rk", [P, TG, E1])
        posm = sb("posm", [P, 2, TG, E1])
        posf = sb("posf", [P, 2, TG])
        pos = sb("pos", [P, 2, TG], U32)
        padrow = sb("padrow", [P, XW])
        padci = sb("padci", [P, 2], I32)
        padc = sb("padc", [P, 2])
        padi = sb("padi", [P, 2, E1], U32)
        ui = sb("ui", [1, NUN], I32)
        uf = sb("uf", [1, NUN])
        row0f = sb("row0f", [P, E1])
        nun = sb("nun", [1, E1])
        nuni = sb("nuni", [1, E1], U32)
        cun = sb("cun", [1, E1])
        past = sb("past", [1, NUN, E1])
        ux = sb("ux", [1, NUN])
        ur = sb("ur", [1, NUN])
        unit_x = sb("unit_x", [1, NUN], U32)
        unit_r = sb("unit_r", [1, NUN], U32)
        xTu = kb[:, 2592:3104].rearrange("p (u t) -> p u t", u=2)
        pcf = pc[:].rearrange("p e t -> p (e t)")
        hTu = pcf[:, 0:1024].rearrange("p (u k t) -> p u k t", u=2, k=2)
        tu = pcf[:, 1024:1536].rearrange("p (u j c) -> p u j c", u=2, j=2)
        w1u = pcf[:, 2048:2560].rearrange("p (u f) -> p u f", u=2)
        w2u = pcf[:, 2560:3072].rearrange("p (u f) -> p u f", u=2)
        b2s = pcf[:, 3072:4096].rearrange("p (x c) -> p x c", x=E1)
        vof = vo_place[:].rearrange("p k n -> p (k n)")
        xu = vof[:, 0:2 * XR * XW].rearrange("p (u j c) -> p u j c", u=XR, j=2)
        yu = vof[:, 2 * XR * XW:2 * XR * XW + 2 * YR * C].rearrange("p (u j c) -> p u j c", u=YR, j=2)
        zx = vof[:, 0:2048].rearrange("p (q j c) -> p q j c", q=2, j=TG)
        h3x = vof[:, 2048:3072].rearrange("p (q j c) -> p q j c", q=2, j=TG)
        res = vof[:, 3072:4096].rearrange("p (q j c) -> p q j c", q=2, j=TG)

        w_in = sem("w_in")
        consts = sem("consts")
        prep_t = sem("prep_t")
        prep_c = sem("prep_c")
        ids_ready = sem("ids_ready")
        idst_ready = sem("idst_ready")
        gathered = [sem(f"gathered{p}") for p in range(2)]
        xb_ready = sem("xb_ready")
        xn_ready = sem("xn_ready")
        xT_mm = sem("xT_mm")
        xT_ready = sem("xT_ready")
        kv_mm = sem("kv_mm")
        kv_ready = sem("kv_ready")
        q_mm = sem("q_mm")
        q_ready = sem("q_ready")
        kvs_mm = sem("kvs_mm")
        md_ready = sem("md_ready")
        o_mm = sem("o_mm")
        o_ready = sem("o_ready")
        oT_mm = sem("oT_mm")
        oT_ready = sem("oT_ready")
        y_mm = sem("y_mm")
        h1_ready = sem("h1_ready")
        x2_ready = sem("x2_ready")
        x2T_mm = sem("x2T_mm")
        x2T_ready = sem("x2T_ready")
        lg_mm = sem("lg_mm")
        lg_sub = sem("lg_sub")
        lg_exp = sem("lg_exp")
        p_ready = sem("p_ready")
        pa_ready = sem("pa_ready")
        pT_mm = sem("pT_mm")
        pT_ready = sem("pT_ready")
        stored = [sem(f"stored{p}") for p in range(2)]
        dve_step = sem("dve_step")

        consts2 = sem("consts2")
        lanes_s = sem("lanes_s")
        w_b = sem("w_b")
        pcT_mm = sem("pcT_mm")
        pc_ready = sem("pc_ready")
        bup_mm = sem("bup_mm")
        bup_ready = sem("bup_ready")
        cnt_ready = sem("cnt_ready")
        cnt_mm = sem("cnt_mm")
        find_step = sem("find_step")
        diag_ready = sem("diag_ready")
        tq_mm = sem("tq_mm")
        tq_ready = sem("tq_ready")
        cum_ready = sem("cum_ready")
        base_mm = sem("base_mm")
        sel_step = sem("sel_step")
        oneh_ready = sem("oneh_ready")
        tab_mm = sem("tab_mm")
        idx_ready = sem("idx_ready")
        xe_in = [sem(f"xe_in{p}") for p in range(2)]
        xeT_mm = sem("xeT_mm")
        xeT_ready = sem("xeT_ready")
        wup_in = [sem(f"wup_in{p}") for p in range(2)]
        wdn_in = [sem(f"wdn_in{p}") for p in range(2)]
        up_mm = sem("up_mm")
        ac_ready = sem("ac_ready")
        dn_mm = sem("dn_mm")
        ye_ready = sem("ye_ready")
        added = [sem(f"added{p}") for p in range(2)]

        consts3 = sem("consts3")
        w_c = sem("w_c")
        wT_mm = sem("wT_mm")
        wT_ready = sem("wT_ready")
        fold_mm = sem("fold_mm")
        fold_ready = sem("fold_ready")
        h2_in = [sem(f"h2_in{p}") for p in range(2)]
        hb_ready = sem("hb_ready")
        prep_step = sem("prep_step")
        xn3_ready = sem("xn3_ready")
        xT3_mm = sem("xT3_mm")
        xT3_ready = sem("xT3_ready")
        g_mm = sem("g_mm")
        g_ready = sem("g_ready")
        vo_mm = sem("vo_mm")
        vo_ready = sem("vo_ready")
        s_mm = sem("s_mm")
        max_ready = sem("max_ready")
        exp_ready = sem("exp_ready")
        rinv_ready = sem("rinv_ready")
        pr_ready = sem("pr_ready")
        prT_mm = sem("prT_mm")
        prT_ready = sem("prT_ready")
        head_mm = sem("head_mm")
        h3_ready = sem("h3_ready")
        h3_out = [sem(f"h3_out{p}") for p in range(2)]

        NB = NTOK // (2 * P)
        GBANK, VBANK, SBANK, TBANK, OBANK = 0, 2, (3, 4), (5, 6), (1, 7)
        S_LAG, N_LAG, T_LAG, O_LAG = 1, 2, 3, 4

        def there(u, count=NB * H1):
            return not isinstance(u, int) or 0 <= u < count

        consts4 = sem("consts4")
        w_d = sem("w_d")
        w_d2 = sem("w_d2")
        b1_mm = sem("b1_mm")
        b1_ready = sem("b1_ready")
        d_step = sem("d_step")
        xn4_ready = sem("xn4_ready")
        xT4_mm = sem("xT4_mm")
        xT4_ready = sem("xT4_ready")
        gate_mm = sem("gate_mm")
        lg4_ready = sem("lg4_ready")
        gap_ready = sem("gap_ready")
        gap_exp = sem("gap_exp")
        mask_ready = sem("mask_ready")
        rank_mm = sem("rank_mm")
        rank_read = sem("rank_read")
        twice = sem("twice")
        pos_ready = sem("pos_ready")
        spread = sem("spread")
        dummies = sem("dummies")
        pad_ready = sem("pad_ready")
        padded = sem("padded")
        table_step = sem("table_step")
        table_ready = sem("table_ready")
        xu_in = [sem(f"xu_in{q}") for q in range(XR)]
        xTu_mm = sem("xTu_mm")
        xTu_ready = sem("xTu_ready")
        w1u_ready = sem("w1u_ready")
        w2u_ready = sem("w2u_ready")
        upu_mm = sem("upu_mm")
        hTu_ready = sem("hTu_ready")
        dnu_mm = sem("dnu_mm")
        tu_ready = sem("tu_ready")
        yu_ready = sem("yu_ready")
        z_out = [sem(f"z_out{q}") for q in range(XR)]
        z_in = [sem(f"z_in{p}") for p in range(2)]
        res_step = sem("res_step")
        res_ready = sem("res_ready")
        out_done = [sem(f"out_done{p}") for p in range(2)]

        NU = E0 // 4
        block = ctx.enter_context(nc.Block())

        @block.sync
        def _(sp):
            sp.dma_start(idrow[:], x.rearrange("b (t p) -> (b t) p", p=P)).then_inc(w_in, 16)
            sp.dma_start(wqkv_n[:], L0_attn_Wqkv.rearrange("(k p) c -> p k c", p=P)).then_inc(w_in, 16)
            sp.dma_start(wproj_n[:], L0_attn_Wproj).then_inc(w_in, 16)
            sp.dma_start(bproj[:], L0_attn_bproj.partition_broadcast(P)).then_inc(w_in, 16)
            sp.dma_start(wrout[:], L0_ffn_W_router).then_inc(w_in, 16)
            sp.dma_start(brout[:], L0_ffn_b_router.partition_broadcast(P)).then_inc(w_in, 16)
            sp.dma_start(temp[:], L0_attn_temperature.rearrange("h a b -> h (a b)")).then_inc(w_in, 16)

            sp.dma_start(wqn[:], L1_attn_Wq).then_inc(w_c, 16)
            sp.dma_start(wkn[:], L1_attn_Wk).then_inc(w_c, 16)
            sp.dma_start(wvn[:], L1_attn_Wv).then_inc(w_c, 16)
            sp.dma_start(won[:], L1_attn_Wo.rearrange("(h e) m -> e h m", h=H1)).then_inc(w_c, 16)
            sp.dma_start(bo[:], L1_attn_bo.partition_broadcast(P)).then_inc(w_c, 16)

            sp.dma_start(gw[:], L1_ffn_gate_w).then_inc(w_d, 16)
            sp.dma_start(gb[:], L1_ffn_gate_b.partition_broadcast(P)).then_inc(w_d, 16)
            sp.dma_start(b1n[:], L1_ffn_b1).then_inc(w_d, 16)

            def store(i):
                for p in range(2):
                    g = 2 * i + p
                    sp.wait_ge(h1_ready, g + 1)
                    sp.dma_start(hbuf_g[bass.ds(g, 1)].rearrange("a p j c -> (a p) j c"), h1[:, p]).then_inc(stored[p], 16)
                for p in range(2):
                    g = 2 * i + p
                    sp.wait_ge(p_ready, g + 1)
                    sp.dma_start(xrow_g[bass.ds(g, 1)].rearrange("a p j c -> (a p) j c"), xr[:, p]).then_inc(stored[p], 16)
            with sp.Fori(0, NG // 2) as i:
                store(i)
            for p in range(2):
                sp.wait_ge(stored[p], 32 * (NG // 2))


            sp.dma_start(bup_n[:], L0_ffn_b_up).then_inc(w_b, 16)

            def load_up(u, p):
                sp.dma_start(wup[:, p], L0_ffn_W_up[bass.ds(u, 1)].rearrange("a h f -> (a h) f")).then_inc(wup_in[p], 16)

            def load_down(e, p):
                w = L0_ffn_W_down[bass.ds(e, 1)].rearrange("a f h -> (a f) h")
                sp.dma_start(wdn[:, p, 0:2], w[0:2 * P].rearrange("(k p) h -> p k h", p=P)).then_inc(wdn_in[p], 16)
                sp.dma_start(wdn[0:FCH[2], p, 2], w[2 * P:FF]).then_inc(wdn_in[p], 16)
                sp.dma_start(wdn[FCH[2]:FCH[2] + 1, p, 2], L0_ffn_b_down[bass.ds(e, 1)]).then_inc(wdn_in[p], 16)

            for e in range(2):
                load_up(0, e)
                load_down(e, e)

            def reload(v, last):
                for q in range(2 if last else 4):
                    e, p = 4 * v + q, q % 2
                    sp.wait_ge(dn_mm, e + 1)
                    load_up(v + q // 2, p)
                    load_down(e + 2, p)
            with sp.Fori(0, NU - 1) as v:
                reload(v, False)
            reload(NU - 1, True)

            def load_h2(n, p):
                sp.dma_start(hx[:, p], hbuf_b[bass.ds(n, 1)].rearrange("a p j c -> (a p) j c")).then_inc(h2_in[p], 16)

            for p in range(2):
                sp.wait_ge(added[p], 64 * (E0 // 2))
            for p in range(2):
                load_h2(p, p)

            sp.dma_start(w1s, L1_ffn_w1.rearrange("x h f -> h x f")).then_inc(w_d2, 16)
            sp.dma_start(w2s.rearrange("p x (k m) -> p x k m", k=2), L1_ffn_w2.rearrange("x (k p) m -> p x k m", p=P)).then_inc(w_d2, 16)
            sp.dma_start(b2s, L1_ffn_b2.partition_broadcast(P)).then_inc(w_d2, 16)
            sp.wait_ge(consts4, 15)
            sp.dma_start(spread_rows[E1 * REG:E1 * REG + 8 * UT].rearrange("(j p) c -> p j c", p=P),
                         padrow[:].unsqueeze(1).to_broadcast([P, 16, XW])).then_inc(dummies, 16)

            def pass_h(i, last):
                for p in range(2):
                    n = 2 * i + p
                    if not last:
                        sp.wait_ge(hb_ready, n + 1)
                        sp.wait_ge(xn3_ready, n + 1)
                        load_h2(n + 2, p)
                    sp.wait_ge(h3_ready, n + 1)
                    sp.dma_start(h3buf_b[bass.ds(n, 1)].rearrange("a p j c -> (a p) j c"), h3[:, p]).then_inc(h3_out[p], 16)
            with sp.Fori(0, NB // 2 - 1) as i:
                pass_h(i, False)
            pass_h(NB // 2 - 1, True)
            for p in range(2):
                sp.wait_ge(h3_out[p], 16 * (NB // 2))

            sp.wait_ge(spread, 128 * NG)
            sp.wait_ge(padded, 16 * 2 * E1)
            sp.wait_ge(dummies, 16)
            sp.wait_ge(table_ready, 1)

            def load_unit(u, q):
                r = sp.value_load(unit_r[0:1, bass.ds(u, 1)], min_val=0, max_val=E1 * REG + (XR - 1) * UT)
                sp.dma_start(xu[:, q], spread_rows[bass.ds(r, UT)].rearrange("(j p) c -> p j c", p=P)).then_inc(xu_in[q], 16)

            for q in range(XR):
                load_unit(q, q)

            def units(v):
                for q in range(XR):
                    sp.wait_ge(z_out[q], 32 * (v + 1))
                    load_unit(XR * v + q + XR, q)
            with sp.Fori(0, NUN // XR - 1) as v:
                units(v)
            for q in range(XR):
                sp.wait_ge(z_out[q], 32 * (NUN // XR))

            def load_z(g, p):
                sp.dma_start(zx[:, p], zbuf_g[bass.ds(g, 1)].rearrange("a p j c -> (a p) j c")).then_inc(z_in[p], 16)
                sp.dma_start(h3x[:, p], h3buf_g[bass.ds(g, 1)].rearrange("a p j c -> (a p) j c")).then_inc(z_in[p], 16)

            for p in range(2):
                load_z(p, p)

            def results(i, last):
                for p in range(2):
                    g = 2 * i + p
                    sp.wait_ge(res_ready, g + 1)
                    sp.dma_start(out_g[bass.ds(g, 1)].rearrange("a p j c -> (a p) j c"), res[:, p]).then_inc(out_done[p], 16)
                    if not last:
                        load_z(g + 2, p)
            with sp.Fori(0, NG // 2 - 1) as i:
                results(i, False)
            results(NG // 2 - 1, True)
            for p in range(2):
                sp.wait_ge(out_done[p], 16 * (NG // 2))

        @block.gpsimd
        def _(pool):
            pool.memset(ident[:], 0.0).then_inc(consts, 1)
            pool.memset(ones[:], 1.0).then_inc(consts, 1)
            pool.memset(head[:], 1.0).then_inc(consts, 1)
            pool.memset(vv[:, :, :, C:C + 1], 1.0).then_inc(consts, 1)
            pool.wait_ge(consts, 4)
            pool.affine_select(out=ident[:], in_=ident[:], compare_op=ALU.not_equal, fill=1.0, base=0,
                               pattern=[[-1, P]], channel_multiplier=1).then_inc(consts, 1)
            pool.affine_select(out=head[:], in_=head[:], compare_op=ALU.is_ge, fill=0.0, base=0,
                               pattern=[[1, P]], channel_multiplier=-D0).then_inc(consts, 1)
            pool.wait_ge(consts, 6)
            pool.affine_select(out=head[:], in_=head[:], compare_op=ALU.is_ge, fill=0.0, base=D0 - 1,
                               pattern=[[-1, P]], channel_multiplier=D0).then_inc(consts, 1)
            pool.memset(lanes[:], 0.0).then_inc(consts2, 1)
            pool.memset(before[:], 1.0).then_inc(consts2, 1)
            pool.memset(ac[:], 1.0).then_inc(consts2, 1)
            pool.iota(junkf[:], pattern=[[1, CAP]], base=0, channel_multiplier=0).then_inc(consts2, 1)
            pool.iota(slotf[:], pattern=[[P, TG]], base=0, channel_multiplier=1).then_inc(consts2, 1)
            pool.iota(tilef[:], pattern=[[0, 1]], base=0, channel_multiplier=P).then_inc(consts2, 1)
            pool.wait_ge(consts2, 6)
            pool.affine_select(out=before[:], in_=before[:], compare_op=ALU.is_gt, fill=0.0, base=0,
                               pattern=[[1, P]], channel_multiplier=-1).then_inc(consts2, 1)
            pool.tensor_copy(slot16[:], junkf[:]).then_inc(consts2, 1)
            pool.tensor_copy(slotc[:], slotf[:]).then_inc(consts2, 1)
            pool.tensor_copy(tab[:, P:P + 1], tilef[:]).then_inc(consts2, 1)
            for k in range(4):
                v = lanes[:].rearrange("p (b m) -> p b m", b=4)
                pool.affine_select(out=v, in_=v, compare_op=ALU.not_equal, fill=1.0, base=-E0 * k,
                                   pattern=[[0, 4], [-1, E0]], channel_multiplier=1).then_inc(lanes_s, 1)
                pool.wait_ge(lanes_s, k + 1)
            pool.iota(whichi[:], pattern=[[1, E1]], base=0, channel_multiplier=0).then_inc(consts4, 1)
            pool.iota(row0[:], pattern=[[REG, E1]], base=0, channel_multiplier=0).then_inc(consts4, 1)
            pool.iota(desti[:], pattern=[[1, 2], [2 * P, TG]], base=0, channel_multiplier=2).then_inc(consts4, 1)
            pool.iota(padci[:], pattern=[[P, 2]], base=0, channel_multiplier=1).then_inc(consts4, 1)
            pool.iota(ui[:], pattern=[[1, NUN]], base=0, channel_multiplier=0).then_inc(consts4, 1)
            pool.memset(padrow[:, 0:C + 1], 0.0).then_inc(consts4, 1)
            pool.memset(padrow[:, C + 1:XW].bitcast(U32), NOWHERE).then_inc(consts4, 1)
            pool.wait_ge(consts4, 7)
            pool.tensor_copy(which[:], whichi[:]).then_inc(consts4, 1)
            pool.tensor_copy(nextrow[:], row0[:]).then_inc(consts4, 1)
            pool.tensor_copy(row0f[:], row0[:]).then_inc(consts4, 1)
            pool.tensor_copy(dest[:], desti[:]).then_inc(consts4, 1)
            pool.tensor_copy(padc[:], padci[:]).then_inc(consts4, 1)
            pool.tensor_copy(uf[:], ui[:]).then_inc(consts4, 1)
            pool.tensor_copy(onesb[:], ones[:]).then_inc(consts4, 1)
            pool.tensor_copy(beforeb[:], before[:]).then_inc(consts4, 1)
            pool.memset(causal[:], 0.0).then_inc(consts3, 1)
            pool.tensor_copy(identb[:], ident[:]).then_inc(consts3, 1)
            pool.wait_ge(consts3, 2)
            pool.affine_select(out=causal[:], in_=causal[:], compare_op=ALU.is_ge, fill=-BIG, base=0,
                               pattern=[[-1, P]], channel_multiplier=1).then_inc(consts3, 1)
            pool.wait_ge(ids_ready, 1)

            def gather(g, p):
                pool.tensor_copy(idst[:, p], ids[:, bass.ds(TG * g, TG)]).then_inc(idst_ready, 1)
                pool.wait_ge(idst_ready, g + 1)
                pool.nop(nofuse=True)
                for j in range(TG):
                    pool.indirect_dma_start(out=xg[:, p, j], out_offset=None, in_=L0_tok_weight,
                                            in_offset=bass.IndirectOffsetOnAxis(ap=idst[:, p, j:j + 1], axis=0))\
                        .then_inc(gathered[p], 16)

            def pair(i, more):
                for p in range(2):
                    g = 2 * i + p
                    pool.wait_ge(gathered[p], 64 * (i + 1))
                    if not first(i):
                        pool.wait_ge(h1_ready, g - 1)
                    pool.tensor_tensor(xb[:, p], xg[:, p], bproj[:].unsqueeze(1).to_broadcast([P, TG, C]), ALU.add)\
                        .then_inc(xb_ready, 1)
                if more:
                    for p in range(2):
                        g = 2 * i + p
                        pool.wait_ge(xn_ready, g + 1)
                        pool.wait_ge(xb_ready, g + 1)
                        gather(g + 2, p)
                for p in range(2):
                    g = 2 * i + p
                    pool.wait_ge(p_ready, g + 1)
                    pool.nop(nofuse=True)
                    pool.tensor_copy(pa[:, bass.ds(g * TG, TG)], pg[:, p]).then_inc(pa_ready, 1)

            for p in range(2):
                gather(p, p)
            pair(0, True)
            with pool.Fori(1, NG // 2 - 1) as i:
                pair(i, True)
            pair(NG // 2 - 1, False)

            def take(e, q):
                p = q % 2
                pool.wait_ge(idx_ready, e + 1)
                pool.nop(nofuse=True)
                for c in range(TG):
                    pool.indirect_dma_start(out=xe[:, p, c], out_offset=None, in_=xrow,
                                            in_offset=bass.IndirectOffsetOnAxis(ap=idx[:, q, c:c + 1], axis=0))\
                        .then_inc(xe_in[p], 16)

            def give(e, p, q):
                pool.wait_ge(ye_ready, e + 1)
                pool.nop(nofuse=True)
                for c in range(TG):
                    pool.indirect_dma_start(out=hbuf, out_offset=bass.IndirectOffsetOnAxis(ap=idx[:, q, c:c + 1], axis=0),
                                            in_=ye[:, p, c], in_offset=None, compute_op=ALU.add).then_inc(added[p], 16)

            for p in range(2):
                pool.wait_ge(stored[p], 32 * (NG // 2))
            take(0, 0)
            take(1, 1)

            def serve(v, last):
                for q in range(4):
                    e, p = 4 * v + q, q % 2
                    if not (last and q >= 2):
                        take(e + 2, (q + 2) % 4)
                    if not (first(v) and q == 0):
                        n = 2 * v + (q + 1) // 2 if q % 2 else 2 * v + q // 2
                        pool.wait_ge(added[1 - p], 64 * n)
                    give(e, p, q)
            serve(0, False)
            with pool.Fori(1, NU - 1) as v:
                serve(v, False)
            serve(NU - 1, True)
            for p in range(2):
                pool.wait_ge(added[p], 64 * (E0 // 2))

            pool.wait_ge(w_c, 16 * 5)

            def scatter(g):
                pool.wait_ge(xn4_ready, g + 1)
                pool.nop(nofuse=True)
                pool.tensor_copy(xr4[:, 1, :, 0:C], xr4[:, 0, :, 0:C]).then_inc(twice, 1)
                pool.wait_ge(twice, g + 1)
                pool.wait_ge(pos_ready, g + 1)
                pool.nop(nofuse=True)
                for k in range(2):
                    for j in range(TG):
                        pool.indirect_dma_start(out=spread_rows, out_offset=bass.IndirectOffsetOnAxis(ap=pos[:, k, j:j + 1], axis=0),
                                                in_=xr4[:, k, j], in_offset=None).then_inc(spread, 16)

            def residual(i):
                for p in range(2):
                    n = 2 * i + p
                    pool.wait_ge(h2_in[p], 16 * (i + 1))
                    if not first(i):
                        pool.wait_ge(h3_ready, n - 1)
                    pool.tensor_tensor(hb[:, p], hx[:, p], bo[:].unsqueeze(1).to_broadcast([P, 2, C]), ALU.add)\
                        .then_inc(hb_ready, 1)
                if not first(i):
                    scatter(i - 1)
            residual(0)
            with pool.Fori(1, NB // 2) as i:
                residual(i)
            scatter(NG - 1)

            pool.wait_ge(pad_ready, 1)
            for k in range(2):
                for x in range(E1):
                    pool.indirect_dma_start(out=spread_rows, out_offset=bass.IndirectOffsetOnAxis(ap=padi[:, k, x:x + 1], axis=0),
                                            in_=padrow[:], in_offset=None).then_inc(padded, 16)

            def give_unit(u, q, v):
                pool.wait_ge(yu_ready, u + 1)
                pool.nop(nofuse=True)
                for j in range(2):
                    pool.indirect_dma_start(out=zbuf, out_offset=bass.IndirectOffsetOnAxis(
                        ap=xu[:, q, j, C + 1:XW].bitcast(U32), axis=0), in_=yu[:, q % YR, j], in_offset=None,
                        bounds_check=2 * NTOK - 1, oob_is_err=False).then_inc(z_out[q], 16)
            with pool.Fori(0, NUN // XR) as v:
                for q in range(XR):
                    give_unit(XR * v + q, q, v)
            for q in range(XR):
                pool.wait_ge(z_out[q], 32 * (NUN // XR))

        @block.scalar
        def _(act):
            act.wait_ge(consts, 7)
            act.wait_ge(prep_t, 5)
            act.activation(ids[:], bank[0][:, 0:P], ACT.Copy).then_inc(ids_ready, 1)
            act.activation(wqkvT[:], bank[1][:, 0:3 * C], ACT.Copy).then_inc(prep_c, 1)
            act.activation(wprojT[:], bank[2][:, 0:C], ACT.Copy).then_inc(prep_c, 1)
            act.wait_ge(prep_t, 7)
            act.activation(headc[:], bank[3][:, 0:H0], ACT.Copy).then_inc(prep_c, 1)
            act.activation(mtemp[:], bank[4][:, 0:P], ACT.Copy).then_inc(prep_c, 1)

            def pair(i, more):
                for p in range(2):
                    g = 2 * i + p
                    act.wait_ge(xT_mm, g + 1)
                    act.activation(xT[:, p], bank[4 * p][:, :], ACT.Copy).then_inc(xT_ready, 1)
                for p in range(2):
                    g = 2 * i + p
                    for m in range(2):
                        b2 = bank[4 * p + 1 + m][:, :].rearrange("p (j n) -> p j n", j=2)
                        act.wait_ge(kv_mm, 2 * g + m + 1)
                        act.activation(kk[:, p, 2 * m:2 * m + 2], b2[:, :, 0:C], ACT.Relu).then_inc(kv_ready, 1)
                        act.activation(vv[:, p, 2 * m:2 * m + 2, 0:C], b2[:, :, C:2 * C], ACT.Copy).then_inc(kv_ready, 1)
                for p in range(2):
                    g = 2 * i + p
                    act.wait_ge(q_mm, g + 1)
                    act.activation(qT[:, p], bank[4 * p + 3][:, :], ACT.Relu).then_inc(q_ready, 1)
                for p in range(2):
                    g = 2 * i + p
                    act.wait_ge(oT_mm, g + 1)
                    act.activation(oT[:, p], bank[4 * p][:, :], ACT.Copy).then_inc(oT_ready, 1)
                for p in range(2):
                    g = 2 * i + p
                    act.wait_ge(x2T_mm, g + 1)
                    act.activation(x2T[:, p], bank[4 * p][:, :], ACT.Copy).then_inc(x2T_ready, 1)
                for p in range(2):
                    g = 2 * i + p
                    act.wait_ge(lg_sub, g + 1)
                    act.activation(lg[:, p], lg[:, p], ACT.Exp).then_inc(lg_exp, 1)
                for p in range(2):
                    g = 2 * i + p
                    act.wait_ge(pT_mm, g + 1)
                    act.activation(kb[:, bass.ds(g * P, P)], bank[4 * p + 3][:, 0:P], ACT.Copy).then_inc(pT_ready, 1)

            with act.Fori(0, NG // 2 - 1) as i:
                pair(i, True)
            pair(NG // 2 - 1, False)

            for k in range(0, 8, 2):
                act.wait_ge(pcT_mm, k + 1)
                act.activation(pc[:, 4 * k:4 * k + 4], bank[k][:, :].rearrange("p (e t) -> p e t", e=4), ACT.Copy).then_inc(pc_ready, 1)
            act.wait_ge(bup_mm, 1)
            act.activation(bupT[:, 0:2], bank[1][:, 0:16].rearrange("p (k u) -> p k u", k=2), ACT.Copy).then_inc(bup_ready, 1)
            act.activation(bupT[0:FCH[2], 2], bank[1][0:FCH[2], 16:24], ACT.Copy).then_inc(bup_ready, 1)

            for h in range(H1):
                act.wait_ge(wT_mm, h + 1)
                act.activation(wT[:], bank[2][:, 0:3 * C].rearrange("p (k c) -> p k c", k=3), ACT.Copy).then_inc(wT_ready, 1)
                act.wait_ge(fold_mm, h + 1)
                act.activation(wqk[:, h], bank[3][:, 0:C], ACT.Copy, scale=float(C) ** -0.5).then_inc(fold_ready, 1)
                act.activation(wvo[:, h], bank[3][:, C:2 * C], ACT.Copy).then_inc(fold_ready, 1)

            act.wait_ge(b1_mm, 1)
            act.activation(b1T[:], bank[2][:, 0:2 * E1].rearrange("p (k x) -> p k x", k=2), ACT.Copy).then_inc(b1_ready, 1)
            act.wait_ge(bup_ready, 2)
            act.wait_ge(consts2, 10)

            def rows_turned(e):
                act.wait_ge(xeT_mm, e + 1)
                act.activation(xeT[:], bank[0][:, :], ACT.Copy).then_inc(xeT_ready, 1)

            def hidden(v, last):
                if not first(v):
                    act.wait_ge(ac_ready, 12 * v)
                act.activation(bupg[:, 0:2], bupT[:, 0:2, bass.ds(v, 1)].rearrange("p k a -> p (k a)"), ACT.Copy).then_inc(bup_ready, 1)
                act.activation(bupg[0:FCH[2], 2:3], bupT[0:FCH[2], 2, bass.ds(v, 1)], ACT.Copy).then_inc(bup_ready, 1)
                act.wait_ge(bup_ready, 4 + 2 * v)
                for q in range(4):
                    e = 4 * v + q
                    for k in range(3):
                        act.wait_ge(up_mm, 3 * e + k + 1)
                        act.activation(ac[0:FCH[k], k], bank[1 + k][0:FCH[k], :], ACT.Silu, bias=bupg[0:FCH[k], k:k + 1])\
                            .then_inc(ac_ready, 1)
                    if not (last and q == 3):
                        rows_turned(e + 1)
            rows_turned(0)
            hidden(0, False)
            with act.Fori(1, NU - 1) as v:
                hidden(v, False)
            hidden(NU - 1, True)

            def turned(n, p):
                act.wait_ge(xT3_mm, n + 1)
                act.activation(xT3[:, p], bank[VBANK][:, 0:2 * P], ACT.Copy).then_inc(xT3_ready, 1)

            def exps(u, h):
                act.wait_ge(max_ready, u + 1)
                if not isinstance(u, int) or u >= 4:
                    act.wait_ge(prT_mm, u - 3)
                s2 = bank[SBANK[h % 2]]
                act.activation(pr[:, h % 4, 0:P], s2[:, 0:P], ACT.Exp, bias=nmax[:, h % 4, 0:1],
                               accum_out=rsum[:, h % 4, 0:1])
                act.activation(pr[:, h % 4, P:3 * P], s2[:, P:3 * P], ACT.Exp, bias=nmax[:, h % 4, 1:2],
                               accum_out=rsum[:, h % 4, 1:2]).then_inc(exp_ready, 1)

            turned(0, 0)

            def gates_turned(g):
                act.wait_ge(xT4_mm, g + 1)
                act.activation(xT4, bank[GBANK][:, :], ACT.Copy).then_inc(xT4_ready, 1)

            def gaps(g):
                act.wait_ge(gap_ready, g + 1)
                act.activation(tw[:, 1], gap[:], ACT.Exp).then_inc(gap_exp, 1)

            def heads(i, last):
                for p in range(2):
                    n = 2 * i + p
                    for h in range(H1):
                        u = H1 * n + h
                        if (p, h) == (1, 1) and there(i - 1):
                            gates_turned(i - 1)
                        if h % 2 == 0:
                            act.wait_ge(g_mm, 4 * n + h // 2 + 1)
                            act.activation(gT[:, h // 2 % 2], bank[GBANK][:, :], ACT.Copy).then_inc(g_ready, 1)
                        if h < 4:
                            act.wait_ge(vo_mm, 4 * n + h + 1)
                            act.activation(vo[:, p, h % 2, (h // 2) * 512:(h // 2 + 1) * 512], bank[VBANK][:, :], ACT.Copy)\
                                .then_inc(vo_ready, 1)
                        if h == 6 and not (last and p == 1):
                            turned(n + 1, 1 - p)
                        if there(u - S_LAG):
                            exps(u - S_LAG, (h - S_LAG) % H1)
                        if (p, h) == (1, 5) and there(i - 1):
                            gaps(i - 1)
            heads(0, False)
            with act.Fori(1, NB // 2 - 1) as i:
                heads(i, False)
            heads(NB // 2 - 1, True)
            exps(NB * H1 - 1, H1 - 1)
            gates_turned(NG - 1)
            gaps(NG - 1)

            act.wait_ge(table_ready, 1)

            def act_turn(u, q):
                act.wait_ge(xTu_mm, u + 1)
                act.activation(xTu[:, q % 2], bank[q % 2][:, 0:UT], ACT.Copy).then_inc(xTu_ready, 1)

            def units(v, last):
                for q in range(XR):
                    u = XR * v + q
                    if not (last and q == XR - 1):
                        act_turn(u + 1, q + 1)
                    x = act.value_load(unit_x[0:1, bass.ds(u, 1)], min_val=0, max_val=E1 - 1)
                    act.wait_ge(upu_mm, u + 1)
                    if not isinstance(u, int) or u >= 2:
                        act.wait_ge(dnu_mm, u - 1)
                    for k in range(2):
                        ins = act.activation(hTu[:, q % 2, k], bank[2 + q % 2][:, k * UT:(k + 1) * UT], ACT.Relu,
                                             bias=b1T[:, k, bass.ds(x, 1)])
                    ins.then_inc(hTu_ready, 1)
            act_turn(0, 0)
            units(0, False)
            with act.Fori(1, NUN // XR - 1) as v:
                units(v, False)
            units(NUN // XR - 1, True)

        @block.vector
        def _(dve):
            dve.wait_ge(w_in, 16 * 7)
            dve.tensor_copy(idrowf[:], idrow[:]).then_inc(prep_c, 1)
            dve.wait_ge(consts, 7)
            dve.tensor_scalar(headt[:], head[:], temp[:, 0:1], None, ALU.mult).then_inc(prep_c, 1)

            def stats(src, p, steps):
                for j in range(TG):
                    steps.done(dve.bn_stats(st[:, p, j], src[:, p, j]))
                steps.wait()
                dve.nop(nofuse=True)
                for j in range(TG):
                    ins = dve.bn_aggr(mv[:, p, j], st[:, p, j])
                steps.done(ins)

            ROOT = 13

            def inv_sqrt(k, steps, v, y, t, h):
                if k != 3:
                    steps.wait()
                if k == 0:
                    ins = dve.tensor_scalar(h, v, EPS, None, ALU.add)
                elif k == 1:
                    ins = dve.tensor_scalar(t.bitcast(U32), h.bitcast(U32), 1, None, ALU.logical_shift_right)
                elif k == 2:
                    ins = dve.tensor_scalar(y.bitcast(I32), t.bitcast(I32), -1.0, float(0x5F3759DF), ALU.mult, ALU.add)
                elif k == 3:
                    ins = dve.tensor_scalar(h, h, -0.5, None, ALU.mult)
                elif k % 3 == 1:
                    ins = dve.tensor_tensor(t, y, y, ALU.mult)
                elif k % 3 == 2:
                    ins = dve.tensor_tensor(t, t, h, ALU.mult)
                else:
                    ins = dve.scalar_tensor_tensor(out=y, in0=t, scalar=1.5, in1=y, op0=ALU.add, op1=ALU.mult)
                steps.done(ins)

            def normalise(dst, src, p, out_sem):
                for j in range(TG):
                    ins = dve.tensor_scalar(dst[:, p, j, 0:C], src[:, p, j], mv[:, p, j, 0:1], rs[:, p, j:j + 1],
                                            ALU.subtract, ALU.mult)
                ins.then_inc(out_sem, 1)

            PER_LN = 2 * TG + 2 + 13
            REST = 2 * (2 + 2 + 2) + PER_LN

            def ln_first(i, steps):
                for p in range(2):
                    g = 2 * i + p
                    dve.wait_ge(gathered[p], 64 * (i + 1))
                    stats(xg, p, steps)
                steps.wait()
                for k in range(ROOT):
                    inv_sqrt(k, steps, mv[:, :, :, 1], rs[:], rt[:], lnv[:])
                steps.wait()
                for p in range(2):
                    g = 2 * i + p
                    if not first(i):
                        dve.wait_ge(xT_mm, g - 1)
                    normalise(xn, xg, p, xn_ready)

            steps = Steps(dve, dve_step)
            ln_first(0, steps)
            assert steps.n == PER_LN, steps.n

            def pair(i, more):
                steps = Steps(dve, dve_step, PER_LN + (REST + PER_LN) * i)
                for p in range(2):
                    g = 2 * i + p
                    s4 = bank[4 * p][:, 0:2 * (C + 1)].rearrange("p (b n) -> p b n", b=2)
                    dve.wait_ge(kvs_mm, g + 1)
                    dve.tensor_tensor(md[:, p, :, 0:C], s4[:, :, 0:C], mtemp[:].unsqueeze(1).to_broadcast([P, 2, C]), ALU.mult)
                    dve.tensor_tensor(md[:, p, :, C:C + H0], headc[:].unsqueeze(1).to_broadcast([P, 2, H0]),
                                      s4[:, :, C:C + 1].to_broadcast([P, 2, H0]), ALU.mult).then_inc(md_ready, 1)
                for p in range(2):
                    g = 2 * i + p
                    for m in range(2):
                        o5 = bank[4 * p + 1 + m][:, 0:2 * (C + H0)].rearrange("p (j n) -> p j n", j=2)
                        dve.wait_ge(o_mm, 2 * g + m + 1)
                        last = dve.tensor_scalar(den[:, p, 2 * m:2 * m + 2], o5[:, :, C:C + H0], 100.0, None, ALU.max)
                    steps.done(last)
                    steps.wait()
                    steps.done(dve.reciprocal(den[:, p], den[:, p]))
                    steps.wait()
                    for m in range(2):
                        for j in range(2):
                            o5 = bank[4 * p + 1 + m][:, j * (C + H0):j * (C + H0) + C].rearrange("p (h d) -> p h d", h=H0)
                            last = dve.tensor_tensor(oo[:, p, 2 * m + j].rearrange("p (h d) -> p h d", h=H0), o5,
                                                     den[:, p, 2 * m + j].unsqueeze(2).to_broadcast([P, H0, D0]), ALU.mult)
                    last.then_inc(o_ready, 1)
                for p in range(2):
                    g = 2 * i + p
                    dve.wait_ge(y_mm, g + 1)
                    dve.wait_ge(xb_ready, g + 1)
                    if not first(i):
                        dve.wait_ge(stored[p], 32 * i)
                    dve.tensor_tensor(h1[:, p], bank[4 * p + 1][:, :].rearrange("p (j c) -> p j c", j=TG), xb[:, p], ALU.add)\
                        .then_inc(h1_ready, 1)
                    dve.wait_ge(h1_ready, g + 1)
                    stats(h1, p, steps)
                steps.wait()
                for k in range(ROOT):
                    inv_sqrt(k, steps, mv[:, :, :, 1], rs[:], rt[:], lnv[:])
                steps.wait()
                for p in range(2):
                    normalise(xr, h1, p, x2_ready)
                if more:
                    ln_first(i + 1, steps)
                for p in range(2):
                    g = 2 * i + p
                    dve.wait_ge(lg_mm, g + 1)
                    steps.done(dve.tensor_tensor(lg[:, p], bank[4 * p + 2][:, 0:TG * E0].rearrange("p (j e) -> p j e", j=TG),
                                                 brout[:].unsqueeze(1).to_broadcast([P, TG, E0]), ALU.add))
                    steps.wait()
                    steps.done(dve.tensor_reduce(mx[:, p], lg[:, p], AX.X, ALU.max))
                    steps.wait()
                    dve.tensor_tensor(lg[:, p], lg[:, p], mx[:, p].unsqueeze(2).to_broadcast([P, TG, E0]), ALU.subtract)\
                        .then_inc(lg_sub, 1)
                for p in range(2):
                    g = 2 * i + p
                    dve.wait_ge(lg_exp, g + 1)
                    steps.done(dve.tensor_reduce(sm[:, p], lg[:, p], AX.X, ALU.add))
                    steps.wait()
                    steps.done(dve.reciprocal(sm[:, p], sm[:, p]))
                    steps.wait()
                    if not first(i):
                        dve.wait_ge(pa_ready, g - 1)
                        dve.wait_ge(pT_mm, g - 1)
                    dve.tensor_tensor(pg[:, p], lg[:, p], sm[:, p].unsqueeze(2).to_broadcast([P, TG, E0]), ALU.mult)
                    dve.tensor_tensor(xr[:, p, :, C:ROW], lg[:, p], sm[:, p].unsqueeze(2).to_broadcast([P, TG, E0]), ALU.mult)\
                        .then_inc(p_ready, 1)
                return steps.n

            assert pair(0, True) == REST + PER_LN
            with dve.Fori(1, NG // 2 - 1) as i:
                pair(i, True)
            pair(NG // 2 - 1, False)

            for k in range(1, 8, 2):
                dve.wait_ge(pcT_mm, k + 1)
                dve.tensor_copy(pc[:, 4 * k:4 * k + 4], bank[k][:, :].rearrange("p (e t) -> p e t", e=4)).then_inc(pc_ready, 1)

            dve.wait_ge(pT_ready, NG)
            find = Steps(dve, find_step)
            find.done(dve.memset(thr[:], 0))
            find.done(dve.memset(bit[:], 1 << 29))
            find.done(dve.memset(cand[:], 1 << 29))
            find.wait()

            def settle(b):
                n = Steps(dve, find_step, 3 + 4 * b)
                dve.tensor_scalar(junk[:], kb[:], cand[:, 0:1].bitcast(F32), None, ALU.is_ge, ALU.add, accum_out=cnt[:, 0:1])\
                    .then_inc(cnt_ready, 1)
                dve.wait_ge(cnt_mm, b + 1)
                n.done(dve.tensor_scalar(keep[:].bitcast(I32), bank[0][:, 0:1], float(CAP), -1.0, ALU.is_ge, ALU.mult))
                n.wait()
                n.done(dve.scalar_tensor_tensor(out=thr[:], in0=keep[:], scalar=bit[:, 0:1], in1=thr[:],
                                                op0=ALU.bitwise_and, op1=ALU.bitwise_or))
                n.wait()
                n.done(dve.tensor_scalar(bit[:], bit[:], 1, None, ALU.logical_shift_right))
                n.wait()
                n.done(dve.tensor_tensor(cand[:], thr[:], bit[:], ALU.bitwise_or))
                n.wait()
            with dve.Fori(0, 30) as b:
                settle(b)
            dve.tensor_scalar(junk[:], kb[:], thr[:, 0:1].bitcast(F32), None, ALU.is_gt, ALU.add, accum_out=cnt[:, 0:1])\
                .then_inc(cnt_ready, 1)
            dve.wait_ge(cnt_mm, 31)
            find = Steps(dve, find_step, 3 + 4 * 30)
            find.done(dve.tensor_scalar(quota[:], bank[0][:, 0:1], -1.0, float(CAP), ALU.mult, ALU.add))
            find.wait()
            dve.tensor_scalar(diag[:, 0], ident[0:E0, 0:E0], thr[0:E0, 0:1].bitcast(F32), None, ALU.mult)
            dve.tensor_scalar(diag[:, 1], ident[0:E0, 0:E0], quota[0:E0, 0:1], None, ALU.mult).then_inc(diag_ready, 1)
            dve.wait_ge(tq_mm, 1)
            dve.tensor_copy(tq[:], bank[1][:, 0:2 * E0].rearrange("p (k e) -> p k e", k=2)).then_inc(tq_ready, 1)
            dve.wait_ge(tq_ready, 1)
            dve.wait_ge(pc_ready, 8)
            dve.wait_ge(consts2, 10)

            def rank(e, n):
                v = pc[:, bass.ds(e, 1)].rearrange("p a t -> p (a t)")
                n.done(dve.tensor_scalar(sel[:, 0], v, tq[:, 0, bass.ds(e, 1)], None, ALU.is_gt))
                n.done(dve.tensor_scalar(sel[:, 1], v, tq[:, 0, bass.ds(e, 1)], None, ALU.is_equal))
                n.wait()
                dve.tensor_tensor_scan(cum[:, 0], ones[:], sel[:, 0], 0.0, ALU.mult, ALU.add)
                dve.tensor_tensor_scan(cum[:, 1], ones[:], sel[:, 1], 0.0, ALU.mult, ALU.add).then_inc(cum_ready, 1)

            def place(e, n):
                dve.wait_ge(base_mm, e + 1)
                n.done(dve.tensor_copy(base[:], bank[7][:, 0:2]))
                n.wait()
                q = tq[:, 1, bass.ds(e, 1)]
                n.done(dve.tensor_scalar(edge[:, 0:1], base[:, 1:2], q, base[:, 0:1], ALU.min, ALU.add))
                n.done(dve.tensor_scalar(sel[:, 1], cum[:, 1], base[:, 1:2], q, ALU.add, ALU.min))
                n.wait()
                n.done(dve.scalar_tensor_tensor(out=tab[:, 0:P], in0=cum[:, 0], scalar=base[:, 0:1], in1=sel[:, 1],
                                                op0=ALU.add, op1=ALU.add))
                n.done(dve.tensor_scalar(from0[:], slot16[:], edge[:, 0:1], None, ALU.is_ge))
                n.wait()
                n.done(dve.tensor_copy(edge[:, 1:2], tab[:, P - 1:P]))
                n.wait()
                dve.scalar_tensor_tensor(out=oneh[:], in0=slot16[:], scalar=edge[:, 1:2], in1=from0[:],
                                         op0=ALU.is_lt, op1=ALU.mult).then_inc(oneh_ready, 1)

            def number(e, q, n, guard):
                dve.wait_ge(tab_mm, e + 1)
                n.done(dve.tensor_copy(tbase[:].rearrange("p (k c) -> p k c", k=2)[:, 0], bank[5][:, 0:2 * (P + 1)].rearrange("p (c t) -> p c t", c=2)[:, :, P]))
                n.done(dve.tensor_copy(tbase[:].rearrange("p (k c) -> p k c", k=2)[:, 1], bank[6][:, 0:2 * (P + 1)].rearrange("p (c t) -> p c t", c=2)[:, :, P]))
                n.wait()
                for c in range(TG):
                    row = bank[5 + c // 2][:, (c % 2) * (P + 1):(c % 2) * (P + 1) + P]
                    ins = dve.tensor_scalar(junk[:, c * P:(c + 1) * P], row, slotc[:, c:c + 1], tbase[:, c:c + 1], ALU.is_le, ALU.add,
                                            accum_out=cnt4[:, c:c + 1])
                    if c == TG - 1:
                        n.done(ins)
                n.wait()
                if guard is not None:
                    dve.wait_ge(added[q % 2], guard)
                dve.tensor_copy(idx[:, q], cnt4[:]).then_inc(idx_ready, 1)

            def gates(e, p, n, guard):
                dve.wait_ge(xe_in[p], guard)
                if not isinstance(e, int) or e >= 2:
                    dve.wait_ge(ye_ready, e - 1)
                n.done(dve.tensor_copy(gate[:, p], xe[:, p, :, bass.ds(C + e, 1)].rearrange("p c a -> p (c a)")))
                n.wait()

            def weigh(e, p):
                dve.wait_ge(dn_mm, e + 1)
                dve.tensor_tensor(ye[:, p], bank[4][:, :].rearrange("p (c h) -> p c h", c=TG),
                                  gate[:, p].unsqueeze(2).to_broadcast([P, TG, C]), ALU.mult).then_inc(ye_ready, 1)

            PER = 12
            n = Steps(dve, sel_step)
            for e in range(3):
                rank(e, n)
                place(e, n)
                if e < 2:
                    number(e, e, n, None)
            gates(0, 0, n, 64)
            pre = n.n

            def serve(v, last):
                n = Steps(dve, sel_step, pre + 4 * PER * v)
                for q in range(4):
                    e, p = 4 * v + q, q % 2
                    if not (last and q >= 2):
                        number(e + 2, (q + 2) % 4, n, None if first(v) and q < 2 else 64 * (2 * v + q // 2))
                    else:
                        dve.wait_ge(added[p], 64 * (2 * v + q // 2))
                    if not (last and q >= 1):
                        rank(e + 3, n)
                        place(e + 3, n)
                    if not (last and q == 3):
                        gates(e + 1, 1 - p, n, 64 * (2 * v + (q + 1) // 2 + 1))
                    weigh(e, p)
                return n.n
            assert serve(0, False) == 4 * PER
            with dve.Fori(1, NU - 1) as v:
                serve(v, False)
            serve(NU - 1, True)

            PREP = 2 + 1 + 13

            prep_now = {}

            def prep_stats(n, p, i):
                n_ = prep_now["steps"] = Steps(dve, prep_step, PREP * n)
                dve.wait_ge(h2_in[p], 16 * (i + 1))
                for j in range(2):
                    n_.done(dve.bn_stats(st3[:, j], hx[:, p, j]))
                n_.wait()
                dve.nop(nofuse=True)
                for j in range(2):
                    ins = dve.bn_aggr(mv3[:, j], st3[:, j])
                n_.done(ins)
                n_.wait()

            def prep_root(k):
                if k < ROOT:
                    inv_sqrt(k, prep_now["steps"], mv3[:, :, 1], r3[:, 0], r3[:, 1], r3[:, 2])

            def prep_norm(n, p):
                prep_now["steps"].wait()
                if not first(n):
                    dve.wait_ge(xT3_mm, n)
                for j in range(2):
                    ins = dve.tensor_scalar(xn3[:, j], hx[:, p, j], mv3[:, j, 0:1], r3[:, 0, j:j + 1], ALU.subtract, ALU.mult)
                ins.then_inc(xn3_ready, 1)

            def maxima(u, h):
                dve.wait_ge(s_mm, u + 1)
                s2 = bank[SBANK[h % 2]]
                dve.tensor_reduce(nmax[:, h % 4, 0:1], s2[:, 0:P], AX.X, ALU.max, negate=True)
                dve.tensor_reduce(nmax[:, h % 4, 1:2], s2[:, P:3 * P], AX.X, ALU.max, negate=True).then_inc(max_ready, 1)

            def inverses(u, h):
                dve.wait_ge(exp_ready, u + 1)
                dve.reciprocal(rinv[:, h % 4], rsum[:, h % 4]).then_inc(rinv_ready, 1)

            def norm_first(u, h):
                dve.wait_ge(rinv_ready, u + 1)
                dve.tensor_scalar(pr[:, h % 4, 0:P], pr[:, h % 4, 0:P], rinv[:, h % 4, 0:1], None, ALU.mult)

            def norm_rest(u, h):
                dve.tensor_scalar(pr[:, h % 4, P:3 * P], pr[:, h % 4, P:3 * P], rinv[:, h % 4, 1:2], None, ALU.mult)\
                    .then_inc(pr_ready, 1)

            def turn(u, h):
                dve.wait_ge(prT_mm, u + 1)
                if not isinstance(u, int) or u >= 2:
                    dve.wait_ge(head_mm, u - 1)
                dve.tensor_copy(prT[:, h % 2], bank[TBANK[h % 2]][:, 0:3 * P]).then_inc(prT_ready, 1)

            gate_steps = {"per": 0}
            dve.wait_ge(consts4, 15)
            dve.wait_ge(w_d, 16 * 3)

            def gate_stats(g):
                n_ = gate_steps["now"] = Steps(dve, d_step, gate_steps["per"] * g)
                hh = h3[:].rearrange("p q j c -> p (q j) c")
                dve.wait_ge(h3_ready, 2 * g + 2)
                for j in range(TG):
                    n_.done(dve.bn_stats(st4[:, j], hh[:, j]))
                n_.wait()
                dve.nop(nofuse=True)
                for j in range(TG):
                    ins = dve.bn_aggr(mv4[:, j], st4[:, j])
                n_.done(ins)
                n_.wait()

            def gate_root(k):
                if k < ROOT:
                    inv_sqrt(k, gate_steps["now"], mv4[:, :, 1], r4[:, 0], r4[:, 1], r4[:, 2])

            def gate_norm(g):
                gate_steps["now"].wait()
                hh = h3[:].rearrange("p q j c -> p (q j) c")
                if not first(g):
                    dve.wait_ge(spread, 128 * g)
                for j in range(TG):
                    ins = dve.tensor_scalar(xr4[:, 0, j, 0:C], hh[:, j], mv4[:, j, 0:1], r4[:, 0, j:j + 1], ALU.subtract, ALU.mult)
                ins.then_inc(xn4_ready, 1)

            def gate_logits(g):
                dve.wait_ge(gate_mm, g + 1)
                dve.tensor_tensor(lg4[:], bank[GBANK][:, 0:TG * E1].rearrange("p (j x) -> p j x", j=TG),
                                  gb[:].unsqueeze(1).to_broadcast([P, TG, E1]), ALU.add).then_inc(lg4_ready, 1)

            def gate_top(g):
                n_ = gate_steps["now"]
                dve.wait_ge(lg4_ready, g + 1)
                dve.nop(nofuse=True)
                for j in range(TG):
                    ins = dve.max(top[:, j], lg4[:, j])
                n_.done(ins)
                n_.wait()
                dve.nop(nofuse=True)
                for j in range(TG):
                    ins = dve.max_index(topi[:, j], top[:, j], lg4[:, j])
                n_.done(ins)
                dve.tensor_tensor(gap[:], top[:, :, 1], top[:, :, 0], ALU.subtract).then_inc(gap_ready, 1)

            def gate_mask(g):
                n_ = gate_steps["now"]
                n_.wait()
                n_.done(dve.tensor_copy(topf[:], topi[:, :, 0:2]))
                n_.wait()
                for k in range(2):
                    ins = dve.tensor_tensor(hit[:, k], which[:].unsqueeze(1).to_broadcast([P, TG, E1]),
                                            topf[:, :, k:k + 1].to_broadcast([P, TG, E1]), ALU.is_equal)
                n_.done(ins)
                n_.wait()
                dve.tensor_tensor(mask[:], hit[:, 0], hit[:, 1], ALU.add).then_inc(mask_ready, 1)

            def gate_weights(g):
                n_ = gate_steps["now"]
                dve.wait_ge(gap_exp, g + 1)
                n_.done(dve.tensor_scalar(tw[:, 0], tw[:, 1], 1.0, None, ALU.add))
                n_.done(dve.tensor_copy(xr4[:, :, :, C + 1:XW].bitcast(U32).rearrange("p k j a -> p k (j a)"), dest[:]))
                n_.wait()
                n_.done(dve.reciprocal(tw[:, 0], tw[:, 0]))
                n_.done(dve.tensor_scalar(dest[:], dest[:], float(2 * TG * P), None, ALU.add))
                n_.wait()
                n_.done(dve.tensor_tensor(tw[:, 1], tw[:, 1], tw[:, 0], ALU.mult))
                n_.wait()
                n_.done(dve.tensor_copy(xr4[:, :, :, C:C + 1].rearrange("p k j a -> p k (j a)"), tw[:]))

            def gate_place(g):
                n_ = gate_steps["now"]
                dve.wait_ge(rank_mm, g + 1)
                n_.done(dve.tensor_tensor(rk[:], bank[VBANK][:, 0:TG * E1].rearrange("p (j x) -> p j x", j=TG),
                                          nextrow[:].unsqueeze(1).to_broadcast([P, TG, E1]), ALU.add))
                n_.wait()
                dve.tensor_tensor(nextrow[:], nextrow[:], bank[VBANK][:, TG * E1:(TG + 1) * E1], ALU.add).then_inc(rank_read, 1)
                for k in range(2):
                    ins = dve.tensor_tensor(posm[:, k], hit[:, k], rk[:], ALU.mult)
                n_.done(ins)
                n_.wait()
                n_.done(dve.tensor_reduce(posf[:], posm[:], AX.X, ALU.add))
                n_.wait()
                dve.wait_ge(rank_read, g + 1)
                dve.tensor_copy(pos[:], posf[:]).then_inc(pos_ready, 1)
                gate_steps["per"] = n_.n

            prep_stats(0, 0, 0)
            for k in range(ROOT):
                prep_root(k)
            prep_norm(0, 0)
            assert prep_now["steps"].n == PREP

            def finish(n, q, i, p):
                dve.wait_ge(head_mm, H1 * n + H1)
                dve.wait_ge(hb_ready, n + 1)
                if not isinstance(n, int) or n >= 2:
                    dve.wait_ge(h3_out[q], 16 * (i - 1 + p))
                dve.tensor_tensor(h3[:, q], bank[OBANK[q]][:, 0:2 * P].rearrange("p (j c) -> p j c", j=2), hb[:, q], ALU.add)\
                    .then_inc(h3_ready, 1)

            def slots(i, last):
                for p in range(2):
                    n = 2 * i + p
                    for h in range(H1):
                        u = H1 * n + h
                        if h in (1, 2, 3) and not (last and p == 1):
                            root = [prep_root, 5 * (h - 1)]
                        elif p == 0 and h in (5, 6, 7) and there(i - 1):
                            root = [gate_root, 5 * (h - 5)]
                        else:
                            root = [None, 0]

                        def root_step(root=root):
                            if root[0]:
                                root[0](root[1])
                                root[1] += 1
                        if (p, h) == (1, 7) and there(i - 1):
                            gate_place(i - 1)
                        root_step()
                        if there(u - N_LAG):
                            inverses(u - N_LAG, (h - N_LAG) % H1)
                        if there(u - S_LAG):
                            maxima(u - S_LAG, (h - S_LAG) % H1)
                        root_step()
                        if there(u - N_LAG):
                            norm_first(u - N_LAG, (h - N_LAG) % H1)
                        root_step()
                        if there(u - N_LAG):
                            norm_rest(u - N_LAG, (h - N_LAG) % H1)
                        root_step()
                        if (p, h) == (1, 3) and there(i - 1):
                            gate_logits(i - 1)
                        if there(u - T_LAG):
                            turn(u - T_LAG, (h - T_LAG) % H1)
                        root_step()
                        if h == 0 and not (last and p == 1):
                            prep_stats(n + 1, 1 - p, i + p)
                        if h == 4 and not (last and p == 1):
                            prep_norm(n + 1, 1 - p)
                        if h == O_LAG - 1 and there(u - O_LAG):
                            finish(n - 1, 1 - p, i, p)
                        if (p, h) in GATE_SLOTS and there(i - 1):
                            GATE_SLOTS[p, h](i - 1)
            GATE_SLOTS = {(0, 4): gate_stats, (0, 7): gate_norm, (1, 4): gate_top,
                          (1, 5): gate_mask, (1, 6): gate_weights}
            slots(0, False)
            slots(1, False)
            with dve.Fori(2, NB // 2 - 1) as i:
                slots(i, False)
            slots(NB // 2 - 1, True)
            U = NB * H1
            inverses(U - 2, H1 - 2)
            maxima(U - 1, H1 - 1)
            norm_first(U - 2, H1 - 2)
            norm_rest(U - 2, H1 - 2)
            turn(U - 3, H1 - 3)
            inverses(U - 1, H1 - 1)
            norm_first(U - 1, H1 - 1)
            norm_rest(U - 1, H1 - 1)
            turn(U - 2, H1 - 2)
            turn(U - 1, H1 - 1)
            finish(NB - 1, 1, NB // 2, 0)
            gate_stats(NG - 1)
            for k in range(ROOT):
                gate_root(k)
            gate_norm(NG - 1)
            gate_logits(NG - 1)
            gate_top(NG - 1)
            gate_mask(NG - 1)
            gate_weights(NG - 1)
            gate_place(NG - 1)

            n_ = Steps(dve, table_step)
            n_.done(dve.tensor_tensor(padi[:], nextrow[:].unsqueeze(1).to_broadcast([P, 2, E1]),
                                      padc[:].unsqueeze(2).to_broadcast([P, 2, E1]), ALU.add))
            n_.wait()
            dve.nop().then_inc(pad_ready, 1)
            n_.done(dve.tensor_tensor(nun[:], nextrow[0:1, :], row0f[0:1, :], ALU.subtract))
            n_.wait()
            n_.done(dve.tensor_scalar(nuni[:], nun[:], float(UT - 1), None, ALU.add))
            n_.wait()
            n_.done(dve.tensor_scalar(nuni[:], nuni[:], 8, None, ALU.logical_shift_right))
            n_.wait()
            n_.done(dve.tensor_copy(nun[:], nuni[:]))
            n_.wait()
            n_.done(dve.tensor_tensor_scan(cun[:], ones[0:1, 0:E1], nun[:], 0.0, ALU.mult, ALU.add))
            n_.wait()
            n_.done(dve.tensor_tensor(past[:], uf[:].unsqueeze(2).to_broadcast([1, NUN, E1]),
                                      cun[:].unsqueeze(1).to_broadcast([1, NUN, E1]), ALU.is_ge))
            n_.done(dve.tensor_scalar(nun[:], nun[:], -float(UT), float(REG), ALU.mult, ALU.add))
            n_.wait()
            n_.done(dve.tensor_reduce(ux[:], past[:], AX.X, ALU.add))
            n_.wait()
            n_.done(dve.tensor_scalar(unit_x[:], ux[:], float(E1 - 1), None, ALU.min))
            n_.done(dve.tensor_tensor(past[:], past[:], nun[:].unsqueeze(1).to_broadcast([1, NUN, E1]), ALU.mult))
            n_.wait()
            n_.done(dve.tensor_reduce(ur[:], past[:], AX.X, ALU.add))
            n_.wait()
            dve.scalar_tensor_tensor(out=unit_r[:], in0=uf[:], scalar=float(UT), in1=ur[:], op0=ALU.mult, op1=ALU.add)\
                .then_inc(table_ready, 1)

            dve.wait_ge(table_ready, 1)
            dve.wait_ge(w_d2, 48)

            def weights1(u, q):
                x = dve.value_load(unit_x[0:1, bass.ds(u, 1)], min_val=0, max_val=E1 - 1)
                if not isinstance(u, int) or u >= 2:
                    dve.wait_ge(upu_mm, u - 1)
                dve.nop(nofuse=True)
                dve.tensor_copy(w1u[:, q % 2], w1s[:, bass.ds(x, 1)].rearrange("p a f -> p (a f)")).then_inc(w1u_ready, 1)
                return x

            def weights2(u, q, x):
                if not isinstance(u, int) or u >= 2:
                    dve.wait_ge(dnu_mm, u - 1)
                dve.nop(nofuse=True)
                dve.tensor_copy(w2u[:, q % 2], w2s[:, bass.ds(x, 1)].rearrange("p a f -> p (a f)")).then_inc(w2u_ready, 1)

            def unit_out(u, q, v):
                x = dve.value_load(unit_x[0:1, bass.ds(u, 1)], min_val=0, max_val=E1 - 1)
                dve.wait_ge(dnu_mm, u + 1)
                dve.nop(nofuse=True)
                dve.tensor_tensor(tu[:, q % 2], bank[4 + q % 2][:, 0:2 * C].rearrange("p (j c) -> p j c", j=2),
                                  b2s[:, bass.ds(x, 1)].to_broadcast([P, 2, C]), ALU.add).then_inc(tu_ready, 1)
                dve.wait_ge(tu_ready, u + 1)
                if not isinstance(u, int) or u >= YR:
                    dve.wait_ge(z_out[(q - YR) % XR], 32 * (v + 1 if q >= YR else v))
                dve.tensor_tensor(yu[:, q % YR], tu[:, q % 2], xu[:, q, :, C:C + 1].to_broadcast([P, 2, C]), ALU.mult)\
                    .then_inc(yu_ready, 1)

            def units(v, last):
                for q in range(XR):
                    u = XR * v + q
                    more = not (last and q == XR - 1)
                    if more:
                        x = weights1(u + 1, q + 1)
                        weights2(u + 1, q + 1, x)
                    if there(u - 1):
                        unit_out(u - 1, (q - 1) % XR, v if q else v - 1)
            weights2(0, 0, weights1(0, 0))
            units(0, False)
            with dve.Fori(1, NUN // XR - 1) as v:
                units(v, False)
            units(NUN // XR - 1, True)
            unit_out(NUN - 1, XR - 1, NUN // XR - 1)

            def results(i):
                for p in range(2):
                    g = 2 * i + p
                    dve.wait_ge(z_in[p], 32 * (i + 1))
                    if not first(i):
                        dve.wait_ge(out_done[p], 16 * i)
                    dve.tensor_tensor(res[:, p], zx[:, p, :, 0:C], zx[:, p, :, C:2 * C], ALU.add).then_inc(res_step, 1)
                    dve.wait_ge(res_step, g + 1)
                    dve.tensor_tensor(res[:, p], res[:, p], h3x[:, p], ALU.add).then_inc(res_ready, 1)
            results(0)
            with dve.Fori(1, NG // 2) as i:
                results(i)

        @block.tensor
        def _(pe):
            pe.wait_ge(consts, 7)
            pe.wait_ge(w_in, 16 * 7)
            pe.wait_ge(prep_c, 2)
            pe.transpose(bank[0][:, 0:P], idrowf[:], ident[:]).then_inc(prep_t, 1)
            for k in range(3):
                pe.transpose(bank[1][:, k * P:(k + 1) * P], wqkv_n[:, k], ident[:]).then_inc(prep_t, 1)
            pe.transpose(bank[2][:, 0:P], wproj_n[:], ident[:]).then_inc(prep_t, 1)
            pe.transpose(bank[3][:, 0:H0], head[:], ident[0:H0, 0:H0]).then_inc(prep_t, 1)
            pe.matmul(bank[4][:, 0:P], headt[:], head[:], start=True, stop=True).then_inc(prep_t, 1)
            pe.wait_ge(prep_c, 6)

            def pair(i):
                for p in range(2):
                    g = 2 * i + p
                    pe.wait_ge(xn_ready, g + 1)
                    for j in range(TG):
                        ins = pe.transpose(bank[4 * p][:, j * P:(j + 1) * P], xn[:, p, j], ident[:])
                    ins.then_inc(xT_mm, 1)
                for p in range(2):
                    g = 2 * i + p
                    pe.wait_ge(xT_ready, g + 1)
                    for m in range(2):
                        for j in range(2):
                            t = 2 * m + j
                            ins = pe.matmul(bank[4 * p + 1 + m][:, j * 2 * C:(j + 1) * 2 * C], xT[:, p, t * P:(t + 1) * P],
                                            wqkvT[:, C:3 * C], start=True, stop=True)
                        ins.then_inc(kv_mm, 1)
                for p in range(2):
                    g = 2 * i + p
                    if not first(i):
                        pe.wait_ge(pT_ready, g - 1)
                    pe.matmul(bank[4 * p + 3][:, :], wqkvT[:, 0:C], xT[:, p], start=True, stop=True).then_inc(q_mm, 1)
                for p in range(2):
                    g = 2 * i + p
                    pe.wait_ge(kv_ready, 4 * g + 4)
                    for b in range(2):
                        for j in range(2):
                            ins = pe.matmul(bank[4 * p][:, b * (C + 1):(b + 1) * (C + 1)], kk[:, p, 2 * b + j],
                                            vv[:, p, 2 * b + j], start=(j == 0), stop=(j == 1))
                    ins.then_inc(kvs_mm, 1)
                for p in range(2):
                    g = 2 * i + p
                    pe.wait_ge(q_ready, g + 1)
                    pe.wait_ge(md_ready, g + 1)
                    for m in range(2):
                        for j in range(2):
                            t = 2 * m + j
                            ins = pe.matmul(bank[4 * p + 1 + m][:, j * (C + H0):(j + 1) * (C + H0)], qT[:, p, t * P:(t + 1) * P],
                                            md[:, p, m], start=True, stop=True)
                        ins.then_inc(o_mm, 1)
                for p in range(2):
                    g = 2 * i + p
                    pe.wait_ge(o_ready, g + 1)
                    for j in range(TG):
                        ins = pe.transpose(bank[4 * p][:, j * P:(j + 1) * P], oo[:, p, j], ident[:])
                    ins.then_inc(oT_mm, 1)
                for p in range(2):
                    g = 2 * i + p
                    pe.wait_ge(oT_ready, g + 1)
                    for j in range(TG):
                        ins = pe.matmul(bank[4 * p + 1][:, j * P:(j + 1) * P], oT[:, p, j * P:(j + 1) * P], wprojT[:],
                                        start=True, stop=True)
                    ins.then_inc(y_mm, 1)
                for p in range(2):
                    g = 2 * i + p
                    pe.wait_ge(x2_ready, g + 1)
                    for j in range(TG):
                        ins = pe.transpose(bank[4 * p][:, j * P:(j + 1) * P], xr[:, p, j, 0:C], ident[:])
                    ins.then_inc(x2T_mm, 1)
                for p in range(2):
                    g = 2 * i + p
                    pe.wait_ge(x2T_ready, g + 1)
                    for j in range(TG):
                        ins = pe.matmul(bank[4 * p + 2][:, j * E0:(j + 1) * E0], x2T[:, p, j * P:(j + 1) * P], wrout[:],
                                        start=True, stop=True)
                    ins.then_inc(lg_mm, 1)
                for p in range(2):
                    g = 2 * i + p
                    pe.wait_ge(p_ready, g + 1)
                    pe.transpose(bank[4 * p + 3][:, 0:P], pg[:, p].rearrange("p j e -> p (j e)"), ident[:]).then_inc(pT_mm, 1)

            pair(0)
            with pe.Fori(1, NG // 2) as i:
                pair(i)

            pe.wait_ge(pa_ready, NG)
            pe.wait_ge(pT_ready, NG)
            for k in range(8):
                for j in range(4):
                    ins = pe.transpose(bank[k][:, j * P:(j + 1) * P], pa[:, :, 4 * k + j], ident[:])
                ins.then_inc(pcT_mm, 1)
            pe.wait_ge(w_b, 16)
            pe.wait_ge(pc_ready, 8)
            for k in range(3):
                ins = pe.transpose(bank[1][0:FCH[k], 8 * k:8 * k + 8], bup_n[:, k * P:k * P + FCH[k]], ident[0:8, 0:8])
            ins.then_inc(bup_mm, 1)
            pe.wait_ge(bup_ready, 2)
            pe.wait_ge(lanes_s, 4)

            def count(b):
                pe.wait_ge(cnt_ready, b + 1)
                pe.matmul(bank[0][:, 0:1], lanes[:], cnt[:, 0:1], start=True, stop=True).then_inc(cnt_mm, 1)

            pe.wait_ge(w_c, 16 * 5)
            for h in range(H1):
                count(h)
                if h > 0:
                    pe.wait_ge(fold_ready, 2 * h)
                for k, w in enumerate((wqn, wkn, wvn)):
                    ins = pe.transpose(bank[2][:, k * C:(k + 1) * C], w[:, h * C:(h + 1) * C], ident[:])
                ins.then_inc(wT_mm, 1)
                pe.wait_ge(wT_ready, h + 1)
                pe.matmul(bank[3][:, 0:C], wT[:, 0], wT[:, 1], start=True, stop=True)
                pe.matmul(bank[3][:, C:2 * C], wT[:, 2], won[:, h], start=True, stop=True).then_inc(fold_mm, 1)
            pe.wait_ge(w_d, 16 * 3)
            pe.wait_ge(fold_ready, 2 * H1)
            for k in range(2):
                ins = pe.transpose(bank[2][:, k * E1:(k + 1) * E1], b1n[:, k * P:(k + 1) * P], ident[0:E1, 0:E1])
            ins.then_inc(b1_mm, 1)
            with pe.Fori(H1, 31) as b:
                count(b)
            pe.wait_ge(diag_ready, 1)
            for k in range(2):
                ins = pe.matmul(bank[1][:, k * E0:(k + 1) * E0], ones[0:E0, :], diag[:, k], start=True, stop=True)
            ins.then_inc(tq_mm, 1)

            def bases(e):
                pe.wait_ge(cum_ready, e + 1)
                pe.matmul(bank[7][:, 0:2], before[:], cum[:, :, P - 1], start=True, stop=True).then_inc(base_mm, 1)

            def rows(e):
                pe.wait_ge(oneh_ready, e + 1)
                for c in range(TG):
                    o = bank[5 + c // 2][:, (c % 2) * (P + 1):(c % 2 + 1) * (P + 1)]
                    ins = pe.matmul(o, oneh[:, c * P:(c + 1) * P], tab[:], start=True, stop=True)
                ins.then_inc(tab_mm, 1)

            pe.wait_ge(tq_ready, 1)
            for e in range(3):
                bases(e)
                if e < 2:
                    rows(e)

            def turn_rows(e, p, guard):
                pe.wait_ge(xe_in[p], guard)
                for c in range(TG):
                    ins = pe.transpose(bank[0][:, c * P:(c + 1) * P], xe[:, p, c, 0:C], ident[:])
                ins.then_inc(xeT_mm, 1)
            turn_rows(0, 0, 64)

            def serve(v, last):
                for q in range(4):
                    e, p = 4 * v + q, q % 2
                    if not (last and q >= 2):
                        rows(e + 2)
                    pe.wait_ge(xeT_ready, e + 1)
                    pe.wait_ge(wup_in[p], 16 * (2 * v + q // 2 + 1))
                    for k in range(3):
                        pe.matmul(bank[1 + k][0:FCH[k], :], wup[:, p, k * P:k * P + FCH[k]], xeT[:], start=True, stop=True)\
                            .then_inc(up_mm, 1)
                    if not (last and q >= 1):
                        bases(e + 3)
                    if not (last and q == 3):
                        turn_rows(e + 1, 1 - p, 64 * (2 * v + (q + 1) // 2 + 1))
                    pe.wait_ge(ac_ready, 3 * e + 3)
                    pe.wait_ge(wdn_in[p], 48 * (2 * v + q // 2 + 1))
                    if not (first(v) and q == 0):
                        pe.wait_ge(ye_ready, e)
                    for c in range(TG):
                        for k in range(3):
                            m = FCH[k] + (k == 2)
                            ins = pe.matmul(bank[4][:, c * P:(c + 1) * P], ac[0:m, k, c * P:(c + 1) * P], wdn[0:m, p, k],
                                            start=(k == 0), stop=(k == 2))
                    ins.then_inc(dn_mm, 1)
            serve(0, False)
            with pe.Fori(1, NU - 1) as v:
                serve(v, False)
            serve(NU - 1, True)

            pe.wait_ge(fold_ready, 2 * H1)
            pe.wait_ge(consts3, 3)
            pe.wait_ge(ye_ready, E0)
            pe.wait_ge(idx_ready, E0)

            def turned(n):
                pe.wait_ge(xn3_ready, n + 1)
                if not first(n):
                    pe.wait_ge(vo_ready, 4 * n)
                for j in range(2):
                    ins = pe.transpose(bank[VBANK][:, j * P:(j + 1) * P], xn3[:, j], ident[:])
                ins.then_inc(xT3_mm, 1)

            def scores(u, h, p, n):
                s2 = bank[SBANK[h % 2]]
                g = gT[:, h // 2 % 2, (h % 2) * 2 * P:(h % 2 + 1) * 2 * P]
                pe.wait_ge(g_ready, 4 * n + h // 2 + 1)
                if not isinstance(u, int) or u >= 2:
                    pe.wait_ge(exp_ready, u - 1)
                pe.matmul(s2[:, 0:P], g[:, 0:P], xT3[:, p, 0:P], start=True, stop=False)
                pe.matmul(s2[:, 0:P], identb[:], causal[:], start=False, stop=True)
                pe.matmul(s2[:, 2 * P:3 * P], identb[:], causal[:], start=True, stop=False, skip_group_check=True)
                pe.matmul(s2[:, P:3 * P], g[:, P:2 * P], xT3[:, p], start=False, stop=True, skip_group_check=True)\
                    .then_inc(s_mm, 1)

            def turns(u, h):
                pe.wait_ge(pr_ready, u + 1)
                if not isinstance(u, int) or u >= 2:
                    pe.wait_ge(prT_ready, u - 1)
                for k in range(3):
                    ins = pe.transpose(bank[TBANK[h % 2]][:, k * P:(k + 1) * P], pr[:, h % 4, k * P:(k + 1) * P], ident[:])
                ins.then_inc(prT_mm, 1)

            def sums(u, h, p, n):
                o = bank[OBANK[p]]
                pe.wait_ge(prT_ready, u + 1)
                if h == 0:
                    pe.wait_ge(vo_ready, 4 * n + 4)
                    if not isinstance(n, int) or n >= 2:
                        pe.wait_ge(h3_ready, n - 1)
                v0, v1 = (vo[:, p, j, h * C:(h + 1) * C] for j in range(2))
                pe.matmul(o[:, 0:P], prT[:, h % 2, 0:P], v0, start=(h == 0), stop=False, skip_group_check=True)
                pe.matmul(o[:, P:2 * P], prT[:, h % 2, P:2 * P], v0, start=False, stop=False, skip_group_check=True)
                pe.matmul(o[:, P:2 * P], prT[:, h % 2, 2 * P:3 * P], v1, start=False, stop=(h == H1 - 1),
                          skip_group_check=True).then_inc(head_mm, 1)

            def slots(i, last):
                for p in range(2):
                    n = 2 * i + p
                    for h in range(H1):
                        u = H1 * n + h
                        if h == 0:
                            pe.wait_ge(xT3_ready, n + 1)
                        if (p, h) == (1, 1) and there(i - 1):
                            pe.wait_ge(g_ready, 4 * n + 1)
                            gate_turn(i - 1)
                        if (p, h) == (1, 3) and there(i - 1):
                            pe.wait_ge(g_ready, 4 * n + 2)
                            gate_products(i - 1)
                        if h % 2 == 0:
                            if (p, h) == (1, 2) and there(i - 1):
                                pe.wait_ge(xT4_ready, i)
                            if (p, h) == (1, 4) and there(i - 1):
                                pe.wait_ge(lg4_ready, i)
                            for k in range(2):
                                ins = pe.matmul(bank[GBANK][:, k * 2 * P:(k + 1) * 2 * P], wqk[:, h + k], xT3[:, p], start=True, stop=True)
                            ins.then_inc(g_mm, 1)
                        if h < 4:
                            if h == 0 and p == 0 and there(i - 2):
                                pe.wait_ge(rank_read, i - 1)
                            if h > 0:
                                pe.wait_ge(vo_ready, 4 * n + h)
                            pe.matmul(bank[VBANK][:, :], xT3[:, p, (h % 2) * P:(h % 2 + 1) * P],
                                      wvo[:, 4 * (h // 2):4 * (h // 2) + 4], start=True, stop=True).then_inc(vo_mm, 1)
                        if h == 6 and not (last and p == 1):
                            turned(n + 1)
                        if there(u - S_LAG):
                            scores(u - S_LAG, (h - S_LAG) % H1, p if h >= S_LAG else 1 - p, n if h >= S_LAG else n - 1)
                        if there(u - T_LAG):
                            turns(u - T_LAG, (h - T_LAG) % H1)
                        if there(u - O_LAG):
                            sums(u - O_LAG, (h - O_LAG) % H1, p if h >= O_LAG else 1 - p, n if h >= O_LAG else n - 1)
                        if (p, h) == (1, 6) and there(i - 1):
                            if not last:
                                pe.wait_ge(xT3_ready, n + 2)
                            gate_ranks(i - 1)

            def gate_turn(g):
                pe.wait_ge(xn4_ready, g + 1)
                for j in range(TG):
                    ins = pe.transpose(bank[GBANK][:, j * P:(j + 1) * P], xr4[:, 0, j, 0:C], ident[:])
                ins.then_inc(xT4_mm, 1)

            def gate_products(g):
                pe.wait_ge(xT4_ready, g + 1)
                for j in range(TG):
                    ins = pe.matmul(bank[GBANK][:, j * E1:(j + 1) * E1], xT4[:, j * P:(j + 1) * P], gw[:], start=True, stop=True)
                ins.then_inc(gate_mm, 1)

            def gate_ranks(g):
                pe.wait_ge(mask_ready, g + 1)
                for j in range(TG + 1):
                    o = bank[VBANK][:, j * E1:(j + 1) * E1]
                    if j < TG:
                        pe.matmul(o, beforeb[:], mask[:, j], start=True, stop=(j == 0))
                    for k in range(j):
                        ins = pe.matmul(o, onesb[:], mask[:, k], start=(j == TG and k == 0), stop=(k == j - 1))
                ins.then_inc(rank_mm, 1)

            turned(0)
            slots(0, False)
            slots(1, False)
            with pe.Fori(2, NB // 2 - 1) as i:
                slots(i, False)
            slots(NB // 2 - 1, True)
            U = NB * H1
            scores(U - 1, H1 - 1, 1, NB - 1)
            turns(U - 3, H1 - 3)
            sums(U - 4, H1 - 4, 1, NB - 1)
            turns(U - 2, H1 - 2)
            sums(U - 3, H1 - 3, 1, NB - 1)
            turns(U - 1, H1 - 1)
            sums(U - 2, H1 - 2, 1, NB - 1)
            sums(U - 1, H1 - 1, 1, NB - 1)
            pe.wait_ge(rank_read, NG - 1)
            gate_turn(NG - 1)
            gate_products(NG - 1)
            pe.wait_ge(lg4_ready, NG)
            gate_ranks(NG - 1)

            pe.wait_ge(rank_read, NG)
            pe.wait_ge(h3_ready, NB)

            def unit_turn(u, q, v):
                pe.wait_ge(xu_in[q], 16 * (v + 1))
                for j in range(2):
                    ins = pe.transpose(bank[q % 2][:, j * P:(j + 1) * P], xu[:, q, j, 0:C], ident[:])
                ins.then_inc(xTu_mm, 1)

            def unit_up(u, q):
                pe.wait_ge(xTu_ready, u + 1)
                pe.wait_ge(w1u_ready, u + 1)
                for k in range(2):
                    ins = pe.matmul(bank[2 + q % 2][:, k * UT:(k + 1) * UT], w1u[:, q % 2, k * P:(k + 1) * P], xTu[:, q % 2],
                                    start=True, stop=True)
                ins.then_inc(upu_mm, 1)

            def unit_down(u, q):
                pe.wait_ge(hTu_ready, u + 1)
                pe.wait_ge(w2u_ready, u + 1)
                if not isinstance(u, int) or u >= 2:
                    pe.wait_ge(tu_ready, u - 1)
                for j in range(2):
                    for k in range(2):
                        ins = pe.matmul(bank[4 + q % 2][:, j * C:(j + 1) * C], hTu[:, q % 2, k, j * P:(j + 1) * P],
                                        w2u[:, q % 2, k * C:(k + 1) * C], start=(k == 0), stop=(k == 1))
                ins.then_inc(dnu_mm, 1)

            def units(v, last):
                for q in range(XR):
                    u = XR * v + q
                    if not (last and q == XR - 1):
                        unit_turn(u + 1, (q + 1) % XR, v if q < XR - 1 else v + 1)
                    unit_up(u, q)
                    if there(u - 1):
                        unit_down(u - 1, (q - 1) % XR)
            unit_turn(0, 0, 0)
            units(0, False)
            with pe.Fori(1, NUN // XR - 1) as v:
                units(v, False)
            units(NUN // XR - 1, True)
            unit_down(NUN - 1, XR - 1)


_INS = ['x', 'L0_tok_weight', 'L0_attn_Wqkv', 'L0_attn_temperature', 'L0_attn_Wproj', 'L0_attn_bproj',
        'L0_ffn_W_router', 'L0_ffn_b_router', 'L0_ffn_W_up', 'L0_ffn_b_up', 'L0_ffn_W_down', 'L0_ffn_b_down',
        'L1_attn_Wq', 'L1_attn_Wk', 'L1_attn_Wv', 'L1_attn_Wo', 'L1_attn_bo', 'L1_ffn_gate_w', 'L1_ffn_gate_b',
        'L1_ffn_w1', 'L1_ffn_b1', 'L1_ffn_w2', 'L1_ffn_b2']


def kernel(**inputs):
    import numpy as _np
    import concourse.bacc as _bacc
    from concourse import mybir as _mybir
    from concourse.bass_utils import run_bass_kernel_spmd as _run

    nc = _bacc.Bacc("TRN2", target_bir_lowering=False, num_devices=1)
    arrays, args = {}, []
    for name in _INS:
        a = _np.ascontiguousarray(inputs[name])
        arrays[f"in_{name}_dram"] = a
        args.append(nc.dram_tensor(f"in_{name}_dram", a.shape, _mybir.dt.from_np(a.dtype), kind="ExternalInput").ap())
    args.append(nc.dram_tensor("out_0_dram", (64, 256, C), F32, kind="ExternalOutput").ap())
    lm_tower(nc, *args)
    r = _run(nc, [arrays], core_ids=[0])
    return r.results[0]["out_0_dram"]
```

```python
from contextlib import ExitStack

import concourse.bass as bass
from concourse import mybir

F32 = mybir.dt.float32
F16 = mybir.dt.float16
F32R = mybir.dt.float32r
BF16 = mybir.dt.bfloat16
U32 = mybir.dt.uint32
U16 = mybir.dt.uint16
I32 = mybir.dt.int32
ALU = mybir.AluOpType
ACT = mybir.ActivationFunctionType
AX = mybir.AxisListType

P = 128
C = 128
NTOK = 64 * 256
NT = NTOK // P
TG = 4
NG = NT // TG
EPS = 1e-5
H0, D0 = 8, 16
E0 = 32
CAP = NTOK // E0
FF = 341
FCH = (128, 128, FF - 256)
ROW = C + E0
H1 = 8
E1, F1 = 8, 256
BIG = 1e30
UT = 2 * P
XR = 8
YR = 4
NUN = XR * ((NTOK * 2 // UT + E1 - 1 + XR - 1) // XR)
REG = NTOK + UT
XW = C + 2
NOWHERE = 1 << 20


def first(i):
    return isinstance(i, int) and i == 0


class Steps:

    def __init__(self, eng, sem, base=0):
        self.eng, self.sem, self.base, self.n = eng, sem, base, 0

    def done(self, ins):
        ins.then_inc(self.sem, 1)
        self.n += 1

    def wait(self):
        self.eng.wait_ge(self.sem, self.base + self.n)


def lm_tower(nc, x, L0_tok_weight, L0_attn_Wqkv, L0_attn_temperature, L0_attn_Wproj, L0_attn_bproj,
             L0_ffn_W_router, L0_ffn_b_router, L0_ffn_W_up, L0_ffn_b_up, L0_ffn_W_down, L0_ffn_b_down,
             L1_attn_Wq, L1_attn_Wk, L1_attn_Wv, L1_attn_Wo, L1_attn_bo,
             L1_ffn_gate_w, L1_ffn_gate_b, L1_ffn_w1, L1_ffn_b1, L1_ffn_w2, L1_ffn_b2, out):
    with ExitStack() as ctx:
        def sb(name, shape, dt=F32):
            return ctx.enter_context(nc.sbuf_tensor(name, shape, dt))

        def sem(name):
            return ctx.enter_context(nc.semaphore(name))

        bank = [ctx.enter_context(nc.psum_tensor(f"bank{n}", [P, 512], F32)) for n in range(8)]

        hbuf = nc.dram_tensor("hbuf", (NTOK, C), F32).ap()
        xrow = nc.dram_tensor("xrow", (NTOK, ROW), F32).ap()
        h3buf = nc.dram_tensor("h3buf", (NTOK, C), F32).ap()
        hbuf_b = hbuf.rearrange("(n j p) c -> n p j c", j=2, p=P)
        h3buf_g = h3buf.rearrange("(g j p) c -> g p j c", j=TG, p=P)
        out_g = out.rearrange("b (j p) c -> (b j) p c", p=P).rearrange("(g j) p c -> g p j c", j=TG)
        spread_rows = nc.dram_tensor("spread_rows", (E1 * REG + 8 * UT, XW), F32).ap()
        zbuf = nc.dram_tensor("zbuf", (2 * NTOK, C), F32).ap()
        zbuf_g = zbuf.rearrange("(g j p k) c -> g p j (k c)", j=TG, p=P, k=2)
        h3buf_b = h3buf.rearrange("(n j p) c -> n p j c", j=2, p=P)
        hbuf_g = hbuf.rearrange("(g j p) c -> g p j c", j=TG, p=P)
        xrow_g = xrow.rearrange("(g j p) c -> g p j c", j=TG, p=P)

        ident = sb("ident", [P, P])
        ones = sb("ones", [P, P])
        head = sb("head", [H0, P])
        headt = sb("headt", [H0, P])
        headc = sb("headc", [P, H0])
        mtemp = sb("mtemp", [P, P])
        temp = sb("temp", [H0, 1])
        junkf = sb("junkf", [P, CAP], I32)
        slotf = sb("slotf", [P, TG], I32)
        tilef = sb("tilef", [P, 1], I32)
        whichi = sb("whichi", [P, E1], I32)
        wqkv_n = sb("wqkv_n", [P, 3, C])
        wproj_n = sb("wproj_n", [P, C])
        wqkvT = sb("wqkvT", [P, 3 * C])
        wprojT = sb("wprojT", [P, C])
        bproj = sb("bproj", [P, C])
        wrout = sb("wrout", [P, E0])
        brout = sb("brout", [P, E0])
        idrow = sb("idrow", [P, P], I32)
        idrowf = sb("idrowf", [P, P])
        ids = sb("ids", [P, NT], U32)
        vo_place = sb("vo_place", [P, 4, 2 * TG * C])
        pr_place = sb("pr_place", [P, 3, 2 * TG * C])

        def group_view(place, k):
            return place[:, k].rearrange("p (q j c) -> p q j c", q=2, j=TG)
        idst = sb("idst", [P, 4, TG], U32)
        xg = vo_place[:, 0:2].rearrange("p k (q j c) -> p (k q) j c", q=2, j=TG)
        st = sb("st", [P, 4, TG, 6])
        mv = sb("mv", [P, 4, TG, 2])
        lnv = sb("lnv", [P, 4, TG])
        rs = sb("rs", [P, 4, TG])
        rt = sb("rt", [P, 4, TG])
        nm = sb("nm", [P, 4, TG])
        xn = group_view(vo_place, 2)
        xT = vo_place[:, 3].rearrange("p (q t) -> p q t", q=2)
        kk = group_view(pr_place, 0)
        vv = sb("vv", [P, 2, TG, C + 1])
        qT = sb("qT", [P, 2, TG * P])
        md = sb("md", [P, 2, 2, C + H0])
        den = sb("den", [P, 2, TG, H0])
        oo = group_view(pr_place, 1)
        oT = pr_place[:, 2].rearrange("p (q t) -> p q t", q=2)
        h1 = sb("h1", [P, 2, TG, C])
        xr = sb("xr", [P, 2, TG, ROW])
        x2T = sb("x2T", [P, 2, TG * P])
        lg = sb("lg", [P, 2, TG, E0])
        mx = sb("mx", [P, 2, TG])
        sm = sb("sm", [P, 2, TG])
        pg = sb("pg", [P, 2, TG, E0])
        pa = sb("pa", [P, NT, E0])
        kb = sb("kb", [P, NG * P])

        lanes = sb("lanes", [P, P])
        before = sb("before", [P, P])
        slot16 = sb("slot16", [P, CAP], F16)
        slotc = sb("slotc", [P, TG])
        junk = sb("junk", [P, NG * P], BF16)
        half16 = vo_place[:, 0:2].rearrange("p k n -> p (k n)").bitcast(U16)
        thr = sb("thr", [P, 1])
        thrh = sb("thrh", [P, 1])
        thrw = sb("thrw", [P, 2], U32)
        cand = sb("cand", [P, 1])
        bit = sb("bit", [P, 1])
        nextbit = sb("nextbit", [P, 1])
        keep = sb("keep", [P, 1])
        need = sb("need", [P, 1])
        cnt = sb("cnt", [P, 1])
        quota = sb("quota", [P, 1])
        diag = sb("diag", [E0, 2, E0])
        tq = sb("tq", [P, 2, E0])
        pc = sb("pc", [P, E0, P])
        xb = pc[:, 0:4 * TG].rearrange("p (q j) c -> p q j c", q=4)
        sel = sb("sel", [P, 2, P])
        cum = sb("cum", [P, 2, P])
        base = sb("base", [P, 2])
        edge = sb("edge", [P, 2])
        tab = sb("tab", [P, P + 1], F16)
        from0 = sb("from0", [P, CAP], F16)
        oneh = sb("oneh", [P, CAP], F16)
        tbase = sb("tbase", [P, TG])
        cnt4 = sb("cnt4", [P, TG])
        idx = sb("idx", [P, 4, TG], U32)
        xe = sb("xe", [P, 2, TG, ROW])
        xeT = sb("xeT", [P, TG * P])
        wup = sb("wup", [P, 2, FF])
        bup_n = sb("bup_n", [8, FF])
        bupT = sb("bupT", [P, 3, 8])
        bupg = sb("bupg", [P, 3])
        wdn = sb("wdn", [P, 2, 3, C])
        ac = sb("ac", [P, 3, TG * P])
        gate = sb("gate", [P, 2, TG])
        ye = sb("ye", [P, 2, TG, C])

        identb = sb("identb", [P, P], BF16)
        causal = sb("causal", [P, P], BF16)
        wT = sb("wT", [P, 3, C])
        wqk = sb("wqk", [P, H1, C])
        wvo = sb("wvo", [P, H1, C])
        bo = sb("bo", [P, C])
        hx = sb("hx", [P, 2, 2, C])
        hb = sb("hb", [P, 2, 2, C])
        h3 = sb("h3", [P, 2, 2, C])
        st3 = sb("st3", [P, 2, 6])
        mv3 = sb("mv3", [P, 2, 2])
        r3 = sb("r3", [P, 3, 2])
        xn3 = sb("xn3", [P, 2, C])
        xT3 = sb("xT3", [P, 2, 2 * P])
        gT = sb("gT", [P, 2, 4 * P])
        vo = vo_place[:].rearrange("p (q j) n -> p q j n", q=2)
        nmax = sb("nmax", [P, 4, 2])
        rsum = sb("rsum", [P, 4, 2])
        rinv = sb("rinv", [P, 4, 2])
        pr_flat = pr_place[:].rearrange("p k n -> p (k n)")
        pr = pr_flat[:, 0:12 * P].rearrange("p (k n) -> p k n", k=4)
        prT = pr_flat[:, 12 * P:18 * P].rearrange("p (k n) -> p k n", k=2)

        w1s = pa[:, 0:64].rearrange("p j e -> p (j e)").rearrange("p (x f) -> p x f", x=E1)
        w2s = pa[:, 64:128].rearrange("p j e -> p (j e)").rearrange("p (x k m) -> p x (k m)", x=E1, k=2)
        gw = sb("gw", [P, E1])
        gb = sb("gb", [P, E1])
        b1n = sb("b1n", [E1, F1])
        b1T = sb("b1T", [P, 2, E1])
        which = sb("which", [P, E1])
        beforeb = sb("beforeb", [P, P], BF16)
        onesb = sb("onesb", [P, P], BF16)
        xr4 = kb[:, 0:8 * XW].rearrange("p (k j c) -> p k j c", k=2, j=TG)
        xT4 = kb[:, 1040:1552]
        st4 = sb("st4", [P, TG, 6])
        mv4 = sb("mv4", [P, TG, 2])
        r4 = sb("r4", [P, 3, TG])
        lg4 = sb("lg4", [P, TG, E1])
        top = sb("top", [P, TG, 8])
        topi = sb("topi", [P, TG, 8], U32)
        topf = sb("topf", [P, TG, 2])
        gap = sb("gap", [P, TG])
        tw = sb("tw", [P, 2, TG])
        hit = sb("hit", [P, 2, TG, E1])
        mask = sb("mask", [P, TG, E1], BF16)
        row0 = sb("row0", [P, E1], I32)
        desti = sb("desti", [P, 2, TG], I32)
        dest = sb("dest", [P, 2, TG])
        nextrow = sb("nextrow", [P, E1])
        rk = sb("rk", [P, TG, E1])
        posm = sb("posm", [P, 2, TG, E1])
        posf = sb("posf", [P, 2, TG])
        pos = sb("pos", [P, 2, TG], U32)
        padrow = sb("padrow", [P, XW])
        ends = sb("ends", [1, E1], U32)
        ui = sb("ui", [1, NUN], I32)
        uf = sb("uf", [1, NUN])
        row0f = sb("row0f", [P, E1])
        nun = sb("nun", [1, E1])
        nuni = sb("nuni", [1, E1], U32)
        cun = sb("cun", [1, E1])
        past = sb("past", [1, NUN, E1])
        ux = sb("ux", [1, NUN])
        ur = sb("ur", [1, NUN])
        unit_x = sb("unit_x", [1, NUN], U32)
        unit_r = sb("unit_r", [1, NUN], U32)
        xTu = kb[:, 2592:3104].rearrange("p (u t) -> p u t", u=2)
        pcf = pc[:].rearrange("p e t -> p (e t)")
        hTu = pcf[:, 0:1024].rearrange("p (u k t) -> p u k t", u=2, k=2)
        tu = pcf[:, 1024:1536].rearrange("p (u j c) -> p u j c", u=2, j=2)
        w1u = pcf[:, 2048:2560].rearrange("p (u f) -> p u f", u=2)
        w2u = pcf[:, 2560:3072].rearrange("p (u f) -> p u f", u=2)
        b2s = pcf[:, 3072:4096].rearrange("p (x c) -> p x c", x=E1)
        vof = vo_place[:].rearrange("p k n -> p (k n)")
        xu = vof[:, 0:2 * XR * XW].rearrange("p (u j c) -> p u j c", u=XR, j=2)
        yu = vof[:, 2 * XR * XW:2 * XR * XW + 2 * YR * C].rearrange("p (u j c) -> p u j c", u=YR, j=2)
        zx = vof[:, 0:2048].rearrange("p (q j c) -> p q j c", q=2, j=TG)
        h3x = vof[:, 2048:3072].rearrange("p (q j c) -> p q j c", q=2, j=TG)
        res = vof[:, 3072:4096].rearrange("p (q j c) -> p q j c", q=2, j=TG)

        with ExitStack() as early:
            def sbe(name, shape):
                return early.enter_context(nc.sbuf_tensor(name, shape, F32))
            wqn = sbe("wqn", [P, H1 * C])
            wkn = sbe("wkn", [P, H1 * C])
            wvn = sbe("wvn", [P, H1 * C])
            won = sbe("won", [P, H1, C])
        wqk_part = [sb(f"wqk_part{k}", [P, H1, C], F32R) for k in range(2)]
        wvo_part = [sb(f"wvo_part{k}", [P, H1, C], F32R) for k in range(2)]
        x_part = [sb(f"x_part{k}", [P, 2, 2 * P], F32R) for k in range(2)]

        w_in = sem("w_in")
        consts = sem("consts")
        prep_t = sem("prep_t")
        prep_c = sem("prep_c")
        ids_ready = sem("ids_ready")
        idst_ready = sem("idst_ready")
        gathered = [[sem(f"gathered{w}{p}") for p in range(2)] for w in range(2)]
        root_ready = sem("root_ready")
        xb_ready = sem("xb_ready")
        xn_ready = sem("xn_ready")
        xT_mm = sem("xT_mm")
        xT_ready = sem("xT_ready")
        kv_mm = sem("kv_mm")
        kv_ready = sem("kv_ready")
        q_mm = sem("q_mm")
        q_ready = sem("q_ready")
        kvs_mm = sem("kvs_mm")
        md_ready = sem("md_ready")
        o_mm = sem("o_mm")
        o_ready = sem("o_ready")
        oT_mm = sem("oT_mm")
        oT_ready = sem("oT_ready")
        y_mm = sem("y_mm")
        h1_ready = sem("h1_ready")
        x2_ready = sem("x2_ready")
        x2T_mm = sem("x2T_mm")
        x2T_ready = sem("x2T_ready")
        lg_mm = sem("lg_mm")
        lg_sub = sem("lg_sub")
        lg_exp = sem("lg_exp")
        p_ready = sem("p_ready")
        pa_ready = sem("pa_ready")
        pT_mm = sem("pT_mm")
        pT_ready = sem("pT_ready")
        stored = [sem(f"stored{p}") for p in range(2)]
        stored_x = [sem(f"stored_x{p}") for p in range(2)]
        dve_step = sem("dve_step")

        consts2 = sem("consts2")
        lanes_s = sem("lanes_s")
        pcT_mm = sem("pcT_mm")
        pc_ready = sem("pc_ready")
        bup_mm = sem("bup_mm")
        bup_ready = sem("bup_ready")
        cnt_ready = sem("cnt_ready")
        cnt_mm = sem("cnt_mm")
        find_step = sem("find_step")
        diag_ready = sem("diag_ready")
        tq_mm = sem("tq_mm")
        tq_ready = sem("tq_ready")
        cum_ready = sem("cum_ready")
        base_mm = sem("base_mm")
        sel_step = sem("sel_step")
        oneh_ready = sem("oneh_ready")
        tab_mm = sem("tab_mm")
        idx_ready = sem("idx_ready")
        xe_in = [sem(f"xe_in{p}") for p in range(2)]
        xeT_mm = sem("xeT_mm")
        xeT_ready = sem("xeT_ready")
        wup_in = [sem(f"wup_in{p}") for p in range(2)]
        wdn_in = [sem(f"wdn_in{p}") for p in range(2)]
        up_mm = sem("up_mm")
        ac_ready = sem("ac_ready")
        dn_mm = sem("dn_mm")
        ye_ready = sem("ye_ready")
        added = [sem(f"added{p}") for p in range(2)]

        w_c = sem("w_c")
        wT_mm = sem("wT_mm")
        wT_ready = sem("wT_ready")
        fold_mm = sem("fold_mm")
        fold_ready = sem("fold_ready")
        h2_in = [sem(f"h2_in{p}") for p in range(2)]
        hb_ready = sem("hb_ready")
        prep_step = sem("prep_step")
        xn3_ready = sem("xn3_ready")
        xT3_mm = sem("xT3_mm")
        xT3_ready = sem("xT3_ready")
        part_ready = sem("part_ready")
        parts_split = sem("parts_split")
        g_mm = sem("g_mm")
        g_ready = sem("g_ready")
        vo_mm = sem("vo_mm")
        vo_ready = sem("vo_ready")
        s_mm = sem("s_mm")
        max_ready = sem("max_ready")
        exp_ready = sem("exp_ready")
        rinv_ready = sem("rinv_ready")
        pr_ready = sem("pr_ready")
        prT_mm = sem("prT_mm")
        prT_ready = sem("prT_ready")
        head_mm = sem("head_mm")
        h3_ready = sem("h3_ready")
        h3_out = [sem(f"h3_out{p}") for p in range(2)]

        NB = NTOK // (2 * P)
        GBANK, VBANK, SBANK, TBANK, OBANK = 0, 2, (3, 4), (5, 6), (1, 7)
        S_LAG, N_LAG, T_LAG, O_LAG = 1, 2, 3, 4

        def there(u, count=NB * H1):
            return not isinstance(u, int) or 0 <= u < count

        consts4 = sem("consts4")
        w_d2 = sem("w_d2")
        b1_mm = sem("b1_mm")
        b1_ready = sem("b1_ready")
        d_step = sem("d_step")
        xn4_ready = sem("xn4_ready")
        xT4_mm = sem("xT4_mm")
        xT4_ready = sem("xT4_ready")
        gate_mm = sem("gate_mm")
        lg4_ready = sem("lg4_ready")
        gap_ready = sem("gap_ready")
        gap_exp = sem("gap_exp")
        mask_ready = sem("mask_ready")
        rank_mm = sem("rank_mm")
        rank_read = sem("rank_read")
        twice = sem("twice")
        pos_ready = sem("pos_ready")
        spread = sem("spread")
        padded = sem("padded")
        table_step = sem("table_step")
        table_ready = sem("table_ready")
        xu_in = [sem(f"xu_in{q}") for q in range(XR)]
        xTu_mm = sem("xTu_mm")
        xTu_ready = sem("xTu_ready")
        w1u_ready = sem("w1u_ready")
        w2u_ready = sem("w2u_ready")
        upu_mm = sem("upu_mm")
        hTu_ready = sem("hTu_ready")
        dnu_mm = sem("dnu_mm")
        tu_ready = sem("tu_ready")
        yu_ready = sem("yu_ready")
        z_out = [sem(f"z_out{q}") for q in range(XR)]
        z_in = [sem(f"z_in{p}") for p in range(2)]
        res_step = sem("res_step")
        res_ready = sem("res_ready")
        out_done = [sem(f"out_done{p}") for p in range(2)]

        NU = E0 // 4
        NP = NG // 2

        HIGH = 14
        COUNTS = HIGH + 1 + 16 + 1

        def rounds(eng, one):
            for w in range(2):
                one(0, w)
            with eng.Fori(1, NP // 2 - 1) as v:
                for w in range(2):
                    one(v, w)
            for w in range(2):
                one(NP // 2 - 1, w)

        def within(i):
            return not isinstance(i, int) or 0 <= i < NP
        block = ctx.enter_context(nc.Block())

        @block.sync
        def _(sp):
            sp.dma_start(idrow[:], x.rearrange("b (t p) -> (b t) p", p=P)).then_inc(w_in, 16)
            sp.dma_start(wqkv_n[:], L0_attn_Wqkv.rearrange("(k p) c -> p k c", p=P)).then_inc(w_in, 16)
            sp.dma_start(wproj_n[:], L0_attn_Wproj).then_inc(w_in, 16)
            sp.dma_start(bproj[:], L0_attn_bproj.partition_broadcast(P)).then_inc(w_in, 16)
            sp.dma_start(wrout[:], L0_ffn_W_router).then_inc(w_in, 16)
            sp.dma_start(brout[:], L0_ffn_b_router.partition_broadcast(P)).then_inc(w_in, 16)
            sp.dma_start(temp[:], L0_attn_temperature.rearrange("h a b -> h (a b)")).then_inc(w_in, 16)

            sp.dma_start(wqn[:], L1_attn_Wq).then_inc(w_c, 16)
            sp.dma_start(wkn[:], L1_attn_Wk).then_inc(w_c, 16)
            sp.dma_start(wvn[:], L1_attn_Wv).then_inc(w_c, 16)
            sp.dma_start(won[:], L1_attn_Wo.rearrange("(h e) m -> e h m", h=H1)).then_inc(w_c, 16)
            sp.dma_start(bo[:], L1_attn_bo.partition_broadcast(P)).then_inc(w_c, 16)

            sp.dma_start(gw[:], L1_ffn_gate_w).then_inc(w_c, 16)
            sp.dma_start(gb[:], L1_ffn_gate_b.partition_broadcast(P)).then_inc(w_c, 16)
            sp.dma_start(b1n[:], L1_ffn_b1).then_inc(w_c, 16)
            sp.dma_start(bup_n[:], L0_ffn_b_up).then_inc(w_c, 16)

            def store_rows(g, p):
                sp.wait_ge(p_ready, g + 1)
                sp.dma_start(xrow_g[bass.ds(g, 1)].rearrange("a p j c -> (a p) j c"), xr[:, p]).then_inc(stored_x[p], 16)

            def one(v, w):
                i = 2 * v + w
                if within(i - 1):
                    for p in range(2):
                        store_rows(2 * (i - 1) + p, p)
                for p in range(2):
                    g = 2 * i + p
                    sp.wait_ge(h1_ready, g + 1)
                    sp.dma_start(hbuf_g[bass.ds(g, 1)].rearrange("a p j c -> (a p) j c"), h1[:, p]).then_inc(stored[p], 16)
            rounds(sp, one)
            for p in range(2):
                store_rows(NG - 2 + p, p)
            for p in range(2):
                sp.wait_ge(stored[p], 16 * NP)
                sp.wait_ge(stored_x[p], 16 * NP)

            def load_up(u, p):
                sp.dma_start(wup[:, p], L0_ffn_W_up[bass.ds(u, 1)].rearrange("a h f -> (a h) f")).then_inc(wup_in[p], 16)

            def load_down(e, p):
                w = L0_ffn_W_down[bass.ds(e, 1)].rearrange("a f h -> (a f) h")
                sp.dma_start(wdn[:, p, 0:2], w[0:2 * P].rearrange("(k p) h -> p k h", p=P)).then_inc(wdn_in[p], 16)
                sp.dma_start(wdn[0:FCH[2], p, 2], w[2 * P:FF]).then_inc(wdn_in[p], 16)
                sp.dma_start(wdn[FCH[2]:FCH[2] + 1, p, 2], L0_ffn_b_down[bass.ds(e, 1)]).then_inc(wdn_in[p], 16)

            for e in range(2):
                load_up(0, e)
                load_down(e, e)

            def reload(v, last):
                for q in range(2 if last else 4):
                    e, p = 4 * v + q, q % 2
                    sp.wait_ge(dn_mm, e + 1)
                    load_up(v + q // 2, p)
                    load_down(e + 2, p)
            with sp.Fori(0, NU - 1) as v:
                reload(v, False)
            reload(NU - 1, True)

            def load_h2(n, p):
                sp.dma_start(hx[:, p], hbuf_b[bass.ds(n, 1)].rearrange("a p j c -> (a p) j c")).then_inc(h2_in[p], 16)

            for p in range(2):
                sp.wait_ge(added[p], 64 * (E0 // 2))
            for p in range(2):
                load_h2(p, p)

            sp.dma_start(w1s, L1_ffn_w1.rearrange("x h f -> h x f")).then_inc(w_d2, 16)
            sp.dma_start(w2s.rearrange("p x (k m) -> p x k m", k=2), L1_ffn_w2.rearrange("x (k p) m -> p x k m", p=P)).then_inc(w_d2, 16)
            sp.dma_start(b2s, L1_ffn_b2.partition_broadcast(P)).then_inc(w_d2, 16)
            sp.wait_ge(consts4, 13)
            sp.dma_start(spread_rows[E1 * REG:E1 * REG + 8 * UT].rearrange("(j p) c -> p j c", p=P),
                         padrow[:].unsqueeze(1).to_broadcast([P, 16, XW])).then_inc(w_d2, 16)

            def pass_h(i, last):
                for p in range(2):
                    n = 2 * i + p
                    if not last:
                        sp.wait_ge(hb_ready, n + 1)
                        sp.wait_ge(xn3_ready, n + 1)
                        load_h2(n + 2, p)
                    sp.wait_ge(h3_ready, n + 1)
                    sp.dma_start(h3buf_b[bass.ds(n, 1)].rearrange("a p j c -> (a p) j c"), h3[:, p]).then_inc(h3_out[p], 16)
            with sp.Fori(0, NB // 2 - 1) as i:
                pass_h(i, False)
            pass_h(NB // 2 - 1, True)
            for p in range(2):
                sp.wait_ge(h3_out[p], 16 * (NB // 2))

            sp.wait_ge(spread, 128 * NG)
            sp.wait_ge(table_step, 1)
            for e in range(E1):
                end = sp.value_load(ends[0:1, e:e + 1], min_val=0, max_val=(E1 - 1) * REG + NTOK)
                sp.dma_start(spread_rows[bass.ds(end, UT)].rearrange("(j p) c -> p j c", p=P),
                             padrow[:].unsqueeze(1).to_broadcast([P, 2, XW])).then_inc(padded, 16)
            sp.wait_ge(padded, 16 * E1)
            sp.wait_ge(w_d2, 64)
            sp.wait_ge(table_ready, 1)

            def load_unit(u, q):
                r = sp.value_load(unit_r[0:1, bass.ds(u, 1)], min_val=0, max_val=E1 * REG + (XR - 1) * UT)
                sp.dma_start(xu[:, q], spread_rows[bass.ds(r, UT)].rearrange("(j p) c -> p j c", p=P)).then_inc(xu_in[q], 16)

            for q in range(XR):
                load_unit(q, q)

            def units(v):
                for q in range(XR):
                    sp.wait_ge(z_out[q], 32 * (v + 1))
                    load_unit(XR * v + q + XR, q)
            with sp.Fori(0, NUN // XR - 1) as v:
                units(v)
            for q in range(XR):
                sp.wait_ge(z_out[q], 32 * (NUN // XR))

            def load_z(g, p):
                sp.dma_start(zx[:, p], zbuf_g[bass.ds(g, 1)].rearrange("a p j c -> (a p) j c")).then_inc(z_in[p], 16)
                sp.dma_start(h3x[:, p], h3buf_g[bass.ds(g, 1)].rearrange("a p j c -> (a p) j c")).then_inc(z_in[p], 16)

            for p in range(2):
                load_z(p, p)

            def results(i, last):
                for p in range(2):
                    g = 2 * i + p
                    sp.wait_ge(res_ready, g + 1)
                    sp.dma_start(out_g[bass.ds(g, 1)].rearrange("a p j c -> (a p) j c"), res[:, p]).then_inc(out_done[p], 16)
                    if not last:
                        load_z(g + 2, p)
            with sp.Fori(0, NG // 2 - 1) as i:
                results(i, False)
            results(NG // 2 - 1, True)
            for p in range(2):
                sp.wait_ge(out_done[p], 16 * (NG // 2))

        @block.gpsimd
        def _(pool):
            pool.memset(ident[:], 0.0).then_inc(consts, 1)
            pool.memset(ones[:], 1.0).then_inc(consts, 1)
            pool.memset(head[:], 1.0).then_inc(consts, 1)
            pool.memset(vv[:, :, :, C:C + 1], 1.0).then_inc(consts, 1)
            pool.wait_ge(consts, 4)
            pool.affine_select(out=ident[:], in_=ident[:], compare_op=ALU.not_equal, fill=1.0, base=0,
                               pattern=[[-1, P]], channel_multiplier=1).then_inc(consts, 1)
            pool.affine_select(out=head[:], in_=head[:], compare_op=ALU.is_ge, fill=0.0, base=0,
                               pattern=[[1, P]], channel_multiplier=-D0).then_inc(consts, 1)
            pool.wait_ge(consts, 6)
            pool.affine_select(out=head[:], in_=head[:], compare_op=ALU.is_ge, fill=0.0, base=D0 - 1,
                               pattern=[[-1, P]], channel_multiplier=D0).then_inc(consts, 1)
            pool.memset(lanes[:], 0.0).then_inc(consts2, 1)
            pool.memset(before[:], 1.0).then_inc(consts2, 1)
            pool.memset(ac[:], 1.0).then_inc(consts2, 1)
            pool.iota(junkf[:], pattern=[[1, CAP]], base=0, channel_multiplier=0).then_inc(consts2, 1)
            pool.iota(slotf[:], pattern=[[P, TG]], base=0, channel_multiplier=1).then_inc(consts2, 1)
            pool.iota(tilef[:], pattern=[[0, 1]], base=0, channel_multiplier=P).then_inc(consts2, 1)
            pool.wait_ge(consts2, 6)
            pool.affine_select(out=before[:], in_=before[:], compare_op=ALU.is_gt, fill=0.0, base=0,
                               pattern=[[1, P]], channel_multiplier=-1).then_inc(consts2, 1)
            pool.tensor_copy(slot16[:], junkf[:]).then_inc(consts2, 1)
            pool.tensor_copy(slotc[:], slotf[:]).then_inc(consts2, 1)
            pool.tensor_copy(tab[:, P:P + 1], tilef[:]).then_inc(consts2, 1)
            for k in range(4):
                v = lanes[:].rearrange("p (b m) -> p b m", b=4)
                pool.affine_select(out=v, in_=v, compare_op=ALU.not_equal, fill=1.0, base=-E0 * k,
                                   pattern=[[0, 4], [-1, E0]], channel_multiplier=1).then_inc(lanes_s, 1)
                pool.wait_ge(lanes_s, k + 1)
            pool.iota(whichi[:], pattern=[[1, E1]], base=0, channel_multiplier=0).then_inc(consts4, 1)
            pool.iota(row0[:], pattern=[[REG, E1]], base=0, channel_multiplier=0).then_inc(consts4, 1)
            pool.iota(desti[:], pattern=[[1, 2], [2 * P, TG]], base=0, channel_multiplier=2).then_inc(consts4, 1)
            pool.iota(ui[:], pattern=[[1, NUN]], base=0, channel_multiplier=0).then_inc(consts4, 1)
            pool.memset(padrow[:, 0:C + 1], 0.0).then_inc(consts4, 1)
            pool.memset(padrow[:, C + 1:XW].bitcast(U32), NOWHERE).then_inc(consts4, 1)
            pool.wait_ge(consts4, 6)
            pool.tensor_copy(which[:], whichi[:]).then_inc(consts4, 1)
            pool.tensor_copy(nextrow[:], row0[:]).then_inc(consts4, 1)
            pool.tensor_copy(row0f[:], row0[:]).then_inc(consts4, 1)
            pool.tensor_copy(dest[:], desti[:]).then_inc(consts4, 1)
            pool.tensor_copy(uf[:], ui[:]).then_inc(consts4, 1)
            pool.tensor_copy(onesb[:], ones[:]).then_inc(consts4, 1)
            pool.tensor_copy(beforeb[:], before[:]).then_inc(consts4, 1)
            pool.memset(causal[:], 0.0).then_inc(consts4, 1)
            pool.tensor_copy(identb[:], ident[:]).then_inc(consts4, 1)
            pool.wait_ge(consts4, 15)
            pool.affine_select(out=causal[:], in_=causal[:], compare_op=ALU.is_ge, fill=-BIG, base=0,
                               pattern=[[-1, P]], channel_multiplier=1).then_inc(consts4, 1)
            pool.wait_ge(ids_ready, 1)

            def gather(g, w, p):
                q = 2 * w + p
                pool.tensor_copy(idst[:, q], ids[:, bass.ds(TG * g, TG)]).then_inc(idst_ready, 1)
                pool.wait_ge(idst_ready, g + 1)
                pool.nop(nofuse=True)
                for j in range(TG):
                    pool.indirect_dma_start(out=xg[:, q, j], out_offset=None, in_=L0_tok_weight,
                                            in_offset=bass.IndirectOffsetOnAxis(ap=idst[:, q, j:j + 1], axis=0))\
                        .then_inc(gathered[w][p], 16)

            def add_bias(g, w, p, guard):
                pool.wait_ge(gathered[w][p], guard)
                if not isinstance(g, int) or g >= 4:
                    pool.wait_ge(h1_ready, g - 3)
                pool.tensor_tensor(xb[:, 2 * w + p], xg[:, 2 * w + p], bproj[:].unsqueeze(1).to_broadcast([P, TG, C]), ALU.add)\
                    .then_inc(xb_ready, 1)

            def keep_probs(g, p):
                pool.wait_ge(p_ready, g + 1)
                pool.nop(nofuse=True)
                pool.tensor_copy(pa[:, bass.ds(g * TG, TG)], pg[:, p]).then_inc(pa_ready, 1)

            for w in range(2):
                for p in range(2):
                    gather(2 * w + p, w, p)
            for p in range(2):
                add_bias(p, 0, p, 64)

            def one(v, w):
                i = 2 * v + w
                if within(i + 2):
                    for p in range(2):
                        pool.wait_ge(xn_ready, 2 * i + p + 1)
                        pool.wait_ge(xb_ready, 2 * i + p + 1)
                        gather(2 * (i + 2) + p, w, p)
                if within(i + 1):
                    for p in range(2):
                        add_bias(2 * (i + 1) + p, 1 - w, p, 64 * (v + w + 1))
                if within(i - 1):
                    for p in range(2):
                        keep_probs(2 * (i - 1) + p, p)
            rounds(pool, one)
            for p in range(2):
                keep_probs(NG - 2 + p, p)

            def take(e, q):
                p = q % 2
                pool.wait_ge(idx_ready, e + 1)
                pool.nop(nofuse=True)
                for c in range(TG):
                    pool.indirect_dma_start(out=xe[:, p, c], out_offset=None, in_=xrow,
                                            in_offset=bass.IndirectOffsetOnAxis(ap=idx[:, q, c:c + 1], axis=0))\
                        .then_inc(xe_in[p], 16)

            def give(e, p, q):
                pool.wait_ge(ye_ready, e + 1)
                pool.nop(nofuse=True)
                for c in range(TG):
                    pool.indirect_dma_start(out=hbuf, out_offset=bass.IndirectOffsetOnAxis(ap=idx[:, q, c:c + 1], axis=0),
                                            in_=ye[:, p, c], in_offset=None, compute_op=ALU.add).then_inc(added[p], 16)

            for p in range(2):
                pool.wait_ge(stored[p], 16 * NP)
                pool.wait_ge(stored_x[p], 16 * NP)
            take(0, 0)
            take(1, 1)

            def serve(v, last):
                for q in range(4):
                    e, p = 4 * v + q, q % 2
                    if not (last and q >= 2):
                        take(e + 2, (q + 2) % 4)
                    if not (first(v) and q == 0):
                        n = 2 * v + (q + 1) // 2 if q % 2 else 2 * v + q // 2
                        pool.wait_ge(added[1 - p], 64 * n)
                    give(e, p, q)
            serve(0, False)
            with pool.Fori(1, NU - 1) as v:
                serve(v, False)
            serve(NU - 1, True)
            for p in range(2):
                pool.wait_ge(added[p], 64 * (E0 // 2))

            pool.wait_ge(w_c, 16 * 9)

            def scatter(g):
                pool.wait_ge(xn4_ready, g + 1)
                pool.nop(nofuse=True)
                pool.tensor_copy(xr4[:, 1, :, 0:C], xr4[:, 0, :, 0:C]).then_inc(twice, 1)
                pool.wait_ge(twice, g + 1)
                pool.wait_ge(pos_ready, g + 1)
                pool.nop(nofuse=True)
                for k in range(2):
                    for j in range(TG):
                        pool.indirect_dma_start(out=spread_rows, out_offset=bass.IndirectOffsetOnAxis(ap=pos[:, k, j:j + 1], axis=0),
                                                in_=xr4[:, k, j], in_offset=None).then_inc(spread, 16)

            def residual(i):
                for p in range(2):
                    n = 2 * i + p
                    pool.wait_ge(h2_in[p], 16 * (i + 1))
                    if not first(i):
                        pool.wait_ge(h3_ready, n - 1)
                    pool.tensor_tensor(hb[:, p], hx[:, p], bo[:].unsqueeze(1).to_broadcast([P, 2, C]), ALU.add)\
                        .then_inc(hb_ready, 1)
                if not first(i):
                    scatter(i - 1)
            residual(0)
            with pool.Fori(1, NB // 2) as i:
                residual(i)
            scatter(NG - 1)

            def give_unit(u, q, v):
                pool.wait_ge(yu_ready, u + 1)
                pool.nop(nofuse=True)
                for j in range(2):
                    pool.indirect_dma_start(out=zbuf, out_offset=bass.IndirectOffsetOnAxis(
                        ap=xu[:, q, j, C + 1:XW].bitcast(U32), axis=0), in_=yu[:, q % YR, j], in_offset=None,
                        bounds_check=2 * NTOK - 1, oob_is_err=False).then_inc(z_out[q], 16)
            with pool.Fori(0, NUN // XR) as v:
                for q in range(XR):
                    give_unit(XR * v + q, q, v)
            for q in range(XR):
                pool.wait_ge(z_out[q], 32 * (NUN // XR))

        @block.scalar
        def _(act):
            act.wait_ge(consts, 7)
            act.wait_ge(prep_t, 5)
            act.activation(ids[:], bank[0][:, 0:P], ACT.Copy).then_inc(ids_ready, 1)
            act.activation(wqkvT[:], bank[1][:, 0:3 * C], ACT.Copy).then_inc(prep_c, 1)
            act.activation(wprojT[:], bank[2][:, 0:C], ACT.Copy).then_inc(prep_c, 1)
            act.wait_ge(prep_t, 7)
            act.activation(headc[:], bank[3][:, 0:H0], ACT.Copy).then_inc(prep_c, 1)
            act.activation(mtemp[:], bank[4][:, 0:P], ACT.Copy).then_inc(prep_c, 1)

            def normalise(dst, src, a):
                for j in range(TG):
                    ins = act.activation(dst[:, j, 0:C], src[:, j], ACT.Identity, bias=nm[:, a, j:j + 1], scale=rs[:, a, j:j + 1])
                return ins

            def first_norm(g, w, p):
                if not isinstance(g, int) or g >= 2:
                    act.wait_ge(xT_mm, g - 1)
                normalise(xn[:, p], xg[:, 2 * w + p], 2 + p).then_inc(xn_ready, 1)

            def second_norm(g, p, i):
                if not isinstance(g, int) or g >= 2:
                    act.wait_ge(stored_x[p], 16 * i)
                normalise(xr[:, p], h1[:, p], p).then_inc(x2_ready, 1)

            def second_turned(g, p):
                act.wait_ge(x2T_mm, g + 1)
                act.activation(x2T[:, p], bank[4 * p + 3][:, :], ACT.Copy).then_inc(x2T_ready, 1)

            def router_exp(g, p):
                act.wait_ge(lg_sub, g + 1)
                act.activation(lg[:, p], lg[:, p], ACT.Exp).then_inc(lg_exp, 1)

            def probs_turned(g, p):
                act.wait_ge(pT_mm, g + 1)
                act.activation(kb[:, bass.ds(g * P, P)], bank[4 * p + 3][:, 0:P], ACT.Copy).then_inc(pT_ready, 1)

            def one(v, w):
                i = 2 * v + w
                g0, r0 = 2 * i, 2 * (i - 1)
                for p in range(2):
                    act.wait_ge(xT_mm, g0 + p + 1)
                    act.activation(xT[:, p], bank[4 * p][:, :], ACT.Copy).then_inc(xT_ready, 1)
                for p in range(2):
                    for m in range(2):
                        b2 = bank[4 * p + 1 + m][:, :].rearrange("p (j n) -> p j n", j=2)
                        act.wait_ge(kv_mm, 2 * (g0 + p) + m + 1)
                        act.activation(kk[:, p, 2 * m:2 * m + 2], b2[:, :, 0:C], ACT.Relu).then_inc(kv_ready, 1)
                        act.activation(vv[:, p, 2 * m:2 * m + 2, 0:C], b2[:, :, C:2 * C], ACT.Copy).then_inc(kv_ready, 1)
                if within(i - 2):
                    for p in range(2):
                        probs_turned(r0 - 2 + p, p)
                for p in range(2):
                    act.wait_ge(q_mm, g0 + p + 1)
                    act.activation(qT[:, p], bank[4 * p][:, :], ACT.Relu).then_inc(q_ready, 1)
                act.wait_ge(root_ready, i + 2)
                if within(i - 1):
                    for p in range(2):
                        second_norm(r0 + p, p, i - 1)
                if within(i + 1):
                    first_norm(g0 + 2, 1 - w, 0)
                if within(i - 1):
                    for p in range(2):
                        second_turned(r0 + p, p)
                for p in range(2):
                    act.wait_ge(oT_mm, g0 + p + 1)
                    act.activation(oT[:, p], bank[4 * p + 1][:, :], ACT.Copy).then_inc(oT_ready, 1)
                if within(i + 1):
                    first_norm(g0 + 3, 1 - w, 1)
                if within(i - 1):
                    for p in range(2):
                        router_exp(r0 + p, p)

            act.wait_ge(root_ready, 1)
            for p in range(2):
                first_norm(p, 0, p)
            rounds(act, one)
            act.wait_ge(root_ready, NP + 2)
            for p in range(2):
                probs_turned(NG - 4 + p, p)
            for step in (lambda g, p: second_norm(g, p, NP - 1), second_turned, router_exp, probs_turned):
                for p in range(2):
                    step(NG - 2 + p, p)

            for k in range(0, 8, 2):
                act.wait_ge(pcT_mm, k + 1)
                act.activation(pc[:, 4 * k:4 * k + 4], bank[k][:, :].rearrange("p (e t) -> p e t", e=4), ACT.Copy).then_inc(pc_ready, 1)
            act.wait_ge(bup_mm, 1)
            act.activation(bupT[:, 0:2], bank[1][:, 0:16].rearrange("p (k u) -> p k u", k=2), ACT.Copy).then_inc(bup_ready, 1)
            act.activation(bupT[0:FCH[2], 2], bank[1][0:FCH[2], 16:24], ACT.Copy).then_inc(bup_ready, 1)

            for h in range(H1):
                act.wait_ge(wT_mm, h + 1)
                act.activation(wT[:], bank[2][:, 0:3 * C].rearrange("p (k c) -> p k c", k=3), ACT.Copy).then_inc(wT_ready, 1)
                act.wait_ge(fold_mm, h + 1)
                act.activation(wqk[:, h], bank[3][:, 0:C], ACT.Copy, scale=float(C) ** -0.5).then_inc(fold_ready, 1)
                act.activation(wvo[:, h], bank[3][:, C:2 * C], ACT.Copy).then_inc(fold_ready, 1)

            act.wait_ge(b1_mm, 1)
            act.activation(b1T[:], bank[2][:, 0:2 * E1].rearrange("p (k x) -> p k x", k=2), ACT.Copy).then_inc(b1_ready, 1)
            act.wait_ge(bup_ready, 2)
            act.wait_ge(consts2, 10)

            def rows_turned(e):
                act.wait_ge(xeT_mm, e + 1)
                act.activation(xeT[:], bank[0][:, :], ACT.Copy).then_inc(xeT_ready, 1)

            def hidden(v, last):
                if not first(v):
                    act.wait_ge(ac_ready, 12 * v)
                act.activation(bupg[:, 0:2], bupT[:, 0:2, bass.ds(v, 1)].rearrange("p k a -> p (k a)"), ACT.Copy).then_inc(bup_ready, 1)
                act.activation(bupg[0:FCH[2], 2:3], bupT[0:FCH[2], 2, bass.ds(v, 1)], ACT.Copy).then_inc(bup_ready, 1)
                act.wait_ge(bup_ready, 4 + 2 * v)
                for q in range(4):
                    e = 4 * v + q
                    for k in range(3):
                        act.wait_ge(up_mm, 3 * e + k + 1)
                        act.activation(ac[0:FCH[k], k], bank[1 + k][0:FCH[k], :], ACT.Silu, bias=bupg[0:FCH[k], k:k + 1])\
                            .then_inc(ac_ready, 1)
                    if not (last and q == 3):
                        rows_turned(e + 1)
            rows_turned(0)
            hidden(0, False)
            with act.Fori(1, NU - 1) as v:
                hidden(v, False)
            hidden(NU - 1, True)

            def turned(n, p):
                act.wait_ge(xT3_mm, n + 1)
                act.activation(xT3[:, p], bank[VBANK][:, 0:2 * P], ACT.Copy)
                act.activation(x_part[0][:, p], bank[VBANK][:, 0:2 * P], ACT.Copy).then_inc(xT3_ready, 1)

            def exps(u, h):
                act.wait_ge(max_ready, u + 1)
                if not isinstance(u, int) or u >= 4:
                    act.wait_ge(prT_mm, u - 3)
                s2 = bank[SBANK[h % 2]]
                act.activation(pr[:, h % 4, 0:P], s2[:, 0:P], ACT.Exp, bias=nmax[:, h % 4, 0:1],
                               accum_out=rsum[:, h % 4, 0:1])
                act.activation(pr[:, h % 4, P:3 * P], s2[:, P:3 * P], ACT.Exp, bias=nmax[:, h % 4, 1:2],
                               accum_out=rsum[:, h % 4, 1:2]).then_inc(exp_ready, 1)

            act.wait_ge(fold_ready, 2 * H1)
            act.activation(wqk_part[0][:], wqk[:], ACT.Copy).then_inc(part_ready, 1)
            act.activation(wvo_part[0][:], wvo[:], ACT.Copy).then_inc(part_ready, 1)
            turned(0, 0)

            def gates_turned(g):
                act.wait_ge(xT4_mm, g + 1)
                act.activation(xT4, bank[GBANK][:, :], ACT.Copy).then_inc(xT4_ready, 1)

            def gaps(g):
                act.wait_ge(gap_ready, g + 1)
                act.activation(tw[:, 1], gap[:], ACT.Exp).then_inc(gap_exp, 1)

            def heads(i, last):
                for p in range(2):
                    n = 2 * i + p
                    for h in range(H1):
                        u = H1 * n + h
                        if (p, h) == (1, 1) and there(i - 1):
                            gates_turned(i - 1)
                        if h % 2 == 0:
                            act.wait_ge(g_mm, 4 * n + h // 2 + 1)
                            act.activation(gT[:, h // 2 % 2], bank[GBANK][:, :], ACT.Copy).then_inc(g_ready, 1)
                        if h < 4:
                            act.wait_ge(vo_mm, 4 * n + h + 1)
                            act.activation(vo[:, p, h % 2, (h // 2) * 512:(h // 2 + 1) * 512], bank[VBANK][:, :], ACT.Copy)\
                                .then_inc(vo_ready, 1)
                        if h == 5 and not (last and p == 1):
                            turned(n + 1, 1 - p)
                        if there(u - S_LAG):
                            exps(u - S_LAG, (h - S_LAG) % H1)
                        if (p, h) == (1, 5) and there(i - 1):
                            gaps(i - 1)
            heads(0, False)
            with act.Fori(1, NB // 2 - 1) as i:
                heads(i, False)
            heads(NB // 2 - 1, True)
            exps(NB * H1 - 1, H1 - 1)
            gates_turned(NG - 1)
            gaps(NG - 1)

            act.wait_ge(table_ready, 1)

            def act_turn(u, q):
                act.wait_ge(xTu_mm, u + 1)
                act.activation(xTu[:, q % 2], bank[q % 2][:, 0:UT], ACT.Copy).then_inc(xTu_ready, 1)

            def units(v, last):
                for q in range(XR):
                    u = XR * v + q
                    if not (last and q == XR - 1):
                        act_turn(u + 1, q + 1)
                    x = act.value_load(unit_x[0:1, bass.ds(u, 1)], min_val=0, max_val=E1 - 1)
                    act.wait_ge(upu_mm, u + 1)
                    if not isinstance(u, int) or u >= 2:
                        act.wait_ge(dnu_mm, u - 1)
                    for k in range(2):
                        ins = act.activation(hTu[:, q % 2, k], bank[2 + q % 2][:, k * UT:(k + 1) * UT], ACT.Relu,
                                             bias=b1T[:, k, bass.ds(x, 1)])
                    ins.then_inc(hTu_ready, 1)
            act_turn(0, 0)
            units(0, False)
            with act.Fori(1, NUN // XR - 1) as v:
                units(v, False)
            units(NUN // XR - 1, True)

        @block.vector
        def _(dve):
            dve.wait_ge(w_in, 16 * 7)
            dve.tensor_copy(idrowf[:], idrow[:]).then_inc(prep_c, 1)
            dve.wait_ge(consts, 7)
            dve.tensor_scalar(headt[:], head[:], temp[:, 0:1], None, ALU.mult).then_inc(prep_c, 1)

            def stats(src, a, steps):
                for j in range(TG):
                    steps.done(dve.bn_stats(st[:, a, j], src[:, j]))
                steps.wait()
                dve.nop(nofuse=True)
                for j in range(TG):
                    ins = dve.bn_aggr(mv[:, a, j], st[:, a, j])
                steps.done(ins)

            ROOT = 13

            def inv_sqrt(k, steps, v, y, t, h):
                if k != 3:
                    steps.wait()
                if k == 0:
                    ins = dve.tensor_scalar(h, v, EPS, None, ALU.add)
                elif k == 1:
                    ins = dve.tensor_scalar(t.bitcast(U32), h.bitcast(U32), 1, None, ALU.logical_shift_right)
                elif k == 2:
                    ins = dve.tensor_scalar(y.bitcast(I32), t.bitcast(I32), -1.0, float(0x5F3759DF), ALU.mult, ALU.add)
                elif k == 3:
                    ins = dve.tensor_scalar(h, h, -0.5, None, ALU.mult)
                elif k % 3 == 1:
                    ins = dve.tensor_tensor(t, y, y, ALU.mult)
                elif k % 3 == 2:
                    ins = dve.tensor_tensor(t, t, h, ALU.mult)
                else:
                    ins = dve.scalar_tensor_tensor(out=y, in0=t, scalar=1.5, in1=y, op0=ALU.add, op1=ALU.mult)
                steps.done(ins)

            def roots(a, b, steps, used):
                if used:
                    dve.wait_ge(xn_ready, used[0])
                    if used[1] is not None:
                        dve.wait_ge(x2_ready, used[1])
                for k in range(ROOT):
                    inv_sqrt(k, steps, mv[:, a:b, :, 1], rs[:, a:b], rt[:, a:b], lnv[:, a:b])
                steps.wait()
                dve.scalar_tensor_tensor(out=nm[:, a:b], in0=mv[:, a:b, :, 0], scalar=-1.0, in1=rs[:, a:b],
                                         op0=ALU.mult, op1=ALU.mult).then_inc(root_ready, 1)

            def first_stats(w, p, guard, steps):
                dve.wait_ge(gathered[w][p], guard)
                stats(xg[:, 2 * w + p], 2 + p, steps)

            def second_stats(g, p, steps):
                dve.wait_ge(h1_ready, g + 1)
                stats(h1[:, p], p, steps)

            def router_max(g, p, steps):
                dve.wait_ge(lg_mm, g + 1)
                steps.done(dve.tensor_tensor(lg[:, p], bank[4 * p + 3][:, 0:TG * E0].rearrange("p (j e) -> p j e", j=TG),
                                             brout[:].unsqueeze(1).to_broadcast([P, TG, E0]), ALU.add))
                steps.wait()
                steps.done(dve.tensor_reduce(mx[:, p], lg[:, p], AX.X, ALU.max))
                steps.wait()
                dve.tensor_tensor(lg[:, p], lg[:, p], mx[:, p].unsqueeze(2).to_broadcast([P, TG, E0]), ALU.subtract)\
                    .then_inc(lg_sub, 1)

            def router_probs(g, p, steps):
                dve.wait_ge(lg_exp, g + 1)
                steps.done(dve.tensor_reduce(sm[:, p], lg[:, p], AX.X, ALU.add))
                steps.wait()
                steps.done(dve.reciprocal(sm[:, p], sm[:, p]))
                steps.wait()
                if not isinstance(g, int) or g >= 2:
                    dve.wait_ge(pa_ready, g - 1)
                    dve.wait_ge(pT_mm, g - 1)
                dve.tensor_tensor(pg[:, p], lg[:, p], sm[:, p].unsqueeze(2).to_broadcast([P, TG, E0]), ALU.mult)
                dve.tensor_tensor(xr[:, p, :, C:ROW], lg[:, p], sm[:, p].unsqueeze(2).to_broadcast([P, TG, E0]), ALU.mult)\
                    .then_inc(p_ready, 1)

            LN_STEPS = 2 * (TG + 1)
            BEFORE = LN_STEPS + ROOT
            ROUND0 = LN_STEPS + ROOT + 4
            ROUND = 2 * LN_STEPS + ROOT + 4 + 8

            def one(v, w):
                i = 2 * v + w
                steps = Steps(dve, dve_step, BEFORE if first(i) else BEFORE + ROUND0 + ROUND * (i - 1))
                base = steps.n
                g0, r0 = 2 * i, 2 * (i - 1)
                rear, more = within(i - 1), within(i + 1)
                if rear:
                    for p in range(2):
                        second_stats(r0 + p, p, steps)
                if more:
                    for p in range(2):
                        first_stats(1 - w, p, 64 * (v + w + 1), steps)
                roots(0 if rear else 2, 4 if more else 2, steps, (2 * i + 2, None if isinstance(i, int) and i < 2 else 2 * i - 2))
                for p in range(2):
                    s4 = bank[4 * p + 1][:, 0:2 * (C + 1)].rearrange("p (b n) -> p b n", b=2)
                    dve.wait_ge(kvs_mm, g0 + p + 1)
                    dve.tensor_tensor(md[:, p, :, 0:C], s4[:, :, 0:C], mtemp[:].unsqueeze(1).to_broadcast([P, 2, C]), ALU.mult)
                    dve.tensor_tensor(md[:, p, :, C:C + H0], headc[:].unsqueeze(1).to_broadcast([P, 2, H0]),
                                      s4[:, :, C:C + 1].to_broadcast([P, 2, H0]), ALU.mult).then_inc(md_ready, 1)
                for p in range(2):
                    ob = [bank[4 * p + 2 * m][:, 0:2 * (C + H0)] for m in range(2)]
                    for m in range(2):
                        dve.wait_ge(o_mm, 2 * (g0 + p) + m + 1)
                        last = dve.tensor_scalar(den[:, p, 2 * m:2 * m + 2], ob[m].rearrange("p (j n) -> p j n", j=2)[:, :, C:C + H0],
                                                 100.0, None, ALU.max)
                    steps.done(last)
                    steps.wait()
                    steps.done(dve.reciprocal(den[:, p], den[:, p]))
                    steps.wait()
                    for m in range(2):
                        for j in range(2):
                            o5 = ob[m][:, j * (C + H0):j * (C + H0) + C].rearrange("p (h d) -> p h d", h=H0)
                            last = dve.tensor_tensor(oo[:, p, 2 * m + j].rearrange("p (h d) -> p h d", h=H0), o5,
                                                     den[:, p, 2 * m + j].unsqueeze(2).to_broadcast([P, H0, D0]), ALU.mult)
                    last.then_inc(o_ready, 1)
                if rear:
                    for p in range(2):
                        router_max(r0 + p, p, steps)
                for p in range(2):
                    dve.wait_ge(y_mm, g0 + p + 1)
                    dve.wait_ge(xb_ready, g0 + p + 1)
                    if rear:
                        dve.wait_ge(stored[p], 16 * i)
                        dve.wait_ge(x2_ready, r0 + p + 1)
                    dve.tensor_tensor(h1[:, p], bank[4 * p + 2][:, :].rearrange("p (j c) -> p j c", j=TG), xb[:, 2 * w + p], ALU.add)\
                        .then_inc(h1_ready, 1)
                if rear:
                    for p in range(2):
                        router_probs(r0 + p, p, steps)
                assert not (rear and more) or steps.n == ROUND

            steps = Steps(dve, dve_step)
            for p in range(2):
                first_stats(0, p, 64, steps)
            roots(2, 4, steps, None)
            assert steps.n == BEFORE
            rounds(dve, one)
            steps = Steps(dve, dve_step, BEFORE + ROUND0 + ROUND * (NP - 1) - LN_STEPS)
            for p in range(2):
                second_stats(NG - 2 + p, p, steps)
            roots(0, 2, steps, (NG, NG - 2))
            for p in range(2):
                router_max(NG - 2 + p, p, steps)
            for p in range(2):
                router_probs(NG - 2 + p, p, steps)

            for k in range(1, 8, 2):
                dve.wait_ge(pcT_mm, k + 1)
                dve.tensor_copy(pc[:, 4 * k:4 * k + 4], bank[k][:, :].rearrange("p (e t) -> p e t", e=4)).then_inc(pc_ready, 1)

            dve.wait_ge(pT_ready, NG)
            words = kb[:].bitcast(U16)
            find = Steps(dve, find_step)
            find.done(dve.tensor_copy(half16, words[:, 1::2]))
            find.done(dve.memset(need[:], float(CAP)))

            def start(bits):
                find.done(dve.memset(thr[:], 0.0))
                find.done(dve.memset(bit[:], float(1 << bits - 1)))
                find.done(dve.memset(cand[:], float(1 << bits - 1)))
                find.wait()

            def count_of(than, op, src):
                dve.tensor_scalar(junk[:], src, than, None, op, ALU.add, accum_out=cnt[:, 0:1]).then_inc(cnt_ready, 1)

            def settle(b, base):
                n = Steps(dve, find_step, base)
                count_of(cand[:, 0:1], ALU.is_ge, half16)
                n.done(dve.tensor_scalar(nextbit[:], bit[:], 0.5, None, ALU.mult))
                dve.wait_ge(cnt_mm, b + 1)
                n.done(dve.tensor_scalar(keep[:], bank[0][:, 0:1], need[:, 0:1], bit[:, 0:1], ALU.is_ge, ALU.mult))
                n.wait()
                n.done(dve.scalar_tensor_tensor(out=cand[:], in0=keep[:], scalar=nextbit[:, 0:1], in1=thr[:], op0=ALU.add, op1=ALU.add))
                n.done(dve.tensor_copy(bit[:], nextbit[:]))
                n.wait()
                n.done(dve.tensor_tensor(thr[:], thr[:], keep[:], ALU.add))
                n.wait()
                assert n.n == SETTLE

            SETTLE = 5
            start(HIGH)
            first_base = find.n
            with dve.Fori(0, HIGH) as b:
                settle(b, first_base + SETTLE * b)
            find = Steps(dve, find_step, first_base + SETTLE * HIGH)
            count_of(thr[:, 0:1], ALU.is_gt, half16)
            find.done(dve.tensor_copy(thrh[:], thr[:]))
            dve.wait_ge(cnt_mm, HIGH + 1)
            find.done(dve.tensor_scalar(need[:], bank[0][:, 0:1], -1.0, float(CAP), ALU.mult, ALU.add))
            find.done(dve.scalar_tensor_tensor(out=half16, in0=half16, scalar=thr[:, 0:1], in1=words[:, 0::2],
                                               op0=ALU.is_equal, op1=ALU.mult))
            find.wait()
            start(16)
            second_base = find.base + find.n
            with dve.Fori(HIGH + 1, HIGH + 17) as b:
                settle(b, second_base + SETTLE * (b - (HIGH + 1)))
            find = Steps(dve, find_step, second_base + SETTLE * 16)
            find.done(dve.tensor_copy(thrw[:, 0:1], thrh[:]))
            find.done(dve.tensor_copy(thrw[:, 1:2], thr[:]))
            find.wait()
            find.done(dve.tensor_scalar(thrw[:, 0:1], thrw[:, 0:1], 16, None, ALU.logical_shift_left))
            find.wait()
            find.done(dve.tensor_tensor(thrw[:, 0:1], thrw[:, 0:1], thrw[:, 1:2], ALU.bitwise_or))
            find.wait()
            count_of(thrw[:, 0:1].bitcast(F32), ALU.is_gt, kb[:])
            dve.wait_ge(cnt_mm, COUNTS)
            find.done(dve.tensor_scalar(quota[:], bank[0][:, 0:1], -1.0, float(CAP), ALU.mult, ALU.add))
            find.wait()
            dve.tensor_scalar(diag[:, 0], ident[0:E0, 0:E0], thrw[0:E0, 0:1].bitcast(F32), None, ALU.mult)
            dve.tensor_scalar(diag[:, 1], ident[0:E0, 0:E0], quota[0:E0, 0:1], None, ALU.mult).then_inc(diag_ready, 1)
            dve.wait_ge(tq_mm, 1)
            dve.tensor_copy(tq[:], bank[1][:, 0:2 * E0].rearrange("p (k e) -> p k e", k=2)).then_inc(tq_ready, 1)
            dve.wait_ge(tq_ready, 1)
            dve.wait_ge(pc_ready, 8)
            dve.wait_ge(consts2, 10)

            def rank(e, n):
                v = pc[:, bass.ds(e, 1)].rearrange("p a t -> p (a t)")
                n.done(dve.tensor_scalar(sel[:, 0], v, tq[:, 0, bass.ds(e, 1)], None, ALU.is_gt))
                n.done(dve.tensor_scalar(sel[:, 1], v, tq[:, 0, bass.ds(e, 1)], None, ALU.is_equal))
                n.wait()
                dve.tensor_tensor_scan(cum[:, 0], ones[:], sel[:, 0], 0.0, ALU.mult, ALU.add)
                dve.tensor_tensor_scan(cum[:, 1], ones[:], sel[:, 1], 0.0, ALU.mult, ALU.add).then_inc(cum_ready, 1)

            def place(e, n):
                dve.wait_ge(base_mm, e + 1)
                n.done(dve.tensor_copy(base[:], bank[7][:, 0:2]))
                n.wait()
                q = tq[:, 1, bass.ds(e, 1)]
                n.done(dve.tensor_scalar(edge[:, 0:1], base[:, 1:2], q, base[:, 0:1], ALU.min, ALU.add))
                n.done(dve.tensor_scalar(sel[:, 1], cum[:, 1], base[:, 1:2], q, ALU.add, ALU.min))
                n.wait()
                n.done(dve.scalar_tensor_tensor(out=tab[:, 0:P], in0=cum[:, 0], scalar=base[:, 0:1], in1=sel[:, 1],
                                                op0=ALU.add, op1=ALU.add))
                n.done(dve.tensor_scalar(from0[:], slot16[:], edge[:, 0:1], None, ALU.is_ge))
                n.wait()
                n.done(dve.tensor_copy(edge[:, 1:2], tab[:, P - 1:P]))
                n.wait()
                dve.scalar_tensor_tensor(out=oneh[:], in0=slot16[:], scalar=edge[:, 1:2], in1=from0[:],
                                         op0=ALU.is_lt, op1=ALU.mult).then_inc(oneh_ready, 1)

            def number(e, q, n, guard):
                dve.wait_ge(tab_mm, e + 1)
                n.done(dve.tensor_copy(tbase[:].rearrange("p (k c) -> p k c", k=2)[:, 0], bank[5][:, 0:2 * (P + 1)].rearrange("p (c t) -> p c t", c=2)[:, :, P]))
                n.done(dve.tensor_copy(tbase[:].rearrange("p (k c) -> p k c", k=2)[:, 1], bank[6][:, 0:2 * (P + 1)].rearrange("p (c t) -> p c t", c=2)[:, :, P]))
                n.wait()
                for c in range(TG):
                    row = bank[5 + c // 2][:, (c % 2) * (P + 1):(c % 2) * (P + 1) + P]
                    ins = dve.tensor_scalar(junk[:, c * P:(c + 1) * P], row, slotc[:, c:c + 1], tbase[:, c:c + 1], ALU.is_le, ALU.add,
                                            accum_out=cnt4[:, c:c + 1])
                    if c == TG - 1:
                        n.done(ins)
                n.wait()
                if guard is not None:
                    dve.wait_ge(added[q % 2], guard)
                dve.tensor_copy(idx[:, q], cnt4[:]).then_inc(idx_ready, 1)

            def gates(e, p, n, guard):
                dve.wait_ge(xe_in[p], guard)
                if not isinstance(e, int) or e >= 2:
                    dve.wait_ge(ye_ready, e - 1)
                n.done(dve.tensor_copy(gate[:, p], xe[:, p, :, bass.ds(C + e, 1)].rearrange("p c a -> p (c a)")))
                n.wait()

            def weigh(e, p):
                dve.wait_ge(dn_mm, e + 1)
                dve.tensor_tensor(ye[:, p], bank[4][:, :].rearrange("p (c h) -> p c h", c=TG),
                                  gate[:, p].unsqueeze(2).to_broadcast([P, TG, C]), ALU.mult).then_inc(ye_ready, 1)

            PER = 12
            n = Steps(dve, sel_step)
            for e in range(3):
                rank(e, n)
                place(e, n)
                if e < 2:
                    number(e, e, n, None)
            gates(0, 0, n, 64)
            pre = n.n

            def serve(v, last):
                n = Steps(dve, sel_step, pre + 4 * PER * v)
                for q in range(4):
                    e, p = 4 * v + q, q % 2
                    if not (last and q >= 2):
                        number(e + 2, (q + 2) % 4, n, None if first(v) and q < 2 else 64 * (2 * v + q // 2))
                    else:
                        dve.wait_ge(added[p], 64 * (2 * v + q // 2))
                    if not (last and q >= 1):
                        rank(e + 3, n)
                        place(e + 3, n)
                    if not (last and q == 3):
                        gates(e + 1, 1 - p, n, 64 * (2 * v + (q + 1) // 2 + 1))
                    weigh(e, p)
                return n.n
            assert serve(0, False) == 4 * PER
            with dve.Fori(1, NU - 1) as v:
                serve(v, False)
            serve(NU - 1, True)

            PREP = 2 + 1 + 13

            prep_now = {}

            def prep_stats(n, p, i):
                n_ = prep_now["steps"] = Steps(dve, prep_step, PREP * n)
                dve.wait_ge(h2_in[p], 16 * (i + 1))
                for j in range(2):
                    n_.done(dve.bn_stats(st3[:, j], hx[:, p, j]))
                n_.wait()
                dve.nop(nofuse=True)
                for j in range(2):
                    ins = dve.bn_aggr(mv3[:, j], st3[:, j])
                n_.done(ins)
                n_.wait()

            def prep_root(k):
                if k < ROOT:
                    inv_sqrt(k, prep_now["steps"], mv3[:, :, 1], r3[:, 0], r3[:, 1], r3[:, 2])

            def prep_norm(n, p):
                prep_now["steps"].wait()
                if not first(n):
                    dve.wait_ge(xT3_mm, n)
                for j in range(2):
                    ins = dve.tensor_scalar(xn3[:, j], hx[:, p, j], mv3[:, j, 0:1], r3[:, 0, j:j + 1], ALU.subtract, ALU.mult)
                ins.then_inc(xn3_ready, 1)

            def maxima(u, h):
                dve.wait_ge(s_mm, u + 1)
                s2 = bank[SBANK[h % 2]]
                dve.tensor_reduce(nmax[:, h % 4, 0:1], s2[:, 0:P], AX.X, ALU.max, negate=True)
                dve.tensor_reduce(nmax[:, h % 4, 1:2], s2[:, P:3 * P], AX.X, ALU.max, negate=True).then_inc(max_ready, 1)

            def inverses(u, h):
                dve.wait_ge(exp_ready, u + 1)
                dve.reciprocal(rinv[:, h % 4], rsum[:, h % 4]).then_inc(rinv_ready, 1)

            def norm_first(u, h):
                dve.wait_ge(rinv_ready, u + 1)
                dve.tensor_scalar(pr[:, h % 4, 0:P], pr[:, h % 4, 0:P], rinv[:, h % 4, 0:1], None, ALU.mult)

            def norm_rest(u, h):
                dve.tensor_scalar(pr[:, h % 4, P:3 * P], pr[:, h % 4, P:3 * P], rinv[:, h % 4, 1:2], None, ALU.mult)\
                    .then_inc(pr_ready, 1)

            def turn(u, h):
                dve.wait_ge(prT_mm, u + 1)
                if not isinstance(u, int) or u >= 2:
                    dve.wait_ge(head_mm, u - 1)
                dve.tensor_copy(prT[:, h % 2], bank[TBANK[h % 2]][:, 0:3 * P]).then_inc(prT_ready, 1)

            gate_steps = {"per": 0}
            dve.wait_ge(consts4, 13)
            dve.wait_ge(w_c, 16 * 9)

            def gate_stats(g):
                n_ = gate_steps["now"] = Steps(dve, d_step, gate_steps["per"] * g)
                hh = h3[:].rearrange("p q j c -> p (q j) c")
                dve.wait_ge(h3_ready, 2 * g + 2)
                for j in range(TG):
                    n_.done(dve.bn_stats(st4[:, j], hh[:, j]))
                n_.wait()
                dve.nop(nofuse=True)
                for j in range(TG):
                    ins = dve.bn_aggr(mv4[:, j], st4[:, j])
                n_.done(ins)
                n_.wait()

            def gate_root(k):
                if k < ROOT:
                    inv_sqrt(k, gate_steps["now"], mv4[:, :, 1], r4[:, 0], r4[:, 1], r4[:, 2])

            def gate_norm(g):
                gate_steps["now"].wait()
                hh = h3[:].rearrange("p q j c -> p (q j) c")
                if not first(g):
                    dve.wait_ge(spread, 128 * g)
                for j in range(TG):
                    ins = dve.tensor_scalar(xr4[:, 0, j, 0:C], hh[:, j], mv4[:, j, 0:1], r4[:, 0, j:j + 1], ALU.subtract, ALU.mult)
                ins.then_inc(xn4_ready, 1)

            def gate_logits(g):
                dve.wait_ge(gate_mm, g + 1)
                dve.tensor_tensor(lg4[:], bank[GBANK][:, 0:TG * E1].rearrange("p (j x) -> p j x", j=TG),
                                  gb[:].unsqueeze(1).to_broadcast([P, TG, E1]), ALU.add).then_inc(lg4_ready, 1)

            def gate_top(g):
                n_ = gate_steps["now"]
                dve.wait_ge(lg4_ready, g + 1)
                dve.nop(nofuse=True)
                for j in range(TG):
                    ins = dve.max(top[:, j], lg4[:, j])
                n_.done(ins)
                n_.wait()
                dve.nop(nofuse=True)
                for j in range(TG):
                    ins = dve.max_index(topi[:, j], top[:, j], lg4[:, j])
                n_.done(ins)
                dve.tensor_tensor(gap[:], top[:, :, 1], top[:, :, 0], ALU.subtract).then_inc(gap_ready, 1)

            def gate_mask(g):
                n_ = gate_steps["now"]
                n_.wait()
                n_.done(dve.tensor_copy(topf[:], topi[:, :, 0:2]))
                n_.wait()
                for k in range(2):
                    ins = dve.tensor_tensor(hit[:, k], which[:].unsqueeze(1).to_broadcast([P, TG, E1]),
                                            topf[:, :, k:k + 1].to_broadcast([P, TG, E1]), ALU.is_equal)
                n_.done(ins)
                n_.wait()
                dve.tensor_tensor(mask[:], hit[:, 0], hit[:, 1], ALU.add).then_inc(mask_ready, 1)

            def gate_weights(g):
                n_ = gate_steps["now"]
                dve.wait_ge(gap_exp, g + 1)
                n_.done(dve.tensor_scalar(tw[:, 0], tw[:, 1], 1.0, None, ALU.add))
                n_.done(dve.tensor_copy(xr4[:, :, :, C + 1:XW].bitcast(U32).rearrange("p k j a -> p k (j a)"), dest[:]))
                n_.wait()
                n_.done(dve.reciprocal(tw[:, 0], tw[:, 0]))
                n_.done(dve.tensor_scalar(dest[:], dest[:], float(2 * TG * P), None, ALU.add))
                n_.wait()
                n_.done(dve.tensor_tensor(tw[:, 1], tw[:, 1], tw[:, 0], ALU.mult))
                n_.wait()
                n_.done(dve.tensor_copy(xr4[:, :, :, C:C + 1].rearrange("p k j a -> p k (j a)"), tw[:]))

            def gate_place(g):
                n_ = gate_steps["now"]
                dve.wait_ge(rank_mm, g + 1)
                n_.done(dve.tensor_tensor(rk[:], bank[VBANK][:, 0:TG * E1].rearrange("p (j x) -> p j x", j=TG),
                                          nextrow[:].unsqueeze(1).to_broadcast([P, TG, E1]), ALU.add))
                n_.wait()
                dve.tensor_tensor(nextrow[:], nextrow[:], bank[VBANK][:, TG * E1:(TG + 1) * E1], ALU.add).then_inc(rank_read, 1)
                for k in range(2):
                    ins = dve.tensor_tensor(posm[:, k], hit[:, k], rk[:], ALU.mult)
                n_.done(ins)
                n_.wait()
                n_.done(dve.tensor_reduce(posf[:], posm[:], AX.X, ALU.add))
                n_.wait()
                dve.wait_ge(rank_read, g + 1)
                dve.tensor_copy(pos[:], posf[:]).then_inc(pos_ready, 1)
                gate_steps["per"] = n_.n

            for k, (w, part) in enumerate(((wqk, wqk_part), (wvo, wvo_part))):
                dve.wait_ge(part_ready, k + 1)
                dve.tensor_tensor(part[1][:], w[:], part[0][:].bitcast(F32), ALU.subtract).then_inc(parts_split, 1)

            def split(n, p):
                dve.wait_ge(xT3_ready, n + 1)
                dve.tensor_tensor(x_part[1][:, p], xT3[:, p], x_part[0][:, p].bitcast(F32), ALU.subtract).then_inc(parts_split, 1)

            prep_stats(0, 0, 0)
            for k in range(ROOT):
                prep_root(k)
            prep_norm(0, 0)
            assert prep_now["steps"].n == PREP

            def finish(n, q, i, p):
                dve.wait_ge(head_mm, H1 * n + H1)
                dve.wait_ge(hb_ready, n + 1)
                if not isinstance(n, int) or n >= 2:
                    dve.wait_ge(h3_out[q], 16 * (i - 1 + p))
                dve.tensor_tensor(h3[:, q], bank[OBANK[q]][:, 0:2 * P].rearrange("p (j c) -> p j c", j=2), hb[:, q], ALU.add)\
                    .then_inc(h3_ready, 1)

            def slots(i, last):
                for p in range(2):
                    n = 2 * i + p
                    for h in range(H1):
                        u = H1 * n + h
                        if h in (1, 2, 3) and not (last and p == 1):
                            root = [prep_root, 5 * (h - 1)]
                        elif p == 0 and h in (5, 6, 7) and there(i - 1):
                            root = [gate_root, 5 * (h - 5)]
                        else:
                            root = [None, 0]

                        def root_step(root=root):
                            if root[0]:
                                root[0](root[1])
                                root[1] += 1
                        if (p, h) == (1, 7) and there(i - 1):
                            gate_place(i - 1)
                        if (p, h) == (1, 3) and there(i - 1):
                            gate_logits(i - 1)
                        root_step()
                        if there(u - N_LAG):
                            inverses(u - N_LAG, (h - N_LAG) % H1)
                        if there(u - S_LAG):
                            maxima(u - S_LAG, (h - S_LAG) % H1)
                        root_step()
                        if there(u - N_LAG):
                            norm_first(u - N_LAG, (h - N_LAG) % H1)
                        root_step()
                        if there(u - N_LAG):
                            norm_rest(u - N_LAG, (h - N_LAG) % H1)
                        root_step()
                        if there(u - T_LAG):
                            turn(u - T_LAG, (h - T_LAG) % H1)
                        root_step()
                        if h == 0 and not (last and p == 1):
                            prep_stats(n + 1, 1 - p, i + p)
                        if h == 3 and not (last and p == 1):
                            prep_norm(n + 1, 1 - p)
                        if h == 6 and not (last and p == 1):
                            split(n + 1, 1 - p)
                        if h == O_LAG - 1 and there(u - O_LAG):
                            finish(n - 1, 1 - p, i, p)
                        if (p, h) in GATE_SLOTS and there(i - 1):
                            GATE_SLOTS[p, h](i - 1)
            split(0, 0)
            GATE_SLOTS = {(0, 4): gate_stats, (0, 7): gate_norm, (1, 4): gate_top,
                          (1, 5): gate_mask, (1, 6): gate_weights}
            slots(0, False)
            slots(1, False)
            with dve.Fori(2, NB // 2 - 1) as i:
                slots(i, False)
            slots(NB // 2 - 1, True)
            U = NB * H1
            inverses(U - 2, H1 - 2)
            maxima(U - 1, H1 - 1)
            norm_first(U - 2, H1 - 2)
            norm_rest(U - 2, H1 - 2)
            turn(U - 3, H1 - 3)
            inverses(U - 1, H1 - 1)
            norm_first(U - 1, H1 - 1)
            norm_rest(U - 1, H1 - 1)
            turn(U - 2, H1 - 2)
            turn(U - 1, H1 - 1)
            finish(NB - 1, 1, NB // 2, 0)
            gate_stats(NG - 1)
            for k in range(ROOT):
                gate_root(k)
            gate_norm(NG - 1)
            gate_logits(NG - 1)
            gate_top(NG - 1)
            gate_mask(NG - 1)
            gate_weights(NG - 1)
            gate_place(NG - 1)

            n_ = Steps(dve, table_step)
            n_.done(dve.tensor_copy(ends[:], nextrow[0:1, :]))
            n_.done(dve.tensor_tensor(nun[:], nextrow[0:1, :], row0f[0:1, :], ALU.subtract))
            n_.wait()
            n_.done(dve.tensor_scalar(nuni[:], nun[:], float(UT - 1), None, ALU.add))
            n_.wait()
            n_.done(dve.tensor_scalar(nuni[:], nuni[:], 8, None, ALU.logical_shift_right))
            n_.wait()
            n_.done(dve.tensor_copy(nun[:], nuni[:]))
            n_.wait()
            n_.done(dve.tensor_tensor_scan(cun[:], ones[0:1, 0:E1], nun[:], 0.0, ALU.mult, ALU.add))
            n_.wait()
            n_.done(dve.tensor_tensor(past[:], uf[:].unsqueeze(2).to_broadcast([1, NUN, E1]),
                                      cun[:].unsqueeze(1).to_broadcast([1, NUN, E1]), ALU.is_ge))
            n_.done(dve.tensor_scalar(nun[:], nun[:], -float(UT), float(REG), ALU.mult, ALU.add))
            n_.wait()
            n_.done(dve.tensor_reduce(ux[:], past[:], AX.X, ALU.add))
            n_.wait()
            n_.done(dve.tensor_scalar(unit_x[:], ux[:], float(E1 - 1), None, ALU.min))
            n_.done(dve.tensor_tensor(past[:], past[:], nun[:].unsqueeze(1).to_broadcast([1, NUN, E1]), ALU.mult))
            n_.wait()
            n_.done(dve.tensor_reduce(ur[:], past[:], AX.X, ALU.add))
            n_.wait()
            dve.scalar_tensor_tensor(out=unit_r[:], in0=uf[:], scalar=float(UT), in1=ur[:], op0=ALU.mult, op1=ALU.add)\
                .then_inc(table_ready, 1)

            dve.wait_ge(table_ready, 1)
            dve.wait_ge(w_d2, 64)

            def weights1(u, q):
                x = dve.value_load(unit_x[0:1, bass.ds(u, 1)], min_val=0, max_val=E1 - 1)
                if not isinstance(u, int) or u >= 2:
                    dve.wait_ge(upu_mm, u - 1)
                dve.nop(nofuse=True)
                dve.tensor_copy(w1u[:, q % 2], w1s[:, bass.ds(x, 1)].rearrange("p a f -> p (a f)")).then_inc(w1u_ready, 1)
                return x

            def weights2(u, q, x):
                if not isinstance(u, int) or u >= 2:
                    dve.wait_ge(dnu_mm, u - 1)
                dve.nop(nofuse=True)
                dve.tensor_copy(w2u[:, q % 2], w2s[:, bass.ds(x, 1)].rearrange("p a f -> p (a f)")).then_inc(w2u_ready, 1)

            def unit_out(u, q, v):
                x = dve.value_load(unit_x[0:1, bass.ds(u, 1)], min_val=0, max_val=E1 - 1)
                dve.wait_ge(dnu_mm, u + 1)
                dve.nop(nofuse=True)
                dve.tensor_tensor(tu[:, q % 2], bank[4 + q % 2][:, 0:2 * C].rearrange("p (j c) -> p j c", j=2),
                                  b2s[:, bass.ds(x, 1)].to_broadcast([P, 2, C]), ALU.add).then_inc(tu_ready, 1)
                dve.wait_ge(tu_ready, u + 1)
                if not isinstance(u, int) or u >= YR:
                    dve.wait_ge(z_out[(q - YR) % XR], 32 * (v + 1 if q >= YR else v))
                dve.tensor_tensor(yu[:, q % YR], tu[:, q % 2], xu[:, q, :, C:C + 1].to_broadcast([P, 2, C]), ALU.mult)\
                    .then_inc(yu_ready, 1)

            def units(v, last):
                for q in range(XR):
                    u = XR * v + q
                    more = not (last and q == XR - 1)
                    if more:
                        x = weights1(u + 1, q + 1)
                        weights2(u + 1, q + 1, x)
                    if there(u - 1):
                        unit_out(u - 1, (q - 1) % XR, v if q else v - 1)
            weights2(0, 0, weights1(0, 0))
            units(0, False)
            with dve.Fori(1, NUN // XR - 1) as v:
                units(v, False)
            units(NUN // XR - 1, True)
            unit_out(NUN - 1, XR - 1, NUN // XR - 1)

            def results(i):
                for p in range(2):
                    g = 2 * i + p
                    dve.wait_ge(z_in[p], 32 * (i + 1))
                    if not first(i):
                        dve.wait_ge(out_done[p], 16 * i)
                    dve.tensor_tensor(res[:, p], zx[:, p, :, 0:C], zx[:, p, :, C:2 * C], ALU.add).then_inc(res_step, 1)
                    dve.wait_ge(res_step, g + 1)
                    dve.tensor_tensor(res[:, p], res[:, p], h3x[:, p], ALU.add).then_inc(res_ready, 1)
            results(0)
            with dve.Fori(1, NG // 2) as i:
                results(i)

        @block.tensor
        def _(pe):
            pe.wait_ge(consts, 7)
            pe.wait_ge(w_in, 16 * 7)
            pe.wait_ge(prep_c, 2)
            pe.transpose(bank[0][:, 0:P], idrowf[:], ident[:]).then_inc(prep_t, 1)
            for k in range(3):
                pe.transpose(bank[1][:, k * P:(k + 1) * P], wqkv_n[:, k], ident[:]).then_inc(prep_t, 1)
            pe.transpose(bank[2][:, 0:P], wproj_n[:], ident[:]).then_inc(prep_t, 1)
            pe.transpose(bank[3][:, 0:H0], head[:], ident[0:H0, 0:H0]).then_inc(prep_t, 1)
            pe.matmul(bank[4][:, 0:P], headt[:], head[:], start=True, stop=True).then_inc(prep_t, 1)
            pe.wait_ge(prep_c, 6)

            def second_turn(g, p):
                pe.wait_ge(x2_ready, g + 1)
                if not isinstance(g, int) or g >= 2:
                    pe.wait_ge(pT_ready, g - 1)
                for j in range(TG):
                    ins = pe.transpose(bank[4 * p + 3][:, j * P:(j + 1) * P], xr[:, p, j, 0:C], ident[:])
                ins.then_inc(x2T_mm, 1)

            def logits(g, p):
                pe.wait_ge(x2T_ready, g + 1)
                for j in range(TG):
                    ins = pe.matmul(bank[4 * p + 3][:, j * E0:(j + 1) * E0], x2T[:, p, j * P:(j + 1) * P], wrout[:],
                                    start=True, stop=True)
                ins.then_inc(lg_mm, 1)

            def turn_probs(g, p):
                pe.wait_ge(p_ready, g + 1)
                pe.transpose(bank[4 * p + 3][:, 0:P], pg[:, p].rearrange("p j e -> p (j e)"), ident[:]).then_inc(pT_mm, 1)

            def one(v, w):
                i = 2 * v + w
                g0, r0 = 2 * i, 2 * (i - 1)
                for p in range(2):
                    pe.wait_ge(xn_ready, g0 + p + 1)
                    for j in range(TG):
                        ins = pe.transpose(bank[4 * p][:, j * P:(j + 1) * P], xn[:, p, j], ident[:])
                    ins.then_inc(xT_mm, 1)
                for p in range(2):
                    pe.wait_ge(xT_ready, g0 + p + 1)
                    if within(i - 1):
                        pe.wait_ge(h1_ready, r0 + p + 1)
                    for m in range(2):
                        for j in range(2):
                            t = 2 * m + j
                            ins = pe.matmul(bank[4 * p + 1 + m][:, j * 2 * C:(j + 1) * 2 * C], xT[:, p, t * P:(t + 1) * P],
                                            wqkvT[:, C:3 * C], start=True, stop=True)
                        ins.then_inc(kv_mm, 1)
                if within(i - 2):
                    for p in range(2):
                        turn_probs(r0 - 2 + p, p)
                for p in range(2):
                    pe.matmul(bank[4 * p][:, :], wqkvT[:, 0:C], xT[:, p], start=True, stop=True).then_inc(q_mm, 1)
                for p in range(2):
                    pe.wait_ge(kv_ready, 4 * (g0 + p) + 4)
                    for b in range(2):
                        for j in range(2):
                            ins = pe.matmul(bank[4 * p + 1][:, b * (C + 1):(b + 1) * (C + 1)], kk[:, p, 2 * b + j],
                                            vv[:, p, 2 * b + j], start=(j == 0), stop=(j == 1))
                    ins.then_inc(kvs_mm, 1)
                for p in range(2):
                    pe.wait_ge(q_ready, g0 + p + 1)
                    pe.wait_ge(md_ready, g0 + p + 1)
                    for m in range(2):
                        for j in range(2):
                            t = 2 * m + j
                            ins = pe.matmul(bank[4 * p + 2 * m][:, j * (C + H0):(j + 1) * (C + H0)], qT[:, p, t * P:(t + 1) * P],
                                            md[:, p, m], start=True, stop=True)
                        ins.then_inc(o_mm, 1)
                if within(i - 1):
                    for p in range(2):
                        second_turn(r0 + p, p)
                for p in range(2):
                    pe.wait_ge(o_ready, g0 + p + 1)
                    for j in range(TG):
                        ins = pe.transpose(bank[4 * p + 1][:, j * P:(j + 1) * P], oo[:, p, j], ident[:])
                    ins.then_inc(oT_mm, 1)
                if within(i - 1):
                    for p in range(2):
                        logits(r0 + p, p)
                for p in range(2):
                    pe.wait_ge(oT_ready, g0 + p + 1)
                    for j in range(TG):
                        ins = pe.matmul(bank[4 * p + 2][:, j * P:(j + 1) * P], oT[:, p, j * P:(j + 1) * P], wprojT[:],
                                        start=True, stop=True)
                    ins.then_inc(y_mm, 1)
            rounds(pe, one)
            for p in range(2):
                turn_probs(NG - 4 + p, p)
            for step in (second_turn, logits, turn_probs):
                for p in range(2):
                    step(NG - 2 + p, p)

            pe.wait_ge(pa_ready, NG)
            pe.wait_ge(pT_ready, NG)
            for k in range(8):
                for j in range(4):
                    ins = pe.transpose(bank[k][:, j * P:(j + 1) * P], pa[:, :, 4 * k + j], ident[:])
                ins.then_inc(pcT_mm, 1)
            pe.wait_ge(w_c, 16 * 9)
            pe.wait_ge(pc_ready, 8)
            for k in range(3):
                ins = pe.transpose(bank[1][0:FCH[k], 8 * k:8 * k + 8], bup_n[:, k * P:k * P + FCH[k]], ident[0:8, 0:8])
            ins.then_inc(bup_mm, 1)
            pe.wait_ge(bup_ready, 2)
            pe.wait_ge(lanes_s, 4)

            def count(b):
                pe.wait_ge(cnt_ready, b + 1)
                pe.matmul(bank[0][:, 0:1], lanes[:], cnt[:, 0:1], start=True, stop=True).then_inc(cnt_mm, 1)

            pe.wait_ge(w_c, 16 * 9)
            for h in range(H1):
                count(h)
                if h > 0:
                    pe.wait_ge(fold_ready, 2 * h)
                for k, w in enumerate((wqn, wkn, wvn)):
                    ins = pe.transpose(bank[2][:, k * C:(k + 1) * C], w[:, h * C:(h + 1) * C], ident[:])
                ins.then_inc(wT_mm, 1)
                pe.wait_ge(wT_ready, h + 1)
                pe.matmul(bank[3][:, 0:C], wT[:, 0], wT[:, 1], start=True, stop=True)
                pe.matmul(bank[3][:, C:2 * C], wT[:, 2], won[:, h], start=True, stop=True).then_inc(fold_mm, 1)
            pe.wait_ge(fold_ready, 2 * H1)
            for k in range(2):
                ins = pe.transpose(bank[2][:, k * E1:(k + 1) * E1], b1n[:, k * P:(k + 1) * P], ident[0:E1, 0:E1])
            ins.then_inc(b1_mm, 1)
            with pe.Fori(H1, COUNTS) as b:
                count(b)
            pe.wait_ge(diag_ready, 1)
            for k in range(2):
                ins = pe.matmul(bank[1][:, k * E0:(k + 1) * E0], ones[0:E0, :], diag[:, k], start=True, stop=True)
            ins.then_inc(tq_mm, 1)

            def bases(e):
                pe.wait_ge(cum_ready, e + 1)
                pe.matmul(bank[7][:, 0:2], before[:], cum[:, :, P - 1], start=True, stop=True).then_inc(base_mm, 1)

            def rows(e):
                pe.wait_ge(oneh_ready, e + 1)
                for c in range(TG):
                    o = bank[5 + c // 2][:, (c % 2) * (P + 1):(c % 2 + 1) * (P + 1)]
                    ins = pe.matmul(o, oneh[:, c * P:(c + 1) * P], tab[:], start=True, stop=True)
                ins.then_inc(tab_mm, 1)

            pe.wait_ge(tq_ready, 1)
            for e in range(3):
                bases(e)
                if e < 2:
                    rows(e)

            def turn_rows(e, p, guard):
                pe.wait_ge(xe_in[p], guard)
                for c in range(TG):
                    ins = pe.transpose(bank[0][:, c * P:(c + 1) * P], xe[:, p, c, 0:C], ident[:])
                ins.then_inc(xeT_mm, 1)
            turn_rows(0, 0, 64)

            def serve(v, last):
                for q in range(4):
                    e, p = 4 * v + q, q % 2
                    if not (last and q >= 2):
                        rows(e + 2)
                    pe.wait_ge(xeT_ready, e + 1)
                    pe.wait_ge(wup_in[p], 16 * (2 * v + q // 2 + 1))
                    for k in range(3):
                        pe.matmul(bank[1 + k][0:FCH[k], :], wup[:, p, k * P:k * P + FCH[k]], xeT[:], start=True, stop=True)\
                            .then_inc(up_mm, 1)
                    if not (last and q >= 1):
                        bases(e + 3)
                    if not (last and q == 3):
                        turn_rows(e + 1, 1 - p, 64 * (2 * v + (q + 1) // 2 + 1))
                    pe.wait_ge(ac_ready, 3 * e + 3)
                    pe.wait_ge(wdn_in[p], 48 * (2 * v + q // 2 + 1))
                    if not (first(v) and q == 0):
                        pe.wait_ge(ye_ready, e)
                    for c in range(TG):
                        for k in range(3):
                            m = FCH[k] + (k == 2)
                            ins = pe.matmul(bank[4][:, c * P:(c + 1) * P], ac[0:m, k, c * P:(c + 1) * P], wdn[0:m, p, k],
                                            start=(k == 0), stop=(k == 2))
                    ins.then_inc(dn_mm, 1)
            serve(0, False)
            with pe.Fori(1, NU - 1) as v:
                serve(v, False)
            serve(NU - 1, True)

            pe.wait_ge(fold_ready, 2 * H1)
            pe.wait_ge(consts4, 16)
            pe.wait_ge(ye_ready, E0)
            pe.wait_ge(idx_ready, E0)

            PARTS = ((1, 0), (0, 1), (0, 0))

            def turned(n):
                pe.wait_ge(xn3_ready, n + 1)
                if not first(n):
                    pe.wait_ge(vo_ready, 4 * n)
                for j in range(2):
                    ins = pe.transpose(bank[VBANK][:, j * P:(j + 1) * P], xn3[:, j], ident[:])
                ins.then_inc(xT3_mm, 1)

            def scores(u, h, p, n):
                s2 = bank[SBANK[h % 2]]
                g = gT[:, h // 2 % 2, (h % 2) * 2 * P:(h % 2 + 1) * 2 * P]
                pe.wait_ge(g_ready, 4 * n + h // 2 + 1)
                if not isinstance(u, int) or u >= 2:
                    pe.wait_ge(exp_ready, u - 1)
                pe.matmul(s2[:, 0:P], g[:, 0:P], xT3[:, p, 0:P], start=True, stop=False)
                pe.matmul(s2[:, 0:P], identb[:], causal[:], start=False, stop=True)
                pe.matmul(s2[:, 2 * P:3 * P], identb[:], causal[:], start=True, stop=False, skip_group_check=True)
                pe.matmul(s2[:, P:3 * P], g[:, P:2 * P], xT3[:, p], start=False, stop=True, skip_group_check=True)\
                    .then_inc(s_mm, 1)

            def turns(u, h):
                pe.wait_ge(pr_ready, u + 1)
                if not isinstance(u, int) or u >= 2:
                    pe.wait_ge(prT_ready, u - 1)
                for k in range(3):
                    ins = pe.transpose(bank[TBANK[h % 2]][:, k * P:(k + 1) * P], pr[:, h % 4, k * P:(k + 1) * P], ident[:])
                ins.then_inc(prT_mm, 1)

            def sums(u, h, p, n):
                o = bank[OBANK[p]]
                pe.wait_ge(prT_ready, u + 1)
                if h == 0:
                    pe.wait_ge(vo_ready, 4 * n + 4)
                    if not isinstance(n, int) or n >= 2:
                        pe.wait_ge(h3_ready, n - 1)
                v0, v1 = (vo[:, p, j, h * C:(h + 1) * C] for j in range(2))
                pe.matmul(o[:, 0:P], prT[:, h % 2, 0:P], v0, start=(h == 0), stop=False, skip_group_check=True)
                pe.matmul(o[:, P:2 * P], prT[:, h % 2, P:2 * P], v0, start=False, stop=False, skip_group_check=True)
                pe.matmul(o[:, P:2 * P], prT[:, h % 2, 2 * P:3 * P], v1, start=False, stop=(h == H1 - 1),
                          skip_group_check=True).then_inc(head_mm, 1)

            def slots(i, last):
                for p in range(2):
                    n = 2 * i + p
                    for h in range(H1):
                        u = H1 * n + h
                        if h == 0:
                            pe.wait_ge(parts_split, n + 3)
                        if (p, h) == (1, 1) and there(i - 1):
                            pe.wait_ge(g_ready, 4 * n + 1)
                            gate_turn(i - 1)
                        if (p, h) == (1, 3) and there(i - 1):
                            pe.wait_ge(g_ready, 4 * n + 2)
                            gate_products(i - 1)
                        if h % 2 == 0:
                            if (p, h) == (1, 2) and there(i - 1):
                                pe.wait_ge(xT4_ready, i)
                            if (p, h) == (1, 4) and there(i - 1):
                                pe.wait_ge(lg4_ready, i)
                            for k in range(2):
                                for m, (a, b) in enumerate(PARTS):
                                    ins = pe.matmul(bank[GBANK][:, k * 2 * P:(k + 1) * 2 * P], wqk_part[a][:, h + k], x_part[b][:, p],
                                                    start=(m == 0), stop=(m == 2))
                            ins.then_inc(g_mm, 1)
                        if h == 5 and not (last and p == 1):
                            turned(n + 1)
                        if there(u - S_LAG):
                            scores(u - S_LAG, (h - S_LAG) % H1, p if h >= S_LAG else 1 - p, n if h >= S_LAG else n - 1)
                        if h < 4:
                            if h == 0 and p == 0 and there(i - 2):
                                pe.wait_ge(rank_read, i - 1)
                            if h > 0:
                                pe.wait_ge(vo_ready, 4 * n + h)
                            for m, (a, b) in enumerate(PARTS):
                                ins = pe.matmul(bank[VBANK][:, :], x_part[b][:, p, (h % 2) * P:(h % 2 + 1) * P],
                                                wvo_part[a][:, 4 * (h // 2):4 * (h // 2) + 4], start=(m == 0), stop=(m == 2))
                            ins.then_inc(vo_mm, 1)
                        if there(u - T_LAG):
                            turns(u - T_LAG, (h - T_LAG) % H1)
                        if there(u - O_LAG):
                            sums(u - O_LAG, (h - O_LAG) % H1, p if h >= O_LAG else 1 - p, n if h >= O_LAG else n - 1)
                        if (p, h) == (1, 6) and there(i - 1):
                            if not last:
                                pe.wait_ge(xT3_ready, n + 2)
                            gate_ranks(i - 1)

            def gate_turn(g):
                pe.wait_ge(xn4_ready, g + 1)
                for j in range(TG):
                    ins = pe.transpose(bank[GBANK][:, j * P:(j + 1) * P], xr4[:, 0, j, 0:C], ident[:])
                ins.then_inc(xT4_mm, 1)

            def gate_products(g):
                pe.wait_ge(xT4_ready, g + 1)
                for j in range(TG):
                    ins = pe.matmul(bank[GBANK][:, j * E1:(j + 1) * E1], xT4[:, j * P:(j + 1) * P], gw[:], start=True, stop=True)
                ins.then_inc(gate_mm, 1)

            def gate_ranks(g):
                pe.wait_ge(mask_ready, g + 1)
                for j in range(TG + 1):
                    o = bank[VBANK][:, j * E1:(j + 1) * E1]
                    if j < TG:
                        pe.matmul(o, beforeb[:], mask[:, j], start=True, stop=(j == 0))
                    for k in range(j):
                        ins = pe.matmul(o, onesb[:], mask[:, k], start=(j == TG and k == 0), stop=(k == j - 1))
                ins.then_inc(rank_mm, 1)

            turned(0)
            slots(0, False)
            slots(1, False)
            with pe.Fori(2, NB // 2 - 1) as i:
                slots(i, False)
            slots(NB // 2 - 1, True)
            U = NB * H1
            scores(U - 1, H1 - 1, 1, NB - 1)
            turns(U - 3, H1 - 3)
            sums(U - 4, H1 - 4, 1, NB - 1)
            turns(U - 2, H1 - 2)
            sums(U - 3, H1 - 3, 1, NB - 1)
            turns(U - 1, H1 - 1)
            sums(U - 2, H1 - 2, 1, NB - 1)
            sums(U - 1, H1 - 1, 1, NB - 1)
            pe.wait_ge(rank_read, NG - 1)
            gate_turn(NG - 1)
            gate_products(NG - 1)
            pe.wait_ge(lg4_ready, NG)
            gate_ranks(NG - 1)

            pe.wait_ge(rank_read, NG)
            pe.wait_ge(h3_ready, NB)

            def unit_turn(u, q, v):
                pe.wait_ge(xu_in[q], 16 * (v + 1))
                for j in range(2):
                    ins = pe.transpose(bank[q % 2][:, j * P:(j + 1) * P], xu[:, q, j, 0:C], ident[:])
                ins.then_inc(xTu_mm, 1)

            def unit_up(u, q):
                pe.wait_ge(xTu_ready, u + 1)
                pe.wait_ge(w1u_ready, u + 1)
                for k in range(2):
                    ins = pe.matmul(bank[2 + q % 2][:, k * UT:(k + 1) * UT], w1u[:, q % 2, k * P:(k + 1) * P], xTu[:, q % 2],
                                    start=True, stop=True)
                ins.then_inc(upu_mm, 1)

            def unit_down(u, q):
                pe.wait_ge(hTu_ready, u + 1)
                pe.wait_ge(w2u_ready, u + 1)
                if not isinstance(u, int) or u >= 2:
                    pe.wait_ge(tu_ready, u - 1)
                for j in range(2):
                    for k in range(2):
                        ins = pe.matmul(bank[4 + q % 2][:, j * C:(j + 1) * C], hTu[:, q % 2, k, j * P:(j + 1) * P],
                                        w2u[:, q % 2, k * C:(k + 1) * C], start=(k == 0), stop=(k == 1))
                ins.then_inc(dnu_mm, 1)

            def units(v, last):
                for q in range(XR):
                    u = XR * v + q
                    if not (last and q == XR - 1):
                        unit_turn(u + 1, (q + 1) % XR, v if q < XR - 1 else v + 1)
                    unit_up(u, q)
                    if there(u - 1):
                        unit_down(u - 1, (q - 1) % XR)
            unit_turn(0, 0, 0)
            units(0, False)
            with pe.Fori(1, NUN // XR - 1) as v:
                units(v, False)
            units(NUN // XR - 1, True)
            unit_down(NUN - 1, XR - 1)


_INS = ['x', 'L0_tok_weight', 'L0_attn_Wqkv', 'L0_attn_temperature', 'L0_attn_Wproj', 'L0_attn_bproj',
        'L0_ffn_W_router', 'L0_ffn_b_router', 'L0_ffn_W_up', 'L0_ffn_b_up', 'L0_ffn_W_down', 'L0_ffn_b_down',
        'L1_attn_Wq', 'L1_attn_Wk', 'L1_attn_Wv', 'L1_attn_Wo', 'L1_attn_bo', 'L1_ffn_gate_w', 'L1_ffn_gate_b',
        'L1_ffn_w1', 'L1_ffn_b1', 'L1_ffn_w2', 'L1_ffn_b2']


def kernel(**inputs):
    import numpy as _np
    import concourse.bacc as _bacc
    from concourse import mybir as _mybir
    from concourse.bass_utils import run_bass_kernel_spmd as _run

    nc = _bacc.Bacc("TRN2", target_bir_lowering=False, num_devices=1)
    arrays, args = {}, []
    for name in _INS:
        a = _np.ascontiguousarray(inputs[name])
        arrays[f"in_{name}_dram"] = a
        args.append(nc.dram_tensor(f"in_{name}_dram", a.shape, _mybir.dt.from_np(a.dtype), kind="ExternalInput").ap())
    args.append(nc.dram_tensor("out_0_dram", (64, 256, C), F32, kind="ExternalOutput").ap())
    lm_tower(nc, *args)
    r = _run(nc, [arrays], core_ids=[0])
    return r.results[0]["out_0_dram"]
```
